# Optimizing a Trainium2 kernel written in Bass

```python
import numpy as np
import jax
import jax.numpy as jnp

def _softmax(x, axis=-1):
    return jax.nn.softmax(x, axis=axis)

def _gelu(x):
    return jax.nn.gelu(x, approximate=True)

def _silu(x):
    return jax.nn.silu(x)

def _sigmoid(x):
    return jax.nn.sigmoid(x)

def _layernorm(x, axis=-1, eps=1e-05):
    m = jnp.mean(x, axis=axis, keepdims=True)
    v = jnp.var(x, axis=axis, keepdims=True)
    return (x - m) / jnp.sqrt(v + eps)

def _scatter_add(tgt, idx, src, axis=0):
    return tgt.at[idx].add(src)

def _segment_sum(src, seg, n):
    return jax.ops.segment_sum(src, seg, n)
kernel_name = 'mk_adaln_ffn_d2_seqx_r4_dcc8e9'

def setup_inputs(seed: int=0):
    np.random.seed(seed)
    _w = jnp.asarray

    def _rec_inputs():
        import jax
        import jax.numpy as jnp
        _rk = jax.random.key(seed)
        x = -1.394e-06 + 0.9999 * jax.random.normal(jax.random.fold_in(_rk, 1), (8, 256, 512), jnp.float32)
        _lenS = 256 - jax.random.randint(jax.random.fold_in(_rk, 7), (8,), 0, max(1, 256 // 4) + 1, jnp.int32)
        _lenS2 = 256 - jax.random.randint(jax.random.fold_in(_rk, 8), (8,), 0, max(1, 256 // 4) + 1, jnp.int32)
        cond_2048 = -0.00499425 + 1.0058 * jax.random.normal(jax.random.fold_in(_rk, 11), (8, 512), jnp.float32)
        return (x, cond_2048)
    x, cond_2048 = _rec_inputs()

    def _L0_cond_setup():
        import jax, jax.numpy as jnp
        import numpy as np
        B, T, D = (16, 128, 512)
        key = jax.random.key(seed)
        k0, k1, k2, k3 = jax.random.split(key, 4)
        scale = 1.0 / np.sqrt(D)
        return {'initial_state': jax.random.normal(k0, (B, D), jnp.float32), 'inputs': jax.random.normal(k1, (B, T, D), jnp.float32), 'W_ih': jax.random.normal(k2, (D, 3 * D), jnp.float32) * scale, 'W_hh': jax.random.normal(k3, (D, 3 * D), jnp.float32) * scale, 'b_ih': jnp.zeros((3 * D,), jnp.float32), 'b_hh': jnp.zeros((3 * D,), jnp.float32)}
    _L0_cond_all = _L0_cond_setup()
    _L0_cond_in = {k: v for k, v in _L0_cond_all.items() if k in ('W_ih', 'W_hh', 'b_ih', 'b_hh')}
    del _L0_cond_all

    def _L0_ffn_setup():
        import jax, jax.numpy as jnp
        import numpy as np
        TOP_K = 2

        def moe_forward(x, w_gate_router, w_gate_proj, w_up_proj, w_down_proj):
            E = w_gate_router.shape[0]
            scores = jnp.einsum('bsd,ed->bse', x, w_gate_router)
            topk_scores, topk_idx = jax.lax.top_k(scores, TOP_K)
            topk_probs = jax.nn.softmax(topk_scores, axis=-1)
            weights = jnp.sum(topk_probs[..., None] * jax.nn.one_hot(topk_idx, E, dtype=x.dtype), axis=-2)
            gate = jnp.einsum('bsd,efd->bsef', x, w_gate_proj)
            up = jnp.einsum('bsd,efd->bsef', x, w_up_proj)
            hidden = jax.nn.silu(gate) * up
            out = jnp.einsum('bsef,edf,bse->bsd', hidden, w_down_proj, weights)
            return out
        key = jax.random.key(seed)
        k1, k2, k3, k4, k5 = jax.random.split(key, 5)
        B, S, D, E, F = (2, 256, 512, 8, 192)
        scale_in = 1.0 / np.sqrt(D)
        scale_ff = 1.0 / np.sqrt(F)
        return {'x': jax.random.normal(k1, (B, S, D), dtype=jnp.float32), 'w_gate_router': jax.random.normal(k2, (E, D), dtype=jnp.float32) * scale_in, 'w_gate_proj': jax.random.normal(k3, (E, F, D), dtype=jnp.float32) * scale_in, 'w_up_proj': jax.random.normal(k4, (E, F, D), dtype=jnp.float32) * scale_in, 'w_down_proj': jax.random.normal(k5, (E, D, F), dtype=jnp.float32) * scale_ff}
    _L0_ffn_all = _L0_ffn_setup()
    _L0_ffn_in = {k: v for k, v in _L0_ffn_all.items() if k in ('w_gate_router', 'w_gate_proj', 'w_up_proj', 'w_down_proj')}
    del _L0_ffn_all

    def _L1_cond_setup():
        import jax, jax.numpy as jnp
        import numpy as np
        HEADS = 16
        EPS = 1e-06

        def _rms_norm(x, g):
            xf = x.astype(jnp.float32)
            y = xf * jax.lax.rsqrt(jnp.mean(xf * xf, axis=-1, keepdims=True) + EPS)
            return y.astype(x.dtype) * g
        key = jax.random.key(seed)
        ks = jax.random.split(key, 6)
        b, n, dim, emb_dim = (4, 512, 512, 512)
        d_head = dim // HEADS
        return {'x': jax.random.normal(ks[0], (b, n, dim), jnp.float32), 'emb': jax.random.normal(ks[1], (b, 1, emb_dim), jnp.float32), 'W_emb': jax.random.normal(ks[2], (emb_dim, 2 * dim), jnp.float32) * emb_dim ** (-0.5), 'b_emb': jnp.zeros((2 * dim,), jnp.float32), 'g_norm': jnp.ones((dim,), jnp.float32), 'W_qkv': jax.random.normal(ks[3], (dim, 3 * dim), jnp.float32) * dim ** (-0.5), 'g_q': jnp.ones((d_head,), jnp.float32), 'g_k': jnp.ones((d_head,), jnp.float32), 'W_out': jax.random.normal(ks[4], (dim, dim), jnp.float32) * dim ** (-0.5)}
    _L1_cond_all = _L1_cond_setup()
    _L1_cond_in = {k: v for k, v in _L1_cond_all.items() if k in ('W_emb', 'b_emb', 'g_norm', 'W_qkv', 'g_q', 'g_k', 'W_out')}
    del _L1_cond_all

    def _L1_ffn_setup():
        import jax, jax.numpy as jnp
        import numpy as np
        EPS = 1e-08

        def _quantize(w):
            gamma = jnp.mean(jnp.abs(w))
            return jnp.clip(jnp.round(w / (gamma + EPS)), -1.0, 1.0)

        def _bitlinear(x, w):
            return jnp.matmul(x, _quantize(w).T)
        key = jax.random.key(seed)
        k1, k2, k3, k4 = jax.random.split(key, 4)
        d, h = (512, 1408)
        x = jax.random.normal(k1, (4, 512, d), dtype=jnp.float32)
        w1 = jax.random.normal(k2, (h, d), dtype=jnp.float32)
        w2 = jax.random.normal(k3, (h, d), dtype=jnp.float32)
        w3 = jax.random.normal(k4, (d, h), dtype=jnp.float32)
        return {'x': x, 'w1': w1, 'w2': w2, 'w3': w3}
    _L1_ffn_all = _L1_ffn_setup()
    _L1_ffn_in = {k: v for k, v in _L1_ffn_all.items() if k in ('w1', 'w2', 'w3')}
    del _L1_ffn_all
    return {'x': x, 'cond_2048': cond_2048, 'L0_cond_W_ih': _L0_cond_in['W_ih'], 'L0_cond_W_hh': _L0_cond_in['W_hh'], 'L0_cond_b_ih': _L0_cond_in['b_ih'], 'L0_cond_b_hh': _L0_cond_in['b_hh'], 'L0_ffn_w_gate_router': _L0_ffn_in['w_gate_router'], 'L0_ffn_w_gate_proj': _L0_ffn_in['w_gate_proj'], 'L0_ffn_w_up_proj': _L0_ffn_in['w_up_proj'], 'L0_ffn_w_down_proj': _L0_ffn_in['w_down_proj'], 'L1_cond_W_emb': _L1_cond_in['W_emb'], 'L1_cond_b_emb': _L1_cond_in['b_emb'], 'L1_cond_g_norm': _L1_cond_in['g_norm'], 'L1_cond_W_qkv': _L1_cond_in['W_qkv'], 'L1_cond_g_q': _L1_cond_in['g_q'], 'L1_cond_g_k': _L1_cond_in['g_k'], 'L1_cond_W_out': _L1_cond_in['W_out'], 'L1_ffn_w1': _L1_ffn_in['w1'], 'L1_ffn_w2': _L1_ffn_in['w2'], 'L1_ffn_w3': _L1_ffn_in['w3']}

def reference(x, cond_2048, L0_cond_W_ih, L0_cond_W_hh, L0_cond_b_ih, L0_cond_b_hh, L0_ffn_w_gate_router, L0_ffn_w_gate_proj, L0_ffn_w_up_proj, L0_ffn_w_down_proj, L1_cond_W_emb, L1_cond_b_emb, L1_cond_g_norm, L1_cond_W_qkv, L1_cond_g_q, L1_cond_g_k, L1_cond_W_out, L1_ffn_w1, L1_ffn_w2, L1_ffn_w3):
    import jax
    import jax.numpy as jnp

    def _L0_cond_ref(initial_state, inputs, W_ih, W_hh, b_ih, b_hh):
        import jax, jax.numpy as jnp
        import numpy as np
        B, T, D = (16, 128, 512)
        "ScanOverTime(GRU cell): sequential per-timestep module call with\n            dict-state passing; merge_dict_trees stacks the per-step\n            'state_predicted' tensors along axis=1 -> [B, T, D]."

        def cell(h, x):
            gi = x @ W_ih + b_ih
            gh = h @ W_hh + b_hh
            i_r, i_z, i_n = jnp.split(gi, 3, axis=-1)
            h_r, h_z, h_n = jnp.split(gh, 3, axis=-1)
            r = jax.nn.sigmoid(i_r + h_r)
            z = jax.nn.sigmoid(i_z + h_z)
            n = jnp.tanh(i_n + r * h_n)
            h_new = (1.0 - z) * n + z * h
            return (h_new, h_new)
        xs = jnp.swapaxes(inputs, 0, 1)
        _, hs = jax.lax.scan(cell, initial_state, xs)
        return jnp.swapaxes(hs, 0, 1)

    def _L0_ffn_ref(x, w_gate_router, w_gate_proj, w_up_proj, w_down_proj):
        import jax, jax.numpy as jnp
        import numpy as np
        TOP_K = 2

        def moe_forward(x, w_gate_router, w_gate_proj, w_up_proj, w_down_proj):
            E = w_gate_router.shape[0]
            scores = jnp.einsum('bsd,ed->bse', x, w_gate_router)
            topk_scores, topk_idx = jax.lax.top_k(scores, TOP_K)
            topk_probs = jax.nn.softmax(topk_scores, axis=-1)
            weights = jnp.sum(topk_probs[..., None] * jax.nn.one_hot(topk_idx, E, dtype=x.dtype), axis=-2)
            gate = jnp.einsum('bsd,efd->bsef', x, w_gate_proj)
            up = jnp.einsum('bsd,efd->bsef', x, w_up_proj)
            hidden = jax.nn.silu(gate) * up
            out = jnp.einsum('bsef,edf,bse->bsd', hidden, w_down_proj, weights)
            return out
        return moe_forward(x, w_gate_router, w_gate_proj, w_up_proj, w_down_proj)

    def _L1_cond_ref(x, emb, W_emb, b_emb, g_norm, W_qkv, g_q, g_k, W_out):
        import jax, jax.numpy as jnp
        import numpy as np
        HEADS = 16
        EPS = 1e-06

        def _rms_norm(x, g):
            xf = x.astype(jnp.float32)
            y = xf * jax.lax.rsqrt(jnp.mean(xf * xf, axis=-1, keepdims=True) + EPS)
            return y.astype(x.dtype) * g
        b, n, dim = x.shape
        h = HEADS
        d = dim // h
        scale_shift = emb @ W_emb + b_emb
        scale, shift = jnp.split(scale_shift, 2, axis=-1)
        xn = _rms_norm(x, g_norm) * (1.0 + scale) + shift
        qkv = xn @ W_qkv
        qkv = qkv.reshape(b, n, 3, h, d)
        q, k, v = jnp.moveaxis(qkv, 2, 0)
        q = jnp.swapaxes(q, 1, 2)
        k = jnp.swapaxes(k, 1, 2)
        v = jnp.swapaxes(v, 1, 2)
        q = _rms_norm(q, g_q)
        k = _rms_norm(k, g_k)
        logits = jnp.einsum('bhqd,bhkd->bhqk', q, k) * d ** (-0.5)
        attn = jax.nn.softmax(logits, axis=-1)
        o = jnp.einsum('bhqk,bhkd->bhqd', attn, v)
        o = jnp.swapaxes(o, 1, 2).reshape(b, n, dim)
        return o + o @ W_out

    def _L1_ffn_ref(x, w1, w2, w3):
        import jax, jax.numpy as jnp
        import numpy as np
        EPS = 1e-08

        def _quantize(w):
            gamma = jnp.mean(jnp.abs(w))
            return jnp.clip(jnp.round(w / (gamma + EPS)), -1.0, 1.0)

        def _bitlinear(x, w):
            return jnp.matmul(x, _quantize(w).T)
        x1 = _bitlinear(x, w1)
        x2 = _bitlinear(x, w2)
        hidden = jax.nn.sigmoid(x1) * x2
        return _bitlinear(hidden, w3)
    x = x + _L0_ffn_ref(_L0_cond_ref(cond_2048, x, L0_cond_W_ih, L0_cond_W_hh, L0_cond_b_ih, L0_cond_b_hh), L0_ffn_w_gate_router, L0_ffn_w_gate_proj, L0_ffn_w_up_proj, L0_ffn_w_down_proj)
    x = x + _L1_ffn_ref(_L1_cond_ref(x, cond_2048[:, None, :], L1_cond_W_emb, L1_cond_b_emb, L1_cond_g_norm, L1_cond_W_qkv, L1_cond_g_q, L1_cond_g_k, L1_cond_W_out), L1_ffn_w1, L1_ffn_w2, L1_ffn_w3)
    return x

_drawn_inputs = setup_inputs


def setup_inputs(seed=0):
    import zlib

    import numpy as np

    out = dict(_drawn_inputs(seed))
    spreads = {'L0_cond_b_ih': (0.0, 0.455),
     'L0_cond_b_hh': (0.0, 0.65),
     'L1_cond_b_emb': (0.0, 0.1),
     'L1_cond_g_norm': (1.0, 0.2),
     'L1_cond_g_q': (1.0, 0.2),
     'L1_cond_g_k': (1.0, 0.2)}
    factors = {}
    for name, (base, spread) in spreads.items():
        noise = np.random.default_rng([zlib.crc32(name.encode()), seed]).standard_normal(out[name].shape)
        drawn = base * np.exp(spread * noise) if base else spread * noise
        out[name] = jnp.asarray(drawn.astype(out[name].dtype))
    for name, factor in factors.items():
        out[name] = (out[name] * factor).astype(out[name].dtype)
    return out
```

```python
from contextlib import ExitStack

import concourse.bass as bass
from concourse import mybir

F32 = mybir.dt.float32
F16 = mybir.dt.float16
U32 = mybir.dt.uint32
ACT = mybir.ActivationFunctionType
ALU = mybir.AluOpType
AX = mybir.AxisListType

P = 128
D = 512
KT = D // P
T = 256
B = 8
NTOK = T * B
CH = 512
NCH = NTOK // CH
TC = CH // B
G3 = 3 * D
GM = G3 // P
E = 8
F = 192
FM = E * F // P
H = 16
DH = D // H
HF = 1408
HM = HF // P
WN = HF * D

SW = 64.0
SX = 16.0
SWX = SW * SX

UN = 16
ARENA = 190 * 1024


class Mem:

    def __init__(self, arena, start):
        self.arena, self.at = arena, start

    def take(self, shape, dt, parts=P):
        n = 1
        for s in shape:
            n *= s
        size = n * (2 if dt == F16 else 4)
        size = (size + 31) // 32 * 32
        a = self.arena[0:parts, self.at // 4:(self.at + size) // 4]
        self.at += size
        assert self.at <= ARENA, self.at
        a = a.bitcast(dt) if dt != F32 else a
        a = a[:, 0:n]
        if len(shape) > 1:
            names = "abcdef"[:len(shape)]
            a = a.rearrange("p (%s) -> p %s" % (" ".join(names), " ".join(names)),
                            **{c: s for c, s in zip(names, shape)})
        return a


def gru_order():
    RZ, N, ALL = (0, 1), (2,), (0, 1, 2)

    def block(ks, js, gates):
        return [(k, j, gates) for j in js for k in ks]

    return (block((0, 1), (0, 1), ALL) + block((0, 1), (2,), RZ) + block((2, 3), (0, 1), RZ)
            + block((2, 3), (0, 1), N) + block((0, 1), (3,), RZ) + block((2, 3), (2, 3), RZ)
            + block((0, 1, 2, 3), (2, 3), N))


def mixed_net_kernel(nc, xT, condT, wih, whh, bias, wr, wgu, wdn, wemb, avec, gqk, wqkv, wout,
                     w1f, w2f, w3f, w1T, w2T, w3T, consts, out):
    with ExitStack() as ctx:
        def sb(name, shape, dt):
            return ctx.enter_context(nc.sbuf_tensor(name, shape, dt))

        def sem(name):
            return ctx.enter_context(nc.semaphore(name))

        def two(name):
            return [sem(name + "_0"), sem(name + "_1")]

        bank = [ctx.enter_context(nc.psum_tensor(f"bank{i}", [P, 512], F32)) for i in range(8)]
        arena = sb("arena", [P, ARENA // 4], F32)

        cst = sb("cst", [P, 264], F32)
        ident = cst[:, 0:128]
        headones = cst[:, 128:256]
        iota = cst[:, 256:264]
        ones = sb("ones", [P, 128], F32)
        id1 = sb("id1", [P, 128], F16)
        id16 = sb("id16", [P, 128], F16)
        sel = sb("sel", [P, FM, 128], F16)
        bia = sb("bia", [P, 2, GM], F32)
        bgi = sb("bgi", [P, GM], F32)
        bhn = sb("bhn", [P, 2, 4, B], F16)
        bhf = sb("bhf", [P, 4, B], F32)
        cond = sb("cond", [P, KT, B], F32)
        gsum = sb("gsum", [P, NCH, 3], F32)
        thr = sb("thr", [P, 2, 3], F32)
        av = sb("av", [P, 3 * KT], F32)
        gq = sb("gq", [P, 2], F32)
        gqs = sb("gqs", [P, 2], F32)
        ada = sb("ada", [P, 2, KT, B], F32)
        epsb = sb("epsb", [P, 1], F32)
        wrs = sb("wrs", [P, KT, 2, E], F16)
        wrf = sb("wrf", [P, KT, E], F32)

        top = Mem(arena, 0)
        hx = top.take([T, KT * B], F32)
        base = top.at

        m = Mem(arena, base)
        wihs = m.take([2, KT, GM, P], F16)
        whhs = m.take([2, KT, GM, P], F16)
        girz = m.take([TC + 1, 2, 2 * KT * B], F16)
        gin = m.take([TC + 1, KT * B], F32)
        xc = m.take([KT, CH], F32)
        xs = m.take([2, KT, CH], F16)
        raw = m.take([4, G3], F32)
        tmp = m.take([2, CH], F32)
        wal = m.take([3, WN // P // NCH], F32)
        cstage = m.take([FM * 128], F32)
        mv = m.take([2, KT, 4, B], F16)
        H16 = m.take([KT * B], F32)
        rzp = m.take([2, 32], F32)
        rz = m.take([2, 32], F32)
        n5 = m.take([32, 5], F32)
        npre = m.take([32], F32)
        nn = m.take([32], F32)
        om = m.take([32], F32)
        zh = m.take([32], F32)
        uf = m.take([32], F32)

        ORDER = gru_order()
        PZ = [bank[g][:, 0:128].rearrange("p (a g c) -> p a g c", a=4, g=2) for g in range(2)]
        PN = [bank[2 + g][:, 0:64].rearrange("p (a c) -> p a c", a=4) for g in range(2)]
        HALF = [slice(0, 16), slice(16, 32)]

        small_in = sem("small_in")
        raw_in = [sem(f"raw_in{i}") for i in range(4)]
        x_in = sem("x_in")
        wal_in = sem("wal_in")
        wal_used = sem("wal_used")
        consts_done = sem("consts_done")
        w_hi = sem("w_hi")
        w_lo = sem("w_lo")
        x_hi = sem("x_hi")
        x_lo = sem("x_lo")
        gi_mm = sem("gi_mm")
        gi_evac = sem("gi_evac")
        gi_hi = sem("gi_hi")
        gi_lo = sem("gi_lo")
        h_init = sem("h_init")
        pads = sem("pads")
        pad_row = sem("pad_row")
        rz_mm, n_mm = two("rz_mm"), two("n_mm")
        rz_pre, n_read = two("rz_pre"), two("n_read")
        rz_act, n_pre, n_act = two("rz_act"), two("n_pre"), two("n_act")
        om_ready = two("om_ready")
        u_f32, u_hi, u_ready = two("u_f32"), two("u_hi"), two("u_ready")
        zh_hi, zh_f32, zh_ready = two("zh_hi"), two("zh_f32"), two("zh_ready")
        gin_staged = sem("gin_staged")
        h_new = sem("h_new")
        h_kept = sem("h_kept")

        with nc.Block() as block:

            @block.sync
            def _(sp):
                sp.dma_start(cst[:, :], consts[:, 0:264]).then_inc(small_in, 16)
                sp.dma_start(cstage[:, :], consts[:, 264:264 + FM * 128]).then_inc(small_in, 16)
                sp.dma_start(bia[:, :, :], bias).then_inc(small_in, 16)
                sp.dma_start(cond[:, :, :], condT).then_inc(small_in, 16)
                sp.dma_start(av[:, :], avec).then_inc(small_in, 16)
                sp.dma_start(gq[:, :], gqk).then_inc(small_in, 16)
                sp.dma_start(wrf[:, :, :], wr).then_inc(small_in, 16)
                sp.dma_start(xc[:, :, :], xT[:, :, 0:CH]).then_inc(x_in, 16)
                for i in range(2 * KT):
                    if i >= 4:
                        sp.wait_ge(w_lo, i - 3)
                    src = wih if i < KT else whh
                    sp.dma_start(raw[:, i % 4, :], src[:, i % KT, :]).then_inc(raw_in[i % 4], 16)
                def load_w_quarter(c):
                    for i, w in enumerate((w1f, w2f, w3f)):
                        n = WN // P // NCH
                        sp.dma_start(wal[:, i, :], w[:, bass.ts(c, n)]).then_inc(wal_in, 16)

                load_w_quarter(0)
                with sp.Fori(1, NCH) as c:
                    sp.wait_ge(x_lo, c * KT)
                    sp.dma_start(xc[:, :, :], xT[:, :, bass.ts(c, CH)]).then_inc(x_in, 16)
                    sp.wait_ge(wal_used, c)
                    load_w_quarter(c)

            @block.tensor
            def _(pe):
                def project_x(c):
                    for mt in range(GM):
                        if mt == 0:
                            pe.wait_ge(x_lo, c * KT + KT)
                        if mt < 4:
                            pe.wait_ge(gi_evac, c * GM + mt)
                        else:
                            pe.wait_ge(gi_evac, c * GM + (mt - 3))
                        n = 0
                        for wp, xp in ((0, 0), (0, 1), (1, 0)):
                            for k in range(KT):
                                mm = nc.tensor.matmul(bank[4 + mt % 4][:, :], wihs[:, wp, k, mt, :], xs[:, xp, k, :],
                                                      start=(n == 0), stop=(n == 3 * KT - 1))
                                n += 1
                        mm.then_inc(gi_mm, 1)

                def step(n0, n1, s, it):
                    left = {}
                    for k, j, gates in ORDER:
                        for g in gates:
                            left[(j // 2, g == 2)] = left.get((j // 2, g == 2), 0) + 1
                    opened, seen = set(), set()
                    for k, j, gates in ORDER:
                        half, khalf = j // 2, k // 2
                        if gates != (2,) and (half, 0) not in opened:
                            opened.add((half, 0))
                            pe.wait_ge(rz_pre[half], n0)
                            x_part = girz[:, it].rearrange("p a (g c) -> p a g c", g=2)[:, :, :, HALF[half]]
                            nc.tensor.matmul(PZ[half][:, 0:2], id16[:, :], x_part, start=True, stop=False,
                                             skip_group_check=True)
                        if 2 in gates and (half, 1) not in opened:
                            opened.add((half, 1))
                            pe.wait_ge(n_read[half], n0)
                            b_part = bhn.rearrange("p a k b -> p a (k b)")[:, :, HALF[half]]
                            nc.tensor.matmul(PN[half][:, 0:2], id16[:, :], b_part, start=True, stop=False,
                                             skip_group_check=True)
                        if khalf not in seen:
                            seen.add(khalf)
                            pe.wait_ge(zh_ready[khalf], n0)
                            pe.wait_ge(u_ready[khalf], n0)
                        o = (j % 2) * B
                        for g in gates:
                            for part in range(2):
                                dst = PZ[half][:, :, g, o:o + B] if g < 2 else PN[half][:, :, o:o + B]
                                mm = nc.tensor.matmul(dst, whhs[:, part, k, g * KT + j, :], mv[:, 1 - s % 2, k],
                                                      start=False, stop=False, skip_group_check=True)
                            left[(half, g == 2)] -= 1
                            if left[(half, g == 2)] == 0:
                                mm.then_inc((n_mm if g == 2 else rz_mm)[half], 1)

                pe.wait_ge(consts_done, 5)
                pe.wait_ge(w_lo, KT)

                def steps(c):
                    pe.wait_ge(w_lo, 2 * KT)
                    pe.wait_ge(h_init, 4)
                    with pe.Fori(0, TC // UN) as i:
                        n = [pe.snap(c * TC + i * UN + s) for s in range(UN + 1)]
                        pe.wait_ge(gi_lo, c * 8 + 8)
                        for s in range(UN):
                            step(n[s], n[s + 1], s, i * UN + s)

                project_x(0)
                with pe.Fori(0, NCH - 1) as c:
                    steps(c)
                    project_x(c + 1)
                steps(NCH - 1)

            @block.scalar
            def _(act):
                A = nc.scalar
                act.wait_ge(small_in, 7 * 16)
                A.activation(id1[:, :], ident, ACT.Copy).then_inc(consts_done, 1)
                A.activation(id16[:, :], ident, ACT.Copy, scale=SX).then_inc(consts_done, 1)
                A.activation(sel.rearrange("p a b -> p (a b)"), cstage[:, :], ACT.Copy).then_inc(consts_done, 1)
                A.activation(H16[:, :], cond.rearrange("p a b -> p (a b)"), ACT.Copy, scale=SX).then_inc(h_init, 1)
                A.activation(mv[:, 1, :, 0, :], cond[:, :, :], ACT.Copy, scale=SX).then_inc(h_init, 1)
                for i in range(2 * KT):
                    act.wait_ge(raw_in[i % 4], 16 * (i // 4 + 1))
                    w = wihs if i < KT else whhs
                    A.activation(w[:, 0, i % KT].rearrange("p a b -> p (a b)"), raw[:, i % 4, :], ACT.Copy,
                                 scale=SW).then_inc(w_hi, 1)
                    if i == KT - 1:
                        act.wait_ge(x_in, 16)
                        for k in range(KT):
                            A.activation(xs[:, 0, k, :], xc[:, k, :], ACT.Copy, scale=SX).then_inc(x_hi, 1)
                act.wait_ge(consts_done, 5)
                act.wait_ge(pad_row, 1)

                def step(n0, n1, s, it):
                    for g in range(2):
                        act.wait_ge(rz_pre[g], n1)
                        A.activation(rz[:, :, HALF[g]], rzp[:, :, HALF[g]], ACT.Sigmoid,
                                     scale=1 / SWX).then_inc(rz_act[g], 1)
                        act.wait_ge(n_pre[g], n1)
                        A.activation(nn[:, HALF[g]], npre[:, HALF[g]], ACT.Tanh, scale=1 / SWX).then_inc(n_act[g], 1)
                    A.activation(n5[:, :, 4], gin[:, it + 1], ACT.Copy).then_inc(gin_staged, 1)

                def read_projections(c):
                    for mt in range(GM):
                        act.wait_ge(gi_mm, c * GM + mt + 1)
                        if mt < 8:
                            if mt < 2:
                                act.wait_ge(gi_lo, c * 8 + mt)
                            else:
                                act.wait_ge(gi_lo, c * 8 + (mt - 1))
                            A.activation(tmp[:, mt % 2, :], bank[4 + mt % 4][:, :], ACT.Identity,
                                         scale=1 / SX, bias=bgi[:, mt:mt + 1]).then_inc(gi_evac, 1)
                        else:
                            j = mt - 8
                            A.activation(gin[:, 0:TC, j * B:(j + 1) * B],
                                         bank[4 + mt % 4].rearrange("p (t b) -> p t b", b=B), ACT.Identity,
                                         bias=bgi[:, mt:mt + 1]).then_inc(gi_evac, 1)
                    act.wait_ge(gi_evac, c * GM + GM)
                    A.activation(n5[:, :, 4], gin[:, 0], ACT.Copy).then_inc(gin_staged, 1)

                def steps(c):
                    with act.Fori(0, TC // UN) as i:
                        n = [act.snap(c * TC + i * UN + s) for s in range(UN + 1)]
                        for s in range(UN):
                            step(n[s], n[s + 1], s, i * UN + s)

                read_projections(0)
                with act.Fori(0, NCH - 1) as c:
                    steps(c)
                    act.wait_ge(x_in, c * 16 + 32)
                    for k in range(KT):
                        A.activation(xs[:, 0, k, :], xc[:, k, :], ACT.Copy, scale=SX).then_inc(x_hi, 1)
                    read_projections(c + 1)
                steps(NCH - 1)

            @block.vector
            def _(dve):
                V = nc.vector
                V.memset(ones[:, :], 1.0).then_inc(consts_done, 1)
                V.memset(epsb[:, :], 1e-6)
                dve.wait_ge(small_in, 7 * 16)
                V.tensor_tensor(bgi[:, 0:8], bia[:, 0, 0:8], bia[:, 1, 0:8], ALU.add).then_inc(pads, 1)
                dve.wait_ge(pads, 1)
                V.tensor_scalar(bgi[:, 0:8], bgi[:, 0:8], SW, None, ALU.mult)
                V.tensor_scalar(bgi[:, 8:12], bia[:, 0, 8:12], SWX, None, ALU.mult)
                V.tensor_scalar(bhf[:, :, :], bia[:, 1, 8:12].unsqueeze(2).broadcast_to((P, 4, B)), SW, None,
                                ALU.mult).then_inc(pads, 1)
                dve.wait_ge(pads, 2)
                V.tensor_copy(bhn[:, 0], bhf[:, :, :]).then_inc(pads, 1)
                dve.wait_ge(pads, 3)
                V.tensor_tensor(bhn[:, 1], bhf[:, :, :], bhn[:, 0], ALU.subtract).then_inc(consts_done, 1)
                V.memset(mv[:, 1, :, 2:4, :], 0.0).then_inc(h_init, 1)
                dve.wait_ge(h_init, 3)
                V.tensor_tensor(mv[:, 1, :, 1, :], H16.rearrange("p (k b) -> p k b", k=KT), mv[:, 1, :, 0, :],
                                ALU.subtract).then_inc(h_init, 1)
                for i in range(2 * KT):
                    dve.wait_ge(w_hi, i + 1)
                    w = wihs if i < KT else whhs
                    V.scalar_tensor_tensor(w[:, 1, i % KT].rearrange("p a b -> p (a b)"), raw[:, i % 4, :], SW,
                                           w[:, 0, i % KT].rearrange("p a b -> p (a b)"), ALU.mult,
                                           ALU.subtract).then_inc(w_lo, 1)
                    if i == KT - 1:
                        for k in range(KT):
                            dve.wait_ge(x_hi, k + 1)
                            V.scalar_tensor_tensor(xs[:, 1, k, :], xc[:, k, :], SX, xs[:, 0, k, :], ALU.mult,
                                                   ALU.subtract).then_inc(x_lo, 1)

                def halves(a):
                    return a.rearrange("p (j c) -> p j c", j=2)

                def step(n0, n1, s):
                    u_parts = [mv[:, s % 2, 2 * g:2 * g + 2] for g in range(2)]

                    def sum_rz(g):
                        if g == 0:
                            dve.wait_ge(h_new, n0)
                        dve.wait_ge(rz_mm[g], n1)
                        V.tensor_reduce(rzp[:, :, HALF[g]], PZ[g].rearrange("p a g c -> p g c a"), AX.X,
                                        ALU.add).then_inc(rz_pre[g], 1)

                    def times_r(g):
                        dve.wait_ge(rz_act[g], n1)
                        dve.wait_ge(n_mm[g], n1)
                        V.tensor_tensor(n5[:, HALF[g], 0:4], PN[g].rearrange("p a c -> p c a"),
                                        rz[:, 0, HALF[g]].unsqueeze(2).broadcast_to((P, 16, 4)),
                                        ALU.mult).then_inc(n_read[g], 1)

                    def one_minus_z(g):
                        V.tensor_scalar(om[:, HALF[g]], rz[:, 1, HALF[g]], -SX, SX, ALU.mult,
                                        ALU.add).then_inc(om_ready[g], 1)

                    def sum_n(g):
                        dve.wait_ge(n_read[g], n1)
                        V.tensor_reduce(npre[:, HALF[g]], n5[:, HALF[g]], AX.X, ALU.add).then_inc(n_pre[g], 1)

                    def form_u(g):
                        dve.wait_ge(n_act[g], n1)
                        V.tensor_tensor(uf[:, HALF[g]], nn[:, HALF[g]], om[:, HALF[g]], ALU.mult).then_inc(u_f32[g], 1)
                        V.tensor_tensor(u_parts[g][:, :, 2], halves(nn[:, HALF[g]]), halves(om[:, HALF[g]]),
                                        ALU.mult).then_inc(u_hi[g], 1)

                    def low_u(g):
                        dve.wait_ge(u_hi[g], n1)
                        V.tensor_tensor(u_parts[g][:, :, 3], halves(uf[:, HALF[g]]), u_parts[g][:, :, 2],
                                        ALU.subtract).then_inc(u_ready[g], 1)

                    sum_rz(0)
                    times_r(0)
                    one_minus_z(0)
                    sum_n(0)
                    sum_rz(1)
                    form_u(0)
                    times_r(1)
                    low_u(0)
                    one_minus_z(1)
                    sum_n(1)
                    form_u(1)
                    low_u(1)

                def split_projections(c):
                    for mt in range(8):
                        g0, j = mt // 4, mt % 4
                        col = slice(g0 * 32 + j * B, g0 * 32 + (j + 1) * B)
                        src = tmp[:, mt % 2, :].rearrange("p (t b) -> p t b", b=B)
                        dve.wait_ge(gi_evac, c * GM + mt + 1)
                        V.tensor_copy(girz[:, 0:TC, 0, col], src).then_inc(gi_hi, 1)
                        dve.wait_ge(gi_hi, c * 8 + mt + 1)
                        V.tensor_tensor(girz[:, 0:TC, 1, col], src, girz[:, 0:TC, 0, col],
                                        ALU.subtract).then_inc(gi_lo, 1)
                    dve.wait_ge(wal_in, c * 48 + 48)
                    V.tensor_reduce(gsum[:, c, :], wal[:, :, :], AX.X, ALU.add,
                                    apply_absolute_value=True).then_inc(wal_used, 1)
                    dve.wait_ge(gin_staged, c * (TC + 1) + 1)

                def steps(c):
                    with dve.Fori(0, TC // UN) as i:
                        n = [dve.snap(c * TC + i * UN + s) for s in range(UN + 1)]
                        for s in range(UN):
                            step(n[s], n[s + 1], s)

                split_projections(0)
                with dve.Fori(0, NCH - 1) as c:
                    steps(c)
                    for k in range(KT):
                        dve.wait_ge(x_hi, c * KT + KT + k + 1)
                        V.scalar_tensor_tensor(xs[:, 1, k, :], xc[:, k, :], SX, xs[:, 0, k, :], ALU.mult,
                                               ALU.subtract).then_inc(x_lo, 1)
                    split_projections(c + 1)
                steps(NCH - 1)

            @block.gpsimd
            def _(pool):
                G = nc.gpsimd

                def halves(a):
                    return a.rearrange("p (j c) -> p j c", j=2)

                G.memset(gin[:, TC], 0.0).then_inc(pad_row, 1)
                pool.wait_ge(h_init, 4)

                def step(n0, n1, s, t):
                    for g in range(2):
                        z_parts = mv[:, s % 2, 2 * g:2 * g + 2]
                        pool.wait_ge(rz_act[g], n1)
                        if g == 0:
                            pool.wait_ge(h_new, n0)
                        G.tensor_tensor(z_parts[:, :, 0], halves(rz[:, 1, HALF[g]]), halves(H16[:, HALF[g]]),
                                        ALU.mult).then_inc(zh_hi[g], 1)
                        G.tensor_tensor(zh[:, HALF[g]], rz[:, 1, HALF[g]], H16[:, HALF[g]],
                                        ALU.mult).then_inc(zh_f32[g], 1)
                        pool.wait_ge(zh_hi[g], n1)
                        pool.wait_ge(zh_f32[g], n1)
                        G.tensor_tensor(z_parts[:, :, 1], halves(zh[:, HALF[g]]), z_parts[:, :, 0],
                                        ALU.subtract).then_inc(zh_ready[g], 1)
                    pool.wait_ge(u_f32[0], n1)
                    pool.wait_ge(u_f32[1], n1)
                    G.tensor_tensor(H16[:, :], uf[:, :], zh[:, :], ALU.add).then_inc(h_new, 1)
                    pool.wait_ge(h_new, n1)
                    G.tensor_copy(hx[:, t], H16[:, :]).then_inc(h_kept, 1)

                with pool.Fori(0, NCH) as c:
                    with pool.Fori(0, TC // UN) as i:
                        n = [pool.snap(c * TC + i * UN + s) for s in range(UN + 1)]
                        for s in range(UN):
                            step(n[s], n[s + 1], s, c * TC + i * UN + s)

        m = Mem(arena, base)
        wgus = m.take([2, FM, 2, KT, P], F16)
        wdns = m.take([2, FM, D], F16)
        gul = m.take([3, 2 * KT * P], F32)
        dnl = m.take([3, D], F32)
        hc = m.take([2, KT, CH], F16)
        hid = m.take([2, FM, CH], F16)
        xr = m.take([KT, CH], F32)
        sg = m.take([2, CH], F32)
        ga = m.take([CH], F32)
        gb = m.take([CH], F32)
        hf = m.take([2, CH], F32)
        wT = m.take([CH], F16)
        sc = m.take([4, E], F32)
        mx = m.take([4, 8], F32)
        ix = m.take([4, 8], F32).bitcast(U32)
        ixf = m.take([4, 2], F32)
        dif = m.take([4, 2], F32)
        pr = m.take([4, 2], F32)
        w1st = m.take([4, E], F32)
        w2nd = m.take([4, E], F32)
        wgt = m.take([4, E], F32)
        wp = m.take([4, 2 * E], F16)

        raw2_in = [sem(f"raw2_in{i}") for i in range(3)]
        xr_in = sem("xr_in")
        wr_done, wT_zero = sem("wr_done"), sem("wT_zero")
        gu_hi, gu_lo = sem("gu_hi"), sem("gu_lo")
        hc_hi, hc_lo = sem("hc_hi"), sem("hc_lo")
        score_mm, scores = sem("score_mm"), sem("scores")
        top8, top_ix, top_dif, probs = sem("top8"), sem("top_ix"), sem("top_dif"), sem("probs")
        ixf_done = sem("ixf_done")
        wts_a, wts, wp_hi, wp_done = sem("wts_a"), sem("wts"), sem("wp_hi"), sem("wp_done")
        wT_mm, wT_done = sem("wT_mm"), sem("wT_done")
        gate_mm, sig_done, ga_done, gb_done = sem("gate_mm"), sem("sig_done"), sem("ga_done"), sem("gb_done")
        wb_mm, hf_done, hid_hi, hid_lo = sem("wb_mm"), sem("hf_done"), sem("hid_hi"), sem("hid_lo")
        down_mm, down_out = sem("down_mm"), sem("down_out")

        def chunk_of_states(c, k):
            return hx[:, bass.ts(c, TC), k * B:(k + 1) * B]

        def tb(a):
            return a.rearrange("p (t b) -> p t b", b=B)

        with nc.Block() as block:

            @block.sync
            def _(sp):
                sp.dma_start(xr[:, :, :], xT[:, :, 0:CH]).then_inc(xr_in, 16)
                for mt in range(FM):
                    if mt >= 3:
                        sp.wait_ge(gu_lo, 2 * (mt - 2))
                    sp.dma_start(gul[:, mt % 3, :], wgu[:, mt].rearrange("p a k f -> p (a k f)")).then_inc(raw2_in[mt % 3], 16)
                    sp.dma_start(dnl[:, mt % 3, :], wdn[:, mt, :]).then_inc(raw2_in[mt % 3], 16)
                with sp.Fori(1, NCH) as c:
                    sp.wait_ge(down_out, c * KT)
                    sp.dma_start(xr[:, :, :], xT[:, :, bass.ts(c, CH)]).then_inc(xr_in, 16)

            @block.tensor
            def _(pe):
                pe.wait_ge(wr_done, 2)
                pe.wait_ge(wT_zero, 1)

                def chunk(c, first):
                    pe.wait_ge(hc_lo, c * KT + KT)
                    SC = bank[7][:, 0:64].rearrange("p (s e) -> p s e", s=4)
                    for st in range(4):
                        n = 0
                        for part in range(2):
                            for k in range(KT):
                                mm = nc.tensor.matmul(SC[:, st, :], hc[:, part, k, st * P:(st + 1) * P],
                                                      wrs[:, k].rearrange("p a e -> p (a e)"),
                                                      start=(n == 0), stop=(n == 2 * KT - 1))
                                n += 1
                    mm.then_inc(score_mm, 1)
                    for mt in range(FM):
                        if first:
                            pe.wait_ge(gu_lo, 2 * mt + 2)
                        if mt < 2:
                            pe.wait_ge(gb_done, c * FM + mt)
                        else:
                            pe.wait_ge(gb_done, c * FM + (mt - 1))
                        for a in range(2):
                            n = 0
                            for w_, h_ in ((0, 0), (0, 1), (1, 0)):
                                for k in range(KT):
                                    mm = nc.tensor.matmul(bank[2 * a + mt % 2][:, :], wgus[:, w_, mt, a, k, :],
                                                          hc[:, h_, k, :], start=(n == 0), stop=(n == 3 * KT - 1))
                                    n += 1
                        mm.then_inc(gate_mm, 1)
                        if mt == 0:
                            pe.wait_ge(wp_done, c + 1)
                            WT = bank[7].bitcast(F16)[0:2 * E, 0:CH]
                            for st in range(4):
                                mm = nc.tensor.transpose(WT[:, st * P:(st + 1) * P], wp[:, st, :], id1[:, :])
                            mm.then_inc(wT_mm, 1)
                            pe.wait_ge(wT_done, c + 1)
                        pe.wait_ge(hf_done, c * FM + mt)
                        nc.tensor.matmul(bank[6][:, :], sel[:, mt, :], wT[:, :], start=True, stop=True)\
                            .then_inc(wb_mm, 1)
                    pe.wait_ge(hid_lo, c * FM + FM)
                    for j in range(KT):
                        if j < 2:
                            pe.wait_ge(down_out, c * KT + j)
                        else:
                            pe.wait_ge(down_out, c * KT + (j - 1))
                        n = 0
                        for mt in range(FM):
                            for w_, h_ in ((0, 0), (0, 1), (1, 0)):
                                mm = nc.tensor.matmul(bank[4 + j % 2][:, :], wdns[:, w_, mt, j * P:(j + 1) * P],
                                                      hid[:, h_, mt, :], start=(n == 0), stop=(n == 3 * FM - 1))
                                n += 1
                        mm.then_inc(down_mm, 1)

                chunk(0, True)
                with pe.Fori(1, NCH) as c:
                    chunk(c, False)

            @block.scalar
            def _(act):
                A = nc.scalar

                def split_states(c):
                    for k in range(KT):
                        A.activation(tb(hc[:, 0, k, :]), chunk_of_states(c, k), ACT.Copy).then_inc(hc_hi, 1)

                def split_weights(mt):
                    act.wait_ge(raw2_in[mt % 3], 32 * (mt // 3 + 1))
                    A.activation(wgus[:, 0, mt].rearrange("p a k f -> p (a k f)"), gul[:, mt % 3, :], ACT.Copy,
                                 scale=SW).then_inc(gu_hi, 1)
                    A.activation(wdns[:, 0, mt, :], dnl[:, mt % 3, :], ACT.Copy, scale=SW).then_inc(gu_hi, 1)

                def chunk(c, first, last):
                    act.wait_ge(top_dif, 2 * c + 2)
                    A.activation(pr[:, :, :], dif[:, :, :], ACT.Sigmoid, scale=1 / SWX).then_inc(probs, 1)
                    for mt in range(FM + 1):
                        if first and mt + 2 < FM:
                            split_weights(mt + 2)
                        if mt < FM:
                            act.wait_ge(gate_mm, c * FM + mt + 1)
                            A.activation(sg[:, mt % 2, :], bank[mt % 2][:, :], ACT.Sigmoid, scale=1 / SWX)\
                                .then_inc(sig_done, 1)
                        if mt == 0:
                            act.wait_ge(wT_mm, c + 1)
                            A.activation(wT[0:2 * E, :], bank[7].bitcast(F16)[0:2 * E, 0:CH], ACT.Copy)\
                                .then_inc(wT_done, 1)
                        if mt >= 1:
                            act.wait_ge(hf_done, c * FM + mt)
                            if mt == 1:
                                act.wait_ge(down_mm, c * KT)
                            A.activation(hid[:, 0, mt - 1, :], hf[:, (mt - 1) % 2, :], ACT.Copy).then_inc(hid_hi, 1)
                    if not last:
                        split_states(c + 1)

                A.activation(wrs[:, :, 0, :], wrf[:, :, :], ACT.Copy, scale=SW).then_inc(wr_done, 1)
                split_states(0)
                split_weights(0)
                split_weights(1)
                chunk(0, True, False)
                with act.Fori(1, NCH - 1) as c:
                    chunk(c, False, False)
                chunk(NCH - 1, False, True)

            @block.vector
            def _(dve):
                V = nc.vector

                def split_states(c):
                    for k in range(KT):
                        dve.wait_ge(hc_hi, c * KT + k + 1)
                        V.tensor_tensor(tb(hc[:, 1, k, :]), chunk_of_states(c, k), tb(hc[:, 0, k, :]),
                                        ALU.subtract).then_inc(hc_lo, 1)

                def split_weights(mt):
                    dve.wait_ge(gu_hi, 2 * mt + 1)
                    V.scalar_tensor_tensor(wgus[:, 1, mt].rearrange("p a k f -> p (a k f)"), gul[:, mt % 3, :], SW,
                                           wgus[:, 0, mt].rearrange("p a k f -> p (a k f)"), ALU.mult,
                                           ALU.subtract).then_inc(gu_lo, 1)
                    dve.wait_ge(gu_hi, 2 * mt + 2)
                    V.scalar_tensor_tensor(wdns[:, 1, mt, :], dnl[:, mt % 3, :], SW, wdns[:, 0, mt, :], ALU.mult,
                                           ALU.subtract).then_inc(gu_lo, 1)

                def route(c):
                    dve.wait_ge(score_mm, c + 1)
                    V.tensor_reduce(sc[:, :, :], bank[7][:, 0:64].rearrange("p (s a e) -> p s e a", s=4, a=2), AX.X,
                                    ALU.add).then_inc(scores, 1)
                    dve.wait_ge(hc_lo, KT)
                    dve.wait_ge(scores, c + 1)
                    for st in range(4):
                        V.max(mx[:, st, :], sc[:, st, :]).then_inc(top8, 1)
                    dve.wait_ge(top8, 4 * c + 4)
                    V.tensor_tensor(dif[:, :, 0], mx[:, :, 0], mx[:, :, 1], ALU.subtract).then_inc(top_dif, 1)
                    V.tensor_tensor(dif[:, :, 1], mx[:, :, 1], mx[:, :, 0], ALU.subtract).then_inc(top_dif, 1)
                    for st in range(4):
                        V.max_index(ix[:, st, :], mx[:, st, :], sc[:, st, :]).then_inc(top_ix, 1)
                    dve.wait_ge(top_ix, 4 * c + 4)
                    V.tensor_copy(ixf[:, :, :], ix[:, :, 0:2]).then_inc(ixf_done, 1)
                    dve.wait_ge(ixf_done, c + 1)
                    dve.wait_ge(probs, c + 1)
                    for st in range(4):
                        V.tensor_scalar(w1st[:, st, :], iota, ixf[:, st, 0:1], pr[:, st, 0:1], ALU.is_equal,
                                        ALU.mult).then_inc(wts_a, 1)
                        V.tensor_scalar(w2nd[:, st, :], iota, ixf[:, st, 1:2], pr[:, st, 1:2], ALU.is_equal,
                                        ALU.mult).then_inc(wts_a, 1)
                    dve.wait_ge(wts_a, 8 * c + 8)
                    V.tensor_tensor(wgt[:, :, :], w1st[:, :, :], w2nd[:, :, :], ALU.add).then_inc(wts, 1)
                    dve.wait_ge(wts, c + 1)
                    V.tensor_copy(wp[:, :, 0:E], wgt[:, :, :]).then_inc(wp_hi, 1)
                    dve.wait_ge(wp_hi, c + 1)
                    V.tensor_tensor(wp[:, :, E:2 * E], wgt[:, :, :], wp[:, :, 0:E], ALU.subtract).then_inc(wp_done, 1)

                def down(c, j):
                    dve.wait_ge(down_mm, c * KT + j + 1)
                    V.scalar_tensor_tensor(chunk_of_states(c, j), tb(bank[4 + j % 2][:, :]), 1 / SWX,
                                           tb(xr[:, j, :]), ALU.mult, ALU.add).then_inc(down_out, 1)

                def chunk(c, first, last):
                    route(c)
                    for mt in range(FM + 1):
                        if first and mt + 2 < FM:
                            split_weights(mt + 2)
                        if mt < FM:
                            dve.wait_ge(sig_done, c * FM + mt + 1)
                            V.scalar_tensor_tensor(ga[:, :], bank[mt % 2][:, :], 1 / SWX, sg[:, mt % 2, :], ALU.mult,
                                                   ALU.mult).then_inc(ga_done, 1)
                            dve.wait_ge(ga_done, c * FM + mt + 1)
                            V.scalar_tensor_tensor(gb[:, :], bank[2 + mt % 2][:, :], 1 / SW, ga[:, :], ALU.mult,
                                                   ALU.mult).then_inc(gb_done, 1)
                            dve.wait_ge(gb_done, c * FM + mt + 1)
                            dve.wait_ge(wb_mm, c * FM + mt + 1)
                            V.tensor_tensor(hf[:, mt % 2, :], bank[6][:, :], gb[:, :], ALU.mult).then_inc(hf_done, 1)
                        if mt >= 1:
                            dve.wait_ge(hid_hi, c * FM + mt)
                            V.tensor_tensor(hid[:, 1, mt - 1, :], hf[:, (mt - 1) % 2, :], hid[:, 0, mt - 1, :],
                                            ALU.subtract).then_inc(hid_lo, 1)
                    dve.wait_ge(xr_in, 16 * c + 16)
                    for j in range(KT):
                        if j == KT - 1 and not last:
                            split_states(c + 1)
                        down(c, j)

                V.memset(wT[:, :], 0.0).then_inc(wT_zero, 1)
                dve.wait_ge(wr_done, 1)
                V.scalar_tensor_tensor(wrs[:, :, 1, :], wrf[:, :, :], SW, wrs[:, :, 0, :], ALU.mult,
                                       ALU.subtract).then_inc(wr_done, 1)
                split_states(0)
                split_weights(0)
                split_weights(1)
                chunk(0, True, False)
                with dve.Fori(1, NCH - 1) as c:
                    chunk(c, False, False)
                chunk(NCH - 1, False, True)


        S = T
        m = Mem(arena, base)
        o2p = m.take([2, KT, NTOK], F16)
        wqs = m.take([2, KT, G3], F16)
        wos = m.take([2, KT, D], F16)
        rinv = m.take([NTOK], F32)
        start_c = m.at
        wel = m.take([KT, 2 * D], F32)
        wql = m.take([KT, G3], F32)
        wol = m.take([KT, D], F32)
        sqx = m.take([2, CH], F32)
        rms = m.take([2, CH], F32)
        ss = m.take([2 * KT, B], F32)
        g16 = m.take([KT], F32)
        gam = m.take([3], F32)
        gam2 = m.take([3], F32)

        we_in, wo_in = sem("we_in"), sem("wo_in")
        wq_in = [sem(f"wq_in{k}") for k in range(KT)]
        sqx_done, ssx_mm, rms_done, rinv_done = sem("sqx_done"), sem("ssx_mm"), sem("rms_done"), sem("rinv_done")
        wq_hi, wq_lo = sem("wq_hi"), sem("wq_lo")
        ss_mm, gam_mm = sem("ss_mm"), sem("gam_mm")
        prep = sem("prep")

        with nc.Block() as block:

            @block.sync
            def _(sp):
                sp.dma_start(wel[:, :, :], wemb).then_inc(we_in, 16)
                for k in range(KT):
                    sp.dma_start(wql[:, k, :], wqkv[:, k, :]).then_inc(wq_in[k], 16)
                sp.dma_start(wol[:, :, :], wout).then_inc(wo_in, 16)

            @block.tensor
            def _(pe):
                for c in range(NCH):
                    if c >= 2:
                        pe.wait_ge(rms_done, c - 1)
                    for k in range(KT):
                        pe.wait_ge(sqx_done, c * KT + k + 1)
                        nc.tensor.matmul(bank[c % 2][:, :], ones[:, :], sqx[:, k % 2, :], start=(k == 0),
                                         stop=(k == KT - 1)).then_inc(ssx_mm, 1)
                nc.tensor.matmul(bank[3][:, 0:3 * NCH], ones[:, :], gsum.rearrange("p c w -> p (c w)"), start=True,
                                 stop=True).then_inc(gam_mm, 1)
                pe.wait_ge(we_in, 16)
                SS = bank[2][:, 0:2 * KT * B].rearrange("p (m b) -> p m b", b=B)
                for mt in range(2 * KT):
                    for k in range(KT):
                        mm = nc.tensor.matmul(SS[:, mt, :], wel[:, k, mt * P:(mt + 1) * P], cond[:, k, :],
                                              start=(k == 0), stop=(k == KT - 1))
                mm.then_inc(ss_mm, 1)

            @block.scalar
            def _(act):
                A = nc.scalar
                for c in range(NCH):
                    for k in range(KT):
                        n = c * KT + k
                        if n >= 2:
                            act.wait_ge(ssx_mm, n - 1)
                        A.activation(tb(sqx[:, k % 2, :]), chunk_of_states(c, k), ACT.Square).then_inc(sqx_done, 1)
                    act.wait_ge(ssx_mm, c * KT + KT)
                    if c >= 2:
                        act.wait_ge(rinv_done, c - 1)
                    A.activation(rms[:, c % 2, :], bank[c % 2][:, :], ACT.Sqrt, scale=1 / D,
                                 bias=epsb[:, :]).then_inc(rms_done, 1)
                for k in range(KT):
                    act.wait_ge(wq_in[k], 16)
                    A.activation(wqs[:, 0, k, :], wql[:, k, :], ACT.Copy, scale=SW).then_inc(wq_hi, 1)
                act.wait_ge(wo_in, 16)
                A.activation(wos[:, 0], wol[:, :, :], ACT.Copy, scale=SW).then_inc(wq_hi, 1)

            @block.vector
            def _(dve):
                V = nc.vector
                for c in range(NCH):
                    dve.wait_ge(rms_done, c + 1)
                    V.reciprocal(rinv[:, c * CH:(c + 1) * CH], rms[:, c % 2, :]).then_inc(rinv_done, 1)
                dve.wait_ge(gam_mm, 1)
                V.tensor_reduce(gam[:, :], bank[3][:, 0:3 * NCH].rearrange("p (c w) -> p w c", w=3), AX.X,
                                ALU.add).then_inc(prep, 1)
                dve.wait_ge(prep, 1)
                V.tensor_scalar(gam2[:, :], gam[:, :], 1 / WN, 1e-8, ALU.mult, ALU.add).then_inc(prep, 1)
                dve.wait_ge(prep, 2)
                V.tensor_scalar(thr[:, 0, :], gam2[:, :], 0.5, None, ALU.mult)
                V.tensor_scalar(thr[:, 1, :], gam2[:, :], -0.5, None, ALU.mult)
                V.tensor_scalar(g16[:, :], av[:, 2 * KT:3 * KT], SX, None, ALU.mult)
                V.tensor_scalar(gqs[:, :], gq[:, :], 1 / SW, None, ALU.mult).then_inc(prep, 1)
                dve.wait_ge(ss_mm, 1)
                V.tensor_tensor(ss[:, :, :], bank[2][:, 0:2 * KT * B].rearrange("p (m b) -> p m b", b=B),
                                av[:, 0:2 * KT].unsqueeze(2).broadcast_to((P, 2 * KT, B)), ALU.add).then_inc(prep, 1)
                dve.wait_ge(prep, 4)
                V.scalar_tensor_tensor(ada[:, 0], ss[:, 0:KT, :], 1.0,
                                       g16[:, :].unsqueeze(2).broadcast_to((P, KT, B)), ALU.add, ALU.mult)
                V.tensor_scalar(ada[:, 1], ss[:, KT:2 * KT, :], SX, None, ALU.mult).then_inc(prep, 1)
                for k in range(KT):
                    dve.wait_ge(wq_hi, k + 1)
                    V.scalar_tensor_tensor(wqs[:, 1, k, :], wql[:, k, :], SW, wqs[:, 0, k, :], ALU.mult,
                                           ALU.subtract).then_inc(wq_lo, 1)
                dve.wait_ge(wq_hi, KT + 1)
                V.scalar_tensor_tensor(wos[:, 1], wol[:, :, :], SW, wos[:, 0], ALU.mult,
                                       ALU.subtract).then_inc(wq_lo, 1)

        m = Mem(arena, start_c)
        xnt = m.take([KT, S], F32)
        xnf = m.take([KT, S], F32)
        xn = m.take([2, KT, S], F16)
        sqq = m.take([2, 2 * S], F32)
        sr = m.take([2, 2 * S], F32)
        ri = m.take([2 * S], F32)
        qn = m.take([2, 2 * S], F32)
        qkp = m.take([2, 4, 2, S], F16)
        qs = m.take([H, S], F16)
        ks = m.take([H, S], F16)
        vh = m.take([2, H, DH + 1], F16)
        vl = m.take([2, H, DH + 1], F16)
        mxs = m.take([2, H], F32)
        mT = m.take([P], F16)
        pf = m.take([2, 2 * S], F32)
        ph = m.take([2, 2, S], F16)
        pl = m.take([2, 2, S], F16)
        rc = m.take([2, 4], F32)
        of = m.take([2, H, DH], F32)
        oTf = m.take([KT, S], F32)
        oTp = m.take([2, KT, S], F16)
        o2f = m.take([2, 2 * S], F32)

        KC = SX * SX
        vzero = sem("vzero")
        xnt_done, xnf_done, xn_hi, xn_lo = sem("xnt_done"), sem("xnf_done"), sem("xn_hi"), sem("xn_lo")
        s_mm, max_done, mT_mm, mT_done, mrow_in = (sem("s_mm"), sem("max_done"), sem("mT_mm"), sem("mT_done"),
                                                   sem("mrow_in"))
        qk_mm, sq_done, ssq_mm, sqrt_done, ri_done, qn_done, qk_hi, qk_lo = (
            sem("qk_mm"), sem("sq_done"), sem("ssq_mm"), sem("sqrt_done"), sem("ri_done"), sem("qn_done"),
            sem("qk_hi"), sem("qk_lo"))
        stack_in = sem("stack_in")
        st_mm, exp_done, ph_done, pl_done, av_mm, rc_done, o_done, av_head = (
            sem("st_mm"), sem("exp_done"), sem("ph_done"), sem("pl_done"), sem("av_mm"), sem("rc_done"),
            sem("o_done"), sem("av_head"))
        v_mm, vh_done, v_done = sem("v_mm"), sem("vh_done"), sem("v_done")
        oT_mm, oT_done, oTl_done, wo_mm, o2f_done, o2_hi, o2_lo = (
            sem("oT_mm"), sem("oT_done"), sem("oTl_done"), sem("wo_mm"), sem("o2f_done"), sem("o2_hi"), sem("o2_lo"))

        with nc.Block() as block:

            @block.sync
            def _(sp):
                def load_stacks(b):
                    sp.wait_ge(qk_lo, 4 * b + 4)
                    for to, pair, parts in ((qs, 0, (0, 1, 0)), (ks, 2, (0, 0, 1))):
                        for row, part in enumerate(parts):
                            for hh in range(4):
                                dst = to[32 * row:32 * row + 32].rearrange("p (t h) s -> p h t s", h=4)[:, hh]
                                src = qkp[32 * hh:32 * hh + 32, part, pair:pair + 2].rearrange("p a b s -> p (a b) s")
                                sp.dma_start(dst, src).then_inc(stack_in, 16)

                def load_max(b):
                    sp.wait_ge(mT_done, b + 1)
                    for qt in range(2):
                        sp.dma_start(qs[96:97, :, qt * P:(qt + 1) * P], mT[16 * qt:16 * qt + 16, :])\
                            .then_inc(mrow_in, 16)

                load_stacks(0)
                with sp.Fori(0, B - 1) as b:
                    load_max(b)
                    sp.wait_ge(st_mm, H * b + H)
                    load_stacks(b + 1)
                load_max(B - 1)

            @block.tensor
            def _(pe):
                def project_qk(b, first):
                    pe.wait_ge(xn_lo, b + 1)

                    def squares(tp):
                        pe.wait_ge(sq_done, 4 * b + tp + 1)
                        if not first or tp > 0:
                            pe.wait_ge(sqrt_done, 4 * b + tp)
                        if tp == 0 and not first:
                            pe.wait_ge(oT_done, 2 * b - 2)
                        nc.tensor.matmul(bank[6][:, :], headones, sqq[:, tp % 2, :], start=True, stop=True)\
                            .then_inc(ssq_mm, 1)

                    for tp in range(4):
                        if tp >= 2:
                            pe.wait_ge(qn_done, 4 * b + tp - 1)
                        elif not first:
                            pe.wait_ge(o2f_done, 2 * (b - 1))
                        for a in range(2):
                            mt = 2 * tp + a
                            n = 0
                            for w_, x_ in ((0, 0), (0, 1), (1, 0)):
                                for k in range(KT):
                                    mm = nc.tensor.matmul(bank[4 + tp % 2][:, a * S:(a + 1) * S],
                                                          wqs[:, w_, k, mt * P:(mt + 1) * P], xn[:, x_, k, :],
                                                          start=(n == 0), stop=(n == 3 * KT - 1))
                                    n += 1
                        mm.then_inc(qk_mm, 1)
                        if tp > 0:
                            squares(tp - 1)
                    squares(3)

                def project_v(b):
                    pe.wait_ge(qn_done, 4 * b + 4)
                    for vt in range(2):
                        n = 0
                        for w_, x_ in ((0, 0), (0, 1), (1, 0)):
                            for k in range(KT):
                                mm = nc.tensor.matmul(bank[4 + vt][:, :], xn[:, x_, k, vt * P:(vt + 1) * P],
                                                      wqs[:, w_, k, 2 * D:3 * D], start=(n == 0),
                                                      stop=(n == 3 * KT - 1))
                                n += 1
                        mm.then_inc(v_mm, 1)

                def scores(b):
                    pe.wait_ge(stack_in, 24 * 16 * (b + 1))
                    pe.wait_ge(o_done, 4 * b)
                    for h in range(H):
                        if h >= 2:
                            pe.wait_ge(max_done, H * b + h - 1)
                        for qt in range(2):
                            mm = nc.tensor.matmul(bank[h % 2][:, qt * S:(qt + 1) * S],
                                                  qs[0:96, h, qt * P:(qt + 1) * P], ks[0:96, h, :], start=True,
                                                  stop=True)
                        mm.then_inc(s_mm, 1)

                def attend(b):
                    def scores_t(h):
                        if h == 0:
                            pe.wait_ge(mrow_in, 32 * (b + 1))
                        if h < 2:
                            pe.wait_ge(exp_done, H * b)
                        else:
                            pe.wait_ge(exp_done, H * b + h - 1)
                        for kt in range(2):
                            mm = nc.tensor.matmul(bank[2 + h % 2][:, kt * S:(kt + 1) * S],
                                                  ks[0:97, h, kt * P:(kt + 1) * P], qs[0:97, h, :], start=True,
                                                  stop=True)
                        mm.then_inc(st_mm, 1)

                    def values(h):
                        q4 = h // 4
                        O = bank[q4 % 2][:, 0:2 * 4 * (DH + 1)].rearrange("p (q h d) -> p q h d", q=2, h=4)
                        if h % 4 == 0 and q4 >= 2:
                            pe.wait_ge(o_done, 4 * b + q4 - 1)
                        pe.wait_ge(pl_done, H * b + h + 1)
                        for qt in range(2):
                            n = 0
                            for kt in range(2):
                                for p_, v_ in ((ph, vh), (ph, vl), (pl, vh)):
                                    mm = nc.tensor.matmul(O[:, qt, h % 4, :], p_[:, h % 2, kt, qt * P:(qt + 1) * P],
                                                          v_[:, kt, h, :], start=(n == 0), stop=(n == 5))
                                    n += 1
                        mm.then_inc(av_head, 1)

                    scores_t(0)
                    scores_t(1)
                    for h in range(H):
                        values(h)
                        if h + 2 < H:
                            scores_t(h + 2)

                def project_out(b, last):
                    pe.wait_ge(o_done, 4 * b + 4)
                    pe.wait_ge(mT_done, b + 1)
                    pe.wait_ge(sqrt_done, 4 * b + (4 if last else 8))
                    for qt in range(2):
                        for k in range(KT):
                            mm = nc.tensor.transpose(bank[7 - qt][:, k * P:(k + 1) * P],
                                                     of[:, qt].rearrange("p h d -> p (h d)")[:, k * P:(k + 1) * P],
                                                     ident)
                        mm.then_inc(oT_mm, 1)
                    pe.wait_ge(oTl_done, 2 * b + 2)
                    pe.wait_ge(v_done, 2 * b + (2 if last else 4))
                    for jp in range(2):
                        for a in range(2):
                            j = 2 * jp + a
                            n = 0
                            for w_, x_ in ((0, 0), (0, 1), (1, 0)):
                                for k in range(KT):
                                    mm = nc.tensor.matmul(bank[4 + jp][:, a * S:(a + 1) * S],
                                                          wos[:, w_, k, j * P:(j + 1) * P], oTp[:, x_, k, :],
                                                          start=(n == 0), stop=(n == 3 * KT - 1))
                                    n += 1
                        mm.then_inc(wo_mm, 1)

                def turn_max(b):
                    pe.wait_ge(max_done, H * b + H)
                    pe.wait_ge(oT_done, 2 * b)
                    nc.tensor.transpose(bank[7][0:32, 0:P], mxs.rearrange("p q h -> p (q h)"), ident)\
                        .then_inc(mT_mm, 1)

                project_qk(0, True)
                project_v(0)
                pe.wait_ge(vzero, 5)
                with pe.Fori(0, B - 1) as b:
                    scores(b)
                    turn_max(b)
                    project_qk(b + 1, False)
                    attend(b)
                    project_v(b + 1)
                    project_out(b, False)
                scores(B - 1)
                turn_max(B - 1)
                attend(B - 1)
                project_out(B - 1, True)

            @block.scalar
            def _(act):
                A = nc.scalar

                def norm_x(b, first):
                    act.wait_ge(xnt_done, b + 1)
                    for k in range(KT):
                        A.activation(xnf[:, k, :], xnt[:, k, :], ACT.Identity, scale=ada[:, 0, k, bass.ds(b, 1)],
                                     bias=ada[:, 1, k, bass.ds(b, 1)]).then_inc(xnf_done, 1)
                    act.wait_ge(xnf_done, KT * b + KT)
                    if not first:
                        act.wait_ge(v_mm, 2 * b)
                    A.activation(xn[:, 0], xnf[:, :, :], ACT.Copy).then_inc(xn_hi, 1)

                def norm_qk(b):
                    for tp in range(5):
                        if tp < 4:
                            act.wait_ge(qk_mm, 4 * b + tp + 1)
                            A.activation(sqq[:, tp % 2, :], bank[4 + tp % 2][:, :], ACT.Square, scale=1 / SWX)\
                                .then_inc(sq_done, 1)
                        if tp > 0:
                            act.wait_ge(ssq_mm, 4 * b + tp)
                            A.activation(sr[:, (tp - 1) % 2, :], bank[6][:, :], ACT.Sqrt, scale=1 / DH,
                                         bias=epsb[:, :]).then_inc(sqrt_done, 1)
                        if tp > 0:
                            act.wait_ge(qn_done, 4 * b + tp)
                            A.activation(qkp[:, 0, tp - 1].rearrange("p a s -> p (a s)"), qn[:, (tp - 1) % 2, :],
                                         ACT.Copy).then_inc(qk_hi, 1)

                def high_v(b):
                    for vt in range(2):
                        act.wait_ge(v_mm, 2 * b + vt + 1)
                        A.activation(vh[:, vt, :, 0:DH], bank[4 + vt].rearrange("p (h d) -> p h d", h=H), ACT.Copy,
                                     scale=1 / SW).then_inc(vh_done, 1)

                def turn_max(b):
                    act.wait_ge(mT_mm, b + 1)
                    act.wait_ge(mrow_in, 32 * b)
                    A.activation(mT[0:32, :], bank[7][0:32, 0:P], ACT.Copy, scale=-1 / KC).then_inc(mT_done, 1)

                def softmax(b):
                    def exp(h):
                        act.wait_ge(st_mm, H * b + h + 1)
                        if h >= 2:
                            act.wait_ge(pl_done, H * b + h - 1)
                        A.activation(pf[:, h % 2, :], bank[2 + h % 2][:, :], ACT.Exp, scale=DH ** -0.5 / KC)\
                            .then_inc(exp_done, 1)

                    exp(0)
                    for h in range(H):
                        if h + 1 < H:
                            exp(h + 1)
                        act.wait_ge(exp_done, H * b + h + 1)
                        if h >= 2:
                            act.wait_ge(av_head, H * b + h - 1)
                        A.activation(ph[:, h % 2].rearrange("p k s -> p (k s)"), pf[:, h % 2, :], ACT.Copy)\
                            .then_inc(ph_done, 1)

                def finish(b):
                    for qt in range(2):
                        act.wait_ge(oT_mm, 2 * b + qt + 1)
                        src = bank[7 - qt].rearrange("p (k s) -> p k s", k=KT)
                        A.activation(oTf[:, :, qt * P:(qt + 1) * P], src, ACT.Copy)
                        A.activation(oTp[:, 0, :, qt * P:(qt + 1) * P], src, ACT.Copy).then_inc(oT_done, 1)
                    for jp in range(2):
                        act.wait_ge(o2f_done, 2 * b + jp + 1)
                        A.activation(o2p[:, 0, 2 * jp:2 * jp + 2, bass.ts(b, S)],
                                     o2f[:, jp].rearrange("p (a s) -> p a s", a=2), ACT.Copy).then_inc(o2_hi, 1)

                norm_x(0, True)
                norm_qk(0)
                high_v(0)
                with act.Fori(0, B - 1) as b:
                    norm_x(b + 1, False)
                    turn_max(b)
                    norm_qk(b + 1)
                    softmax(b)
                    high_v(b + 1)
                    finish(b)
                turn_max(B - 1)
                softmax(B - 1)
                finish(B - 1)

            @block.vector
            def _(dve):
                V = nc.vector

                def norm_x(b):
                    x1 = hx.rearrange("p t (k b) -> p b k t", k=KT)[:, b]
                    r = rinv.rearrange("p (t b) -> p b t", b=B)[:, b].unsqueeze(1).broadcast_to((P, KT, S))
                    V.tensor_tensor(xnt[:, :, :], x1, r, ALU.mult).then_inc(xnt_done, 1)
                    dve.wait_ge(xn_hi, b + 1)
                    V.tensor_tensor(xn[:, 1], xnf[:, :, :], xn[:, 0], ALU.subtract).then_inc(xn_lo, 1)

                def norm_qk(b):
                    for tp in range(4):
                        dve.wait_ge(sqrt_done, 4 * b + tp + 1)
                        V.reciprocal(ri[:, :], sr[:, tp % 2, :]).then_inc(ri_done, 1)
                        dve.wait_ge(ri_done, 4 * b + tp + 1)
                        V.scalar_tensor_tensor(qn[:, tp % 2, :], bank[4 + tp % 2][:, :], gqs[:, tp // 2:tp // 2 + 1],
                                               ri[:, :], ALU.mult, ALU.mult).then_inc(qn_done, 1)
                        dve.wait_ge(qk_hi, 4 * b + tp + 1)
                        V.tensor_tensor(qkp[:, 1, tp].rearrange("p a s -> p (a s)"), qn[:, tp % 2, :],
                                        qkp[:, 0, tp].rearrange("p a s -> p (a s)"), ALU.subtract).then_inc(qk_lo, 1)

                def low_v(b):
                    for vt in range(2):
                        dve.wait_ge(vh_done, 2 * b + vt + 1)
                        V.scalar_tensor_tensor(vl[:, vt, :, 0:DH], bank[4 + vt].rearrange("p (h d) -> p h d", h=H),
                                               1 / SW, vh[:, vt, :, 0:DH], ALU.mult, ALU.subtract).then_inc(v_done, 1)

                def maxima(b):
                    for h in range(H):
                        dve.wait_ge(s_mm, H * b + h + 1)
                        V.tensor_reduce(mxs[:, :, h], bank[h % 2].rearrange("p (q s) -> p q s", q=2), AX.X,
                                        ALU.max).then_inc(max_done, 1)

                def attend(b):
                    def normalise(q4):
                        O = bank[q4 % 2][:, 0:2 * 4 * (DH + 1)].rearrange("p (q h d) -> p q h d", q=2, h=4)
                        dve.wait_ge(av_head, H * b + 4 * q4 + 4)
                        V.reciprocal(rc[:, :, :], O[:, :, :, DH]).then_inc(rc_done, 1)
                        dve.wait_ge(rc_done, 4 * b + q4 + 1)
                        V.tensor_tensor(of[:, :, 4 * q4:4 * q4 + 4, :], O[:, :, :, 0:DH],
                                        rc[:, :, :].unsqueeze(3).broadcast_to((P, 2, 4, DH)),
                                        ALU.mult).then_inc(o_done, 1)

                    for h in range(H):
                        dve.wait_ge(ph_done, H * b + h + 1)
                        V.tensor_tensor(pl[:, h % 2].rearrange("p k s -> p (k s)"), pf[:, h % 2, :],
                                        ph[:, h % 2].rearrange("p k s -> p (k s)"), ALU.subtract).then_inc(pl_done, 1)
                        if h % 4 == 1 and h > 4:
                            normalise(h // 4 - 1)
                    normalise(3)

                def finish(b):
                    for qt in range(2):
                        dve.wait_ge(oT_done, 2 * b + qt + 1)
                        part = slice(qt * P, (qt + 1) * P)
                        V.tensor_tensor(oTp[:, 1, :, part], oTf[:, :, part], oTp[:, 0, :, part],
                                        ALU.subtract).then_inc(oTl_done, 1)
                    for jp in range(2):
                        dve.wait_ge(wo_mm, 2 * b + jp + 1)
                        V.scalar_tensor_tensor(o2f[:, jp, :], bank[4 + jp][:, :], 1 / SW,
                                               oTf[:, 2 * jp:2 * jp + 2, :].rearrange("p a s -> p (a s)"), ALU.mult,
                                               ALU.add).then_inc(o2f_done, 1)
                    for jp in range(2):
                        dve.wait_ge(o2_hi, 2 * b + jp + 1)
                        V.tensor_tensor(o2p[:, 1, 2 * jp:2 * jp + 2, bass.ts(b, S)],
                                        o2f[:, jp].rearrange("p (a s) -> p a s", a=2),
                                        o2p[:, 0, 2 * jp:2 * jp + 2, bass.ts(b, S)], ALU.subtract).then_inc(o2_lo, 1)

                V.memset(ks[96:97, :, :], KC).then_inc(vzero, 1)
                V.memset(mxs[:, :, :], 0.0).then_inc(vzero, 1)
                V.memset(vh[:, :, :, DH:DH + 1], 1.0).then_inc(vzero, 1)
                V.memset(vl[:, :, :, DH:DH + 1], 0.0).then_inc(vzero, 2)
                norm_x(0)
                norm_qk(0)
                low_v(0)
                with dve.Fori(0, B - 1) as b:
                    norm_x(b + 1)
                    maxima(b)
                    norm_qk(b + 1)
                    attend(b)
                    low_v(b + 1)
                    finish(b)
                maxima(B - 1)
                attend(B - 1)
                finish(B - 1)

        m = Mem(arena, base)
        assert m.take([2, KT, NTOK], F16).shape == o2p.shape
        w12 = m.take([HM, 2, KT, P], F16)
        w3q = m.take([HM, D], F16)
        tl = m.take([3, 3 * D], F32)
        neg = m.take([2, 3 * D], F16)
        sgd = m.take([2, CH], F32)
        hdf = m.take([2, CH], F32)
        hdp = m.take([2, HM, CH], F16)
        yo = m.take([2, CH], F32)

        t_in = [sem(f"t_in{i}") for i in range(3)]
        neg_done, q_done = sem("neg_done"), sem("q_done")
        up_mm, sgd_done, hdf_done, hdp_hi, hdp_lo = (sem("up_mm"), sem("sgd_done"), sem("hdf_done"), sem("hdp_hi"),
                                                     sem("hdp_lo"))
        y_mm, y_done, y_out = sem("y_mm"), sem("y_done"), two("y_out")

        with nc.Block() as block:

            @block.sync
            def _(sp):
                for mt in range(HM):
                    if mt >= 3:
                        sp.wait_ge(q_done, 3 * (mt - 2))
                    for i, w in enumerate((w1T, w2T)):
                        sp.dma_start(tl[:, mt % 3, i * D:(i + 1) * D], w[:, mt].rearrange("p k h -> p (k h)"))\
                            .then_inc(t_in[mt % 3], 16)
                    sp.dma_start(tl[:, mt % 3, 2 * D:3 * D], w3T[:, mt, :]).then_inc(t_in[mt % 3], 16)
                with sp.Fori(0, NCH) as c:
                    for j in range(KT):
                        sp.wait_ge(y_done, c * KT + j + 1)
                        sp.dma_start(out[:, j, bass.ts(c, CH)], yo[:, j % 2, :]).then_inc(y_out[j % 2], 16)
                sp.wait_ge(y_out[0], 8 * KT * NCH)
                sp.wait_ge(y_out[1], 8 * KT * NCH)

            @block.gpsimd
            def _(pool):
                for mt in range(HM):
                    pool.wait_ge(t_in[mt % 3], 48 * (mt // 3 + 1))
                    if mt >= 2:
                        pool.wait_ge(q_done, 3 * (mt - 1))
                    for i in range(3):
                        nc.gpsimd.tensor_scalar(neg[:, mt % 2, i * D:(i + 1) * D], tl[:, mt % 3, i * D:(i + 1) * D],
                                                thr[:, 1, i:i + 1], None, ALU.is_lt).then_inc(neg_done, 1)

            @block.tensor
            def _(pe):
                def chunk(c, first):
                    for mt in range(HM):
                        if first:
                            pe.wait_ge(q_done, 3 * mt + 3)
                        if mt < 2:
                            pe.wait_ge(hdf_done, c * HM + mt)
                        else:
                            pe.wait_ge(hdf_done, c * HM + mt - 1)
                        for a in range(2):
                            n = 0
                            for part in range(2):
                                for k in range(KT):
                                    mm = nc.tensor.matmul(bank[2 * a + mt % 2][:, :], w12[:, mt, a, k, :],
                                                          o2p[:, part, k, bass.ts(c, CH)], start=(n == 0),
                                                          stop=(n == 2 * KT - 1))
                                    n += 1
                        mm.then_inc(up_mm, 1)
                    pe.wait_ge(hdp_lo, c * HM + HM)
                    for j in range(KT):
                        if j < 2:
                            pe.wait_ge(y_done, c * KT + j)
                        else:
                            pe.wait_ge(y_done, c * KT + j - 1)
                        n = 0
                        for mt in range(HM):
                            for part in range(2):
                                mm = nc.tensor.matmul(bank[4 + j % 2][:, :], w3q[:, mt, j * P:(j + 1) * P],
                                                      hdp[:, part, mt, :], start=(n == 0), stop=(n == 2 * HM - 1))
                                n += 1
                        mm.then_inc(y_mm, 1)

                chunk(0, True)
                with pe.Fori(1, NCH) as c:
                    chunk(c, False)

            @block.scalar
            def _(act):
                A = nc.scalar

                def chunk(c):
                    for mt in range(HM + 1):
                        if mt < HM:
                            act.wait_ge(up_mm, c * HM + mt + 1)
                            A.activation(sgd[:, mt % 2, :], bank[mt % 2][:, :], ACT.Sigmoid, scale=1 / SX)\
                                .then_inc(sgd_done, 1)
                        if mt > 0:
                            act.wait_ge(hdf_done, c * HM + mt)
                            if mt == 1:
                                act.wait_ge(y_mm, c * KT)
                            A.activation(hdp[:, 0, mt - 1, :], hdf[:, (mt - 1) % 2, :], ACT.Copy).then_inc(hdp_hi, 1)

                with act.Fori(0, NCH) as c:
                    chunk(c)

            @block.vector
            def _(dve):
                V = nc.vector

                def quantise(mt):
                    for i in range(3):
                        dve.wait_ge(neg_done, 3 * mt + i + 1)
                        dst = w12[:, mt, i].rearrange("p k h -> p (k h)") if i < 2 else w3q[:, mt, :]
                        V.scalar_tensor_tensor(dst, tl[:, mt % 3, i * D:(i + 1) * D], thr[:, 0, i:i + 1],
                                               neg[:, mt % 2, i * D:(i + 1) * D], ALU.is_gt,
                                               ALU.subtract).then_inc(q_done, 1)

                def chunk(c, first):
                    for mt in range(HM + 1):
                        if first and mt + 2 < HM:
                            quantise(mt + 2)
                        if mt < HM:
                            dve.wait_ge(hdp_lo, c * HM + (mt - 1 if mt >= 2 else 0))
                            dve.wait_ge(sgd_done, c * HM + mt + 1)
                            V.scalar_tensor_tensor(hdf[:, mt % 2, :], bank[2 + mt % 2][:, :], 1 / SX,
                                                   sgd[:, mt % 2, :], ALU.mult, ALU.mult).then_inc(hdf_done, 1)
                        if mt > 0:
                            dve.wait_ge(hdp_hi, c * HM + mt)
                            V.tensor_tensor(hdp[:, 1, mt - 1, :], hdf[:, (mt - 1) % 2, :], hdp[:, 0, mt - 1, :],
                                            ALU.subtract).then_inc(hdp_lo, 1)
                    for j in range(KT):
                        dve.wait_ge(y_mm, c * KT + j + 1)
                        if not first or j >= 2:
                            dve.wait_ge(y_out[j % 2], (c * 2 + j // 2) * 16)
                        x1 = hx.rearrange("p t (k b) -> p k b t", k=KT)[:, j, bass.ts(c, 2), :]
                        V.tensor_tensor(yo[:, j % 2, :].rearrange("p (b t) -> p b t", b=2),
                                        bank[4 + j % 2].rearrange("p (b t) -> p b t", b=2), x1,
                                        ALU.add).then_inc(y_done, 1)

                quantise(0)
                quantise(1)
                chunk(0, True)
                with dve.Fori(1, NCH) as c:
                    chunk(c, False)


NAMES = ["xT", "condT", "wih", "whh", "bias", "wr", "wgu", "wdn", "wemb", "avec", "gqk", "wqkv", "wout",
         "w1f", "w2f", "w3f", "w1T", "w2T", "w3T", "consts"]


def kernel(**inputs):
    import numpy as np
    import concourse.bacc as bacc
    from concourse.bass_utils import run_bass_kernel_spmd

    i = {k: np.asarray(v) for k, v in inputs.items()}

    def rows(w):
        return w.reshape(KT, P, -1).transpose(1, 0, 2)

    a = {}
    a["xT"] = rows(i["x"].transpose(2, 1, 0).reshape(D, NTOK))
    a["condT"] = rows(i["cond_2048"].T)
    a["wih"], a["whh"] = rows(i["L0_cond_W_ih"]), rows(i["L0_cond_W_hh"])
    a["bias"] = np.stack([i["L0_cond_b_ih"].reshape(GM, P).T, i["L0_cond_b_hh"].reshape(GM, P).T], 1)
    a["wr"] = rows(i["L0_ffn_w_gate_router"].T)
    gate = i["L0_ffn_w_gate_proj"].reshape(E * F, D).T.reshape(KT, P, FM, P)
    up = i["L0_ffn_w_up_proj"].reshape(E * F, D).T.reshape(KT, P, FM, P)
    a["wgu"] = np.stack([gate, up]).transpose(2, 3, 0, 1, 4)
    a["wdn"] = i["L0_ffn_w_down_proj"].transpose(0, 2, 1).reshape(FM, P, D).transpose(1, 0, 2)
    a["wemb"] = rows(i["L1_cond_W_emb"])
    a["avec"] = np.concatenate([i["L1_cond_b_emb"].reshape(2 * KT, P).T, i["L1_cond_g_norm"].reshape(KT, P).T], 1)
    a["gqk"] = np.stack([np.tile(i["L1_cond_g_q"], 4), np.tile(i["L1_cond_g_k"], 4)], 1)
    a["wqkv"], a["wout"] = rows(i["L1_cond_W_qkv"]), rows(i["L1_cond_W_out"])
    for n in "123":
        a[f"w{n}f"] = i[f"L1_ffn_w{n}"].reshape(P, -1)
    a["w1T"] = i["L1_ffn_w1"].T.reshape(KT, P, HM, P).transpose(1, 2, 0, 3)
    a["w2T"] = i["L1_ffn_w2"].T.reshape(KT, P, HM, P).transpose(1, 2, 0, 3)
    a["w3T"] = i["L1_ffn_w3"].T.reshape(HM, P, D).transpose(1, 0, 2)
    c = np.zeros((P, 264 + FM * P), np.float32)
    c[:, 0:128] = np.eye(P)
    c[:, 128:256] = np.kron(np.eye(P // DH), np.ones((DH, DH)))
    c[:, 256:264] = np.arange(E)
    for f in range(FM * P):
        c[f // F, 264 + f] = 1.0
        c[E + f // F, 264 + f] = 1.0
    a["consts"] = c

    nc = bacc.Bacc("TRN2", target_bir_lowering=False, num_devices=1)
    arrays, args = {}, []
    for name in NAMES:
        v = np.ascontiguousarray(a[name])
        arrays[f"in_{name}"] = v
        args.append(nc.dram_tensor(f"in_{name}", v.shape, mybir.dt.from_np(v.dtype), kind="ExternalInput").ap())
    y = nc.dram_tensor("out_y", (P, KT, NTOK), F32, kind="ExternalOutput").ap()
    mixed_net_kernel(nc, *args, y)
    r = run_bass_kernel_spmd(nc, [arrays], core_ids=[0])
    got = r.results[0]["out_y"]
    return np.ascontiguousarray(got.reshape(P, KT, B, T).transpose(2, 3, 1, 0).reshape(B, T, D))
```

```python
from contextlib import ExitStack

import concourse.bass as bass
from concourse import mybir

F32 = mybir.dt.float32
F16 = mybir.dt.float16
U32 = mybir.dt.uint32
ACT = mybir.ActivationFunctionType
ALU = mybir.AluOpType
AX = mybir.AxisListType

P = 128
D = 512
KT = D // P
T = 256
B = 8
NTOK = T * B
CH = 512
NCH = NTOK // CH
TC = CH // B
G3 = 3 * D
GM = G3 // P
E = 8
F = 192
FM = E * F // P
H = 16
DH = D // H
HF = 1408
HM = HF // P
WN = HF * D

SW = 64.0
SX = 16.0
SWX = SW * SX

UN = 16
ARENA = 190 * 1024


class Mem:

    def __init__(self, arena, start):
        self.arena, self.at = arena, start

    def take(self, shape, dt, parts=P):
        n = 1
        for s in shape:
            n *= s
        size = n * (2 if dt == F16 else 4)
        size = (size + 31) // 32 * 32
        a = self.arena[0:parts, self.at // 4:(self.at + size) // 4]
        self.at += size
        assert self.at <= ARENA, self.at
        a = a.bitcast(dt) if dt != F32 else a
        a = a[:, 0:n]
        if len(shape) > 1:
            names = "abcdef"[:len(shape)]
            a = a.rearrange("p (%s) -> p %s" % (" ".join(names), " ".join(names)),
                            **{c: s for c, s in zip(names, shape)})
        return a


def gru_order():
    RZ, N, ALL = (0, 1), (2,), (0, 1, 2)

    def block(ks, js, gates):
        return [(k, j, gates) for j in js for k in ks]

    return (block((0, 1), (0, 1), ALL) + block((0, 1), (2,), RZ) + block((2, 3), (0, 1), RZ)
            + block((2, 3), (0, 1), N) + block((0, 1), (3,), RZ) + block((2, 3), (2, 3), RZ)
            + block((0, 1, 2, 3), (2, 3), N))


def mixed_net_kernel(nc, xT, condT, wih, whh, bias, wr, wgu, wdn, wemb, avec, gqk, wqkv, wout,
                     w1f, w2f, w3f, w1T, w2T, w3T, consts, out):
    with ExitStack() as ctx:
        def sb(name, shape, dt):
            return ctx.enter_context(nc.sbuf_tensor(name, shape, dt))

        def sem(name):
            return ctx.enter_context(nc.semaphore(name))

        def two(name):
            return [sem(name + "_0"), sem(name + "_1")]

        bank = [ctx.enter_context(nc.psum_tensor(f"bank{i}", [P, 512], F32)) for i in range(8)]
        arena = sb("arena", [P, ARENA // 4], F32)

        cst = sb("cst", [P, 264], F32)
        ident = cst[:, 0:128]
        headones = cst[:, 128:256]
        iota = cst[:, 256:264]
        ones = sb("ones", [P, 128], F32)
        id1 = sb("id1", [P, 128], F16)
        id16 = sb("id16", [P, 128], F16)
        sel = sb("sel", [P, FM, 128], F16)
        bia = sb("bia", [P, 2, GM], F32)
        bgi = sb("bgi", [P, GM], F32)
        bhn = sb("bhn", [P, 2, 4, B], F16)
        bhf = sb("bhf", [P, 4, B], F32)
        cond = sb("cond", [P, KT, B], F32)
        gsum = sb("gsum", [P, NCH, 3], F32)
        thr = sb("thr", [P, 2, 3], F32)
        av = sb("av", [P, 3 * KT], F32)
        gq = sb("gq", [P, 2, DH], F32)
        gg = sb("gg", [P, DH], F32)
        ada = sb("ada", [P, 2, KT, B], F32)
        epsb = sb("epsb", [P, 1], F32)
        wrs = sb("wrs", [P, KT, 2, E], F16)
        wrf = sb("wrf", [P, KT, E], F32)

        top = Mem(arena, 0)
        hx = top.take([T, KT * B], F32)
        base = top.at

        m = Mem(arena, base)
        wihs = m.take([2, KT, GM, P], F16)
        whhs = m.take([2, KT, GM, P], F16)
        girz = m.take([TC + 1, 2, 2 * KT * B], F16)
        gin = m.take([TC + 1, KT * B], F32)
        xc = m.take([KT, CH], F32)
        xs = m.take([2, KT, CH], F16)
        raw = m.take([4, G3], F32)
        tmp = m.take([2, CH], F32)
        wal = m.take([3, WN // P // NCH], F32)
        cstage = m.take([FM * 128], F32)
        mv = m.take([2, KT, 4, B], F16)
        H16 = m.take([KT * B], F32)
        rzp = m.take([2, 32], F32)
        rz = m.take([2, 32], F32)
        n5 = m.take([32, 5], F32)
        npre = m.take([32], F32)
        nn = m.take([32], F32)
        om = m.take([32], F32)
        zh = m.take([32], F32)
        uf = m.take([32], F32)

        ORDER = gru_order()
        PZ = [bank[g][:, 0:128].rearrange("p (a g c) -> p a g c", a=4, g=2) for g in range(2)]
        PN = [bank[2 + g][:, 0:64].rearrange("p (a c) -> p a c", a=4) for g in range(2)]
        HALF = [slice(0, 16), slice(16, 32)]

        small_in = sem("small_in")
        raw_in = [sem(f"raw_in{i}") for i in range(4)]
        x_in = sem("x_in")
        wal_in = sem("wal_in")
        wal_used = sem("wal_used")
        consts_done = sem("consts_done")
        w_hi = sem("w_hi")
        w_lo = sem("w_lo")
        x_hi = sem("x_hi")
        x_lo = sem("x_lo")
        gi_mm = sem("gi_mm")
        gi_evac = sem("gi_evac")
        gi_hi = sem("gi_hi")
        gi_lo = sem("gi_lo")
        h_init = sem("h_init")
        pads = sem("pads")
        pad_row = sem("pad_row")
        rz_mm, n_mm = two("rz_mm"), two("n_mm")
        rz_pre, n_read = two("rz_pre"), two("n_read")
        rz_act, n_pre, n_act = two("rz_act"), two("n_pre"), two("n_act")
        om_ready = two("om_ready")
        u_f32, u_hi, u_ready = two("u_f32"), two("u_hi"), two("u_ready")
        zh_hi, zh_f32, zh_ready = two("zh_hi"), two("zh_f32"), two("zh_ready")
        gin_staged = sem("gin_staged")
        h_new = sem("h_new")
        h_kept = sem("h_kept")

        with nc.Block() as block:

            @block.sync
            def _(sp):
                sp.dma_start(cst[:, :], consts[:, 0:264]).then_inc(small_in, 16)
                sp.dma_start(cstage[:, :], consts[:, 264:264 + FM * 128]).then_inc(small_in, 16)
                sp.dma_start(bia[:, :, :], bias).then_inc(small_in, 16)
                sp.dma_start(cond[:, :, :], condT).then_inc(small_in, 16)
                sp.dma_start(av[:, :], avec).then_inc(small_in, 16)
                sp.dma_start(gq[:, :, :], gqk).then_inc(small_in, 16)
                sp.dma_start(wrf[:, :, :], wr).then_inc(small_in, 16)
                sp.dma_start(xc[:, :, :], xT[:, :, 0:CH]).then_inc(x_in, 16)
                for i in range(2 * KT):
                    if i >= 4:
                        sp.wait_ge(w_lo, i - 3)
                    src = wih if i < KT else whh
                    sp.dma_start(raw[:, i % 4, :], src[:, i % KT, :]).then_inc(raw_in[i % 4], 16)
                def load_w_quarter(c):
                    for i, w in enumerate((w1f, w2f, w3f)):
                        n = WN // P // NCH
                        sp.dma_start(wal[:, i, :], w[:, bass.ts(c, n)]).then_inc(wal_in, 16)

                load_w_quarter(0)
                with sp.Fori(1, NCH) as c:
                    sp.wait_ge(x_lo, c * KT)
                    sp.dma_start(xc[:, :, :], xT[:, :, bass.ts(c, CH)]).then_inc(x_in, 16)
                    sp.wait_ge(wal_used, c)
                    load_w_quarter(c)

            @block.tensor
            def _(pe):
                def project_x(c):
                    for mt in range(GM):
                        if mt == 0:
                            pe.wait_ge(x_lo, c * KT + KT)
                        if mt < 4:
                            pe.wait_ge(gi_evac, c * GM + mt)
                        else:
                            pe.wait_ge(gi_evac, c * GM + (mt - 3))
                        n = 0
                        for wp, xp in ((0, 0), (0, 1), (1, 0)):
                            for k in range(KT):
                                mm = nc.tensor.matmul(bank[4 + mt % 4][:, :], wihs[:, wp, k, mt, :], xs[:, xp, k, :],
                                                      start=(n == 0), stop=(n == 3 * KT - 1))
                                n += 1
                        mm.then_inc(gi_mm, 1)

                def step(n1, n2, s, it):
                    left = {}
                    for k, j, gates in ORDER:
                        for g in gates:
                            left[(j // 2, g == 2)] = left.get((j // 2, g == 2), 0) + 1
                    opened, seen = set(), set()
                    for k, j, gates in ORDER:
                        half, khalf = j // 2, k // 2
                        if gates != (2,) and (half, 0) not in opened:
                            opened.add((half, 0))
                            pe.wait_ge(rz_pre[half], n1)
                            x_part = girz[:, it].rearrange("p a (g c) -> p a g c", g=2)[:, :, :, HALF[half]]
                            nc.tensor.matmul(PZ[half][:, 0:2], id16[:, :], x_part, start=True, stop=False,
                                             skip_group_check=True)
                        if 2 in gates and (half, 1) not in opened:
                            opened.add((half, 1))
                            pe.wait_ge(n_read[half], n1)
                            b_part = bhn.rearrange("p a k b -> p a (k b)")[:, :, HALF[half]]
                            nc.tensor.matmul(PN[half][:, 0:2], id16[:, :], b_part, start=True, stop=False,
                                             skip_group_check=True)
                        if khalf not in seen:
                            seen.add(khalf)
                            pe.wait_ge(zh_ready[khalf], n1)
                            pe.wait_ge(u_ready[khalf], n1)
                        o = (j % 2) * B
                        for g in gates:
                            for part in range(2):
                                dst = PZ[half][:, :, g, o:o + B] if g < 2 else PN[half][:, :, o:o + B]
                                mm = nc.tensor.matmul(dst, whhs[:, part, k, g * KT + j, :], mv[:, 1 - s % 2, k],
                                                      start=False, stop=False, skip_group_check=True)
                            left[(half, g == 2)] -= 1
                            if left[(half, g == 2)] == 0:
                                mm.then_inc((n_mm if g == 2 else rz_mm)[half], 1)

                pe.wait_ge(consts_done, 5)
                pe.wait_ge(w_lo, KT)

                def steps(c):
                    pe.wait_ge(w_lo, 2 * KT)
                    pe.wait_ge(h_init, 4)
                    with pe.Fori(0, TC // UN) as i:
                        n = [pe.snap(c * TC + i * UN + s + 1) for s in range(UN + 1)]
                        pe.wait_ge(gi_lo, c * 8 + 8)
                        for s in range(UN):
                            step(n[s], n[s + 1], s, i * UN + s)

                project_x(0)
                with pe.Fori(0, NCH - 1) as c:
                    steps(c)
                    project_x(c + 1)
                steps(NCH - 1)

            @block.scalar
            def _(act):
                A = nc.scalar
                act.wait_ge(small_in, 7 * 16)
                A.activation(id1[:, :], ident, ACT.Copy).then_inc(consts_done, 1)
                A.activation(id16[:, :], ident, ACT.Copy, scale=SX).then_inc(consts_done, 1)
                A.activation(sel.rearrange("p a b -> p (a b)"), cstage[:, :], ACT.Copy).then_inc(consts_done, 1)
                A.activation(H16[:, :], cond.rearrange("p a b -> p (a b)"), ACT.Copy, scale=SX).then_inc(h_init, 1)
                A.activation(mv[:, 1, :, 0, :], cond[:, :, :], ACT.Copy, scale=SX).then_inc(h_init, 1)
                for i in range(2 * KT):
                    act.wait_ge(raw_in[i % 4], 16 * (i // 4 + 1))
                    w = wihs if i < KT else whhs
                    A.activation(w[:, 0, i % KT].rearrange("p a b -> p (a b)"), raw[:, i % 4, :], ACT.Copy,
                                 scale=SW).then_inc(w_hi, 1)
                    if i == KT - 1:
                        act.wait_ge(x_in, 16)
                        for k in range(KT):
                            A.activation(xs[:, 0, k, :], xc[:, k, :], ACT.Copy, scale=SX).then_inc(x_hi, 1)
                act.wait_ge(consts_done, 5)
                act.wait_ge(pad_row, 1)

                def step(n1, n2, s, it):
                    for g in range(2):
                        act.wait_ge(rz_pre[g], n2)
                        A.activation(rz[:, :, HALF[g]], rzp[:, :, HALF[g]], ACT.Sigmoid,
                                     scale=1 / SWX).then_inc(rz_act[g], 1)
                        act.wait_ge(n_pre[g], n1)
                        A.activation(nn[:, HALF[g]], npre[:, HALF[g]], ACT.Tanh, scale=1 / SWX).then_inc(n_act[g], 1)
                    A.activation(n5[:, :, 4], gin[:, it + 1], ACT.Copy).then_inc(gin_staged, 1)

                def read_projections(c):
                    for mt in range(GM):
                        act.wait_ge(gi_mm, c * GM + mt + 1)
                        if mt < 8:
                            if mt < 2:
                                act.wait_ge(gi_lo, c * 8 + mt)
                            else:
                                act.wait_ge(gi_lo, c * 8 + (mt - 1))
                            A.activation(tmp[:, mt % 2, :], bank[4 + mt % 4][:, :], ACT.Identity,
                                         scale=1 / SX, bias=bgi[:, mt:mt + 1]).then_inc(gi_evac, 1)
                        else:
                            j = mt - 8
                            A.activation(gin[:, 0:TC, j * B:(j + 1) * B],
                                         bank[4 + mt % 4].rearrange("p (t b) -> p t b", b=B), ACT.Identity,
                                         bias=bgi[:, mt:mt + 1]).then_inc(gi_evac, 1)
                    act.wait_ge(gi_evac, c * GM + GM)
                    A.activation(n5[:, :, 4], gin[:, 0], ACT.Copy).then_inc(gin_staged, 1)

                def steps(c):
                    with act.Fori(0, TC // UN) as i:
                        n = [act.snap(c * TC + i * UN + s + 1) for s in range(UN + 1)]
                        for s in range(UN):
                            step(n[s], n[s + 1], s, i * UN + s)

                read_projections(0)
                with act.Fori(0, NCH - 1) as c:
                    steps(c)
                    act.wait_ge(x_in, c * 16 + 32)
                    for k in range(KT):
                        A.activation(xs[:, 0, k, :], xc[:, k, :], ACT.Copy, scale=SX).then_inc(x_hi, 1)
                    read_projections(c + 1)
                steps(NCH - 1)

            @block.vector
            def _(dve):
                V = nc.vector
                V.memset(ones[:, :], 1.0).then_inc(consts_done, 1)
                V.memset(epsb[:, :], 1e-6)
                dve.wait_ge(small_in, 7 * 16)
                V.tensor_tensor(bgi[:, 0:8], bia[:, 0, 0:8], bia[:, 1, 0:8], ALU.add).then_inc(pads, 1)
                dve.wait_ge(pads, 1)
                V.tensor_scalar(bgi[:, 0:8], bgi[:, 0:8], SW, None, ALU.mult)
                V.tensor_scalar(bgi[:, 8:12], bia[:, 0, 8:12], SWX, None, ALU.mult)
                V.tensor_scalar(bhf[:, :, :], bia[:, 1, 8:12].unsqueeze(2).broadcast_to((P, 4, B)), SW, None,
                                ALU.mult).then_inc(pads, 1)
                dve.wait_ge(pads, 2)
                V.tensor_copy(bhn[:, 0], bhf[:, :, :]).then_inc(pads, 1)
                dve.wait_ge(pads, 3)
                V.tensor_tensor(bhn[:, 1], bhf[:, :, :], bhn[:, 0], ALU.subtract).then_inc(consts_done, 1)
                V.memset(mv[:, 1, :, 2:4, :], 0.0).then_inc(h_init, 1)
                dve.wait_ge(h_init, 3)
                V.tensor_tensor(mv[:, 1, :, 1, :], H16.rearrange("p (k b) -> p k b", k=KT), mv[:, 1, :, 0, :],
                                ALU.subtract).then_inc(h_init, 1)
                for i in range(2 * KT):
                    dve.wait_ge(w_hi, i + 1)
                    w = wihs if i < KT else whhs
                    V.scalar_tensor_tensor(w[:, 1, i % KT].rearrange("p a b -> p (a b)"), raw[:, i % 4, :], SW,
                                           w[:, 0, i % KT].rearrange("p a b -> p (a b)"), ALU.mult,
                                           ALU.subtract).then_inc(w_lo, 1)
                    if i == KT - 1:
                        for k in range(KT):
                            dve.wait_ge(x_hi, k + 1)
                            V.scalar_tensor_tensor(xs[:, 1, k, :], xc[:, k, :], SX, xs[:, 0, k, :], ALU.mult,
                                                   ALU.subtract).then_inc(x_lo, 1)

                def halves(a):
                    return a.rearrange("p (j c) -> p j c", j=2)

                def step(n1, n2, s):
                    u_parts = [mv[:, s % 2, 2 * g:2 * g + 2] for g in range(2)]

                    def sum_rz(g):
                        dve.wait_ge(rz_mm[g], n1)
                        if g == 0:
                            dve.wait_ge(h_new, n1)
                        V.tensor_reduce(rzp[:, :, HALF[g]], PZ[g].rearrange("p a g c -> p g c a"), AX.X,
                                        ALU.add).then_inc(rz_pre[g], 1)

                    def times_r(g):
                        dve.wait_ge(rz_act[g], n1)
                        dve.wait_ge(n_mm[g], n1)
                        V.tensor_tensor(n5[:, HALF[g], 0:4], PN[g].rearrange("p a c -> p c a"),
                                        rz[:, 0, HALF[g]].unsqueeze(2).broadcast_to((P, 16, 4)),
                                        ALU.mult).then_inc(n_read[g], 1)

                    def one_minus_z(g):
                        V.tensor_scalar(om[:, HALF[g]], rz[:, 1, HALF[g]], -SX, SX, ALU.mult,
                                        ALU.add).then_inc(om_ready[g], 1)

                    def sum_n(g):
                        dve.wait_ge(n_read[g], n2)
                        V.tensor_reduce(npre[:, HALF[g]], n5[:, HALF[g]], AX.X, ALU.add).then_inc(n_pre[g], 1)

                    def form_u(g):
                        dve.wait_ge(n_act[g], n1)
                        V.tensor_tensor(uf[:, HALF[g]], nn[:, HALF[g]], om[:, HALF[g]], ALU.mult).then_inc(u_f32[g], 1)
                        V.tensor_tensor(u_parts[g][:, :, 2], halves(nn[:, HALF[g]]), halves(om[:, HALF[g]]),
                                        ALU.mult).then_inc(u_hi[g], 1)

                    def low_u(g):
                        dve.wait_ge(u_hi[g], n1)
                        V.tensor_tensor(u_parts[g][:, :, 3], halves(uf[:, HALF[g]]), u_parts[g][:, :, 2],
                                        ALU.subtract).then_inc(u_ready[g], 1)

                    sum_rz(0)
                    times_r(0)
                    one_minus_z(0)
                    sum_n(0)
                    sum_rz(1)
                    form_u(0)
                    times_r(1)
                    low_u(0)
                    one_minus_z(1)
                    sum_n(1)
                    form_u(1)
                    low_u(1)

                def split_projections(c):
                    for mt in range(8):
                        g0, j = mt // 4, mt % 4
                        col = slice(g0 * 32 + j * B, g0 * 32 + (j + 1) * B)
                        src = tmp[:, mt % 2, :].rearrange("p (t b) -> p t b", b=B)
                        dve.wait_ge(gi_evac, c * GM + mt + 1)
                        V.tensor_copy(girz[:, 0:TC, 0, col], src).then_inc(gi_hi, 1)
                        dve.wait_ge(gi_hi, c * 8 + mt + 1)
                        V.tensor_tensor(girz[:, 0:TC, 1, col], src, girz[:, 0:TC, 0, col],
                                        ALU.subtract).then_inc(gi_lo, 1)
                    dve.wait_ge(wal_in, c * 48 + 48)
                    V.tensor_reduce(gsum[:, c, :], wal[:, :, :], AX.X, ALU.add,
                                    apply_absolute_value=True).then_inc(wal_used, 1)
                    dve.wait_ge(gin_staged, c * (TC + 1) + 1)

                def steps(c):
                    with dve.Fori(0, TC // UN) as i:
                        n = [dve.snap(c * TC + i * UN + s + 1) for s in range(UN + 1)]
                        for s in range(UN):
                            step(n[s], n[s + 1], s)

                for g in range(2):
                    V.memset(om[:, HALF[g]], 0.0).then_inc(rz_pre[g], 1)
                    V.memset(npre[:, HALF[g]], 0.0).then_inc(n_read[g], 1)
                    V.memset(uf[:, HALF[g]], 0.0).then_inc(u_ready[g], 1)
                split_projections(0)
                with dve.Fori(0, NCH - 1) as c:
                    steps(c)
                    for k in range(KT):
                        dve.wait_ge(x_hi, c * KT + KT + k + 1)
                        V.scalar_tensor_tensor(xs[:, 1, k, :], xc[:, k, :], SX, xs[:, 0, k, :], ALU.mult,
                                               ALU.subtract).then_inc(x_lo, 1)
                    split_projections(c + 1)
                steps(NCH - 1)

            @block.gpsimd
            def _(pool):
                G = nc.gpsimd

                def halves(a):
                    return a.rearrange("p (j c) -> p j c", j=2)

                G.memset(gin[:, TC], 0.0).then_inc(pad_row, 1)
                pool.wait_ge(h_init, 4)
                for g in range(2):
                    G.memset(zh[:, HALF[g]], 0.0).then_inc(zh_ready[g], 1)
                pool.wait_ge(zh_ready[0], 1)
                pool.wait_ge(zh_ready[1], 1)
                G.memset(zh[:, :], 0.0).then_inc(h_new, 1)

                def step(n1, n2, s, t):
                    for g in range(2):
                        z_parts = mv[:, s % 2, 2 * g:2 * g + 2]
                        pool.wait_ge(rz_act[g], n1)
                        if g == 0:
                            pool.wait_ge(h_new, n1)
                        G.tensor_tensor(z_parts[:, :, 0], halves(rz[:, 1, HALF[g]]), halves(H16[:, HALF[g]]),
                                        ALU.mult).then_inc(zh_hi[g], 1)
                        G.tensor_tensor(zh[:, HALF[g]], rz[:, 1, HALF[g]], H16[:, HALF[g]],
                                        ALU.mult).then_inc(zh_f32[g], 1)
                        pool.wait_ge(zh_hi[g], n1)
                        pool.wait_ge(zh_f32[g], n1)
                        G.tensor_tensor(z_parts[:, :, 1], halves(zh[:, HALF[g]]), z_parts[:, :, 0],
                                        ALU.subtract).then_inc(zh_ready[g], 1)
                    pool.wait_ge(u_f32[0], n1)
                    pool.wait_ge(u_f32[1], n1)
                    G.tensor_tensor(H16[:, :], uf[:, :], zh[:, :], ALU.add).then_inc(h_new, 1)
                    pool.wait_ge(h_new, n2)
                    G.tensor_copy(hx[:, t], H16[:, :]).then_inc(h_kept, 1)

                with pool.Fori(0, NCH) as c:
                    with pool.Fori(0, TC // UN) as i:
                        n = [pool.snap(c * TC + i * UN + s + 1) for s in range(UN + 1)]
                        for s in range(UN):
                            step(n[s], n[s + 1], s, c * TC + i * UN + s)

        m = Mem(arena, base)
        wgus = m.take([2, FM, 2, KT, P], F16)
        wdns = m.take([2, FM, D], F16)
        gul = m.take([3, 2 * KT * P], F32)
        dnl = m.take([3, D], F32)
        hc = m.take([2, KT, CH], F16)
        hid = m.take([2, FM, CH], F16)
        xr = m.take([KT, CH], F32)
        sg = m.take([2, CH], F32)
        ga = m.take([CH], F32)
        gb = m.take([CH], F32)
        hf = m.take([2, CH], F32)
        wT = m.take([CH], F16)
        sc = m.take([4, E], F32)
        mx = m.take([4, 8], F32)
        ix = m.take([4, 8], F32).bitcast(U32)
        ixf = m.take([4, 2], F32)
        dif = m.take([4, 2], F32)
        pr = m.take([4, 2], F32)
        w1st = m.take([4, E], F32)
        w2nd = m.take([4, E], F32)
        wgt = m.take([4, E], F32)
        wp = m.take([4, 2 * E], F16)

        raw2_in = [sem(f"raw2_in{i}") for i in range(3)]
        xr_in = sem("xr_in")
        wr_done, wT_zero = sem("wr_done"), sem("wT_zero")
        gu_hi, gu_lo = sem("gu_hi"), sem("gu_lo")
        hc_hi, hc_lo = sem("hc_hi"), sem("hc_lo")
        score_mm, scores = sem("score_mm"), sem("scores")
        top8, top_ix, top_dif, probs = sem("top8"), sem("top_ix"), sem("top_dif"), sem("probs")
        ixf_done = sem("ixf_done")
        wts_a, wts, wp_hi, wp_done = sem("wts_a"), sem("wts"), sem("wp_hi"), sem("wp_done")
        wT_mm, wT_done = sem("wT_mm"), sem("wT_done")
        gate_mm, sig_done, ga_done, gb_done = sem("gate_mm"), sem("sig_done"), sem("ga_done"), sem("gb_done")
        wb_mm, hf_done, hid_hi, hid_lo = sem("wb_mm"), sem("hf_done"), sem("hid_hi"), sem("hid_lo")
        down_mm, down_out = sem("down_mm"), sem("down_out")

        def chunk_of_states(c, k):
            return hx[:, bass.ts(c, TC), k * B:(k + 1) * B]

        def tb(a):
            return a.rearrange("p (t b) -> p t b", b=B)

        with nc.Block() as block:

            @block.sync
            def _(sp):
                sp.dma_start(xr[:, :, :], xT[:, :, 0:CH]).then_inc(xr_in, 16)
                for mt in range(FM):
                    if mt >= 3:
                        sp.wait_ge(gu_lo, 2 * (mt - 2))
                    sp.dma_start(gul[:, mt % 3, :], wgu[:, mt].rearrange("p a k f -> p (a k f)")).then_inc(raw2_in[mt % 3], 16)
                    sp.dma_start(dnl[:, mt % 3, :], wdn[:, mt, :]).then_inc(raw2_in[mt % 3], 16)
                with sp.Fori(1, NCH) as c:
                    sp.wait_ge(down_out, c * KT)
                    sp.dma_start(xr[:, :, :], xT[:, :, bass.ts(c, CH)]).then_inc(xr_in, 16)

            @block.tensor
            def _(pe):
                pe.wait_ge(wr_done, 2)
                pe.wait_ge(wT_zero, 1)

                def chunk(c, first):
                    pe.wait_ge(hc_lo, c * KT + KT)
                    SC = bank[7][:, 0:64].rearrange("p (s e) -> p s e", s=4)
                    for st in range(4):
                        n = 0
                        for part in range(2):
                            for k in range(KT):
                                mm = nc.tensor.matmul(SC[:, st, :], hc[:, part, k, st * P:(st + 1) * P],
                                                      wrs[:, k].rearrange("p a e -> p (a e)"),
                                                      start=(n == 0), stop=(n == 2 * KT - 1))
                                n += 1
                    mm.then_inc(score_mm, 1)
                    for mt in range(FM):
                        if first:
                            pe.wait_ge(gu_lo, 2 * mt + 2)
                        if mt < 2:
                            pe.wait_ge(gb_done, c * FM + mt)
                        else:
                            pe.wait_ge(gb_done, c * FM + (mt - 1))
                        for a in range(2):
                            n = 0
                            for w_, h_ in ((0, 0), (0, 1), (1, 0)):
                                for k in range(KT):
                                    mm = nc.tensor.matmul(bank[2 * a + mt % 2][:, :], wgus[:, w_, mt, a, k, :],
                                                          hc[:, h_, k, :], start=(n == 0), stop=(n == 3 * KT - 1))
                                    n += 1
                        mm.then_inc(gate_mm, 1)
                        if mt == 0:
                            pe.wait_ge(wp_done, c + 1)
                            WT = bank[7].bitcast(F16)[0:2 * E, 0:CH]
                            for st in range(4):
                                mm = nc.tensor.transpose(WT[:, st * P:(st + 1) * P], wp[:, st, :], id1[:, :])
                            mm.then_inc(wT_mm, 1)
                            pe.wait_ge(wT_done, c + 1)
                        pe.wait_ge(hf_done, c * FM + mt)
                        nc.tensor.matmul(bank[6][:, :], sel[:, mt, :], wT[:, :], start=True, stop=True)\
                            .then_inc(wb_mm, 1)
                    pe.wait_ge(hid_lo, c * FM + FM)
                    for j in range(KT):
                        if j < 2:
                            pe.wait_ge(down_out, c * KT + j)
                        else:
                            pe.wait_ge(down_out, c * KT + (j - 1))
                        n = 0
                        for mt in range(FM):
                            for w_, h_ in ((0, 0), (0, 1), (1, 0)):
                                mm = nc.tensor.matmul(bank[4 + j % 2][:, :], wdns[:, w_, mt, j * P:(j + 1) * P],
                                                      hid[:, h_, mt, :], start=(n == 0), stop=(n == 3 * FM - 1))
                                n += 1
                        mm.then_inc(down_mm, 1)

                chunk(0, True)
                with pe.Fori(1, NCH) as c:
                    chunk(c, False)

            @block.scalar
            def _(act):
                A = nc.scalar

                def split_states(c):
                    for k in range(KT):
                        A.activation(tb(hc[:, 0, k, :]), chunk_of_states(c, k), ACT.Copy).then_inc(hc_hi, 1)

                def split_weights(mt):
                    act.wait_ge(raw2_in[mt % 3], 32 * (mt // 3 + 1))
                    A.activation(wgus[:, 0, mt].rearrange("p a k f -> p (a k f)"), gul[:, mt % 3, :], ACT.Copy,
                                 scale=SW).then_inc(gu_hi, 1)
                    A.activation(wdns[:, 0, mt, :], dnl[:, mt % 3, :], ACT.Copy, scale=SW).then_inc(gu_hi, 1)

                def chunk(c, first, last):
                    act.wait_ge(top_dif, 2 * c + 2)
                    A.activation(pr[:, :, :], dif[:, :, :], ACT.Sigmoid, scale=1 / SWX).then_inc(probs, 1)
                    for mt in range(FM + 1):
                        if first and mt + 2 < FM:
                            split_weights(mt + 2)
                        if mt < FM:
                            act.wait_ge(gate_mm, c * FM + mt + 1)
                            A.activation(sg[:, mt % 2, :], bank[mt % 2][:, :], ACT.Sigmoid, scale=1 / SWX)\
                                .then_inc(sig_done, 1)
                        if mt == 0:
                            act.wait_ge(wT_mm, c + 1)
                            A.activation(wT[0:2 * E, :], bank[7].bitcast(F16)[0:2 * E, 0:CH], ACT.Copy)\
                                .then_inc(wT_done, 1)
                        if mt >= 1:
                            act.wait_ge(hf_done, c * FM + mt)
                            if mt == 1:
                                act.wait_ge(down_mm, c * KT)
                            A.activation(hid[:, 0, mt - 1, :], hf[:, (mt - 1) % 2, :], ACT.Copy).then_inc(hid_hi, 1)
                    if not last:
                        split_states(c + 1)

                A.activation(wrs[:, :, 0, :], wrf[:, :, :], ACT.Copy, scale=SW).then_inc(wr_done, 1)
                split_states(0)
                split_weights(0)
                split_weights(1)
                chunk(0, True, False)
                with act.Fori(1, NCH - 1) as c:
                    chunk(c, False, False)
                chunk(NCH - 1, False, True)

            @block.vector
            def _(dve):
                V = nc.vector

                def split_states(c):
                    for k in range(KT):
                        dve.wait_ge(hc_hi, c * KT + k + 1)
                        V.tensor_tensor(tb(hc[:, 1, k, :]), chunk_of_states(c, k), tb(hc[:, 0, k, :]),
                                        ALU.subtract).then_inc(hc_lo, 1)

                def split_weights(mt):
                    dve.wait_ge(gu_hi, 2 * mt + 1)
                    V.scalar_tensor_tensor(wgus[:, 1, mt].rearrange("p a k f -> p (a k f)"), gul[:, mt % 3, :], SW,
                                           wgus[:, 0, mt].rearrange("p a k f -> p (a k f)"), ALU.mult,
                                           ALU.subtract).then_inc(gu_lo, 1)
                    dve.wait_ge(gu_hi, 2 * mt + 2)
                    V.scalar_tensor_tensor(wdns[:, 1, mt, :], dnl[:, mt % 3, :], SW, wdns[:, 0, mt, :], ALU.mult,
                                           ALU.subtract).then_inc(gu_lo, 1)

                def route(c):
                    dve.wait_ge(score_mm, c + 1)
                    V.tensor_reduce(sc[:, :, :], bank[7][:, 0:64].rearrange("p (s a e) -> p s e a", s=4, a=2), AX.X,
                                    ALU.add).then_inc(scores, 1)
                    dve.wait_ge(hc_lo, KT)
                    dve.wait_ge(scores, c + 1)
                    for st in range(4):
                        V.max(mx[:, st, :], sc[:, st, :]).then_inc(top8, 1)
                    dve.wait_ge(top8, 4 * c + 4)
                    V.tensor_tensor(dif[:, :, 0], mx[:, :, 0], mx[:, :, 1], ALU.subtract).then_inc(top_dif, 1)
                    V.tensor_tensor(dif[:, :, 1], mx[:, :, 1], mx[:, :, 0], ALU.subtract).then_inc(top_dif, 1)
                    for st in range(4):
                        V.max_index(ix[:, st, :], mx[:, st, :], sc[:, st, :]).then_inc(top_ix, 1)
                    dve.wait_ge(top_ix, 4 * c + 4)
                    V.tensor_copy(ixf[:, :, :], ix[:, :, 0:2]).then_inc(ixf_done, 1)
                    dve.wait_ge(ixf_done, c + 1)
                    dve.wait_ge(probs, c + 1)
                    for st in range(4):
                        V.tensor_scalar(w1st[:, st, :], iota, ixf[:, st, 0:1], pr[:, st, 0:1], ALU.is_equal,
                                        ALU.mult).then_inc(wts_a, 1)
                        V.tensor_scalar(w2nd[:, st, :], iota, ixf[:, st, 1:2], pr[:, st, 1:2], ALU.is_equal,
                                        ALU.mult).then_inc(wts_a, 1)
                    dve.wait_ge(wts_a, 8 * c + 8)
                    V.tensor_tensor(wgt[:, :, :], w1st[:, :, :], w2nd[:, :, :], ALU.add).then_inc(wts, 1)
                    dve.wait_ge(wts, c + 1)
                    V.tensor_copy(wp[:, :, 0:E], wgt[:, :, :]).then_inc(wp_hi, 1)
                    dve.wait_ge(wp_hi, c + 1)
                    V.tensor_tensor(wp[:, :, E:2 * E], wgt[:, :, :], wp[:, :, 0:E], ALU.subtract).then_inc(wp_done, 1)

                def down(c, j):
                    dve.wait_ge(down_mm, c * KT + j + 1)
                    V.scalar_tensor_tensor(chunk_of_states(c, j), tb(bank[4 + j % 2][:, :]), 1 / SWX,
                                           tb(xr[:, j, :]), ALU.mult, ALU.add).then_inc(down_out, 1)

                def chunk(c, first, last):
                    route(c)
                    for mt in range(FM + 1):
                        if first and mt + 2 < FM:
                            split_weights(mt + 2)
                        if mt < FM:
                            dve.wait_ge(sig_done, c * FM + mt + 1)
                            V.scalar_tensor_tensor(ga[:, :], bank[mt % 2][:, :], 1 / SWX, sg[:, mt % 2, :], ALU.mult,
                                                   ALU.mult).then_inc(ga_done, 1)
                            dve.wait_ge(ga_done, c * FM + mt + 1)
                            V.scalar_tensor_tensor(gb[:, :], bank[2 + mt % 2][:, :], 1 / SW, ga[:, :], ALU.mult,
                                                   ALU.mult).then_inc(gb_done, 1)
                            dve.wait_ge(gb_done, c * FM + mt + 1)
                            dve.wait_ge(wb_mm, c * FM + mt + 1)
                            V.tensor_tensor(hf[:, mt % 2, :], bank[6][:, :], gb[:, :], ALU.mult).then_inc(hf_done, 1)
                        if mt >= 1:
                            dve.wait_ge(hid_hi, c * FM + mt)
                            V.tensor_tensor(hid[:, 1, mt - 1, :], hf[:, (mt - 1) % 2, :], hid[:, 0, mt - 1, :],
                                            ALU.subtract).then_inc(hid_lo, 1)
                    dve.wait_ge(xr_in, 16 * c + 16)
                    for j in range(KT):
                        if j == KT - 1 and not last:
                            split_states(c + 1)
                        down(c, j)

                V.memset(wT[:, :], 0.0).then_inc(wT_zero, 1)
                dve.wait_ge(wr_done, 1)
                V.scalar_tensor_tensor(wrs[:, :, 1, :], wrf[:, :, :], SW, wrs[:, :, 0, :], ALU.mult,
                                       ALU.subtract).then_inc(wr_done, 1)
                split_states(0)
                split_weights(0)
                split_weights(1)
                chunk(0, True, False)
                with dve.Fori(1, NCH - 1) as c:
                    chunk(c, False, False)
                chunk(NCH - 1, False, True)


        S = T
        m = Mem(arena, base)
        o2p = m.take([2, KT, NTOK], F16)
        wqs = m.take([2, KT, G3], F16)
        wos = m.take([2, KT, D], F16)
        rinv = m.take([NTOK], F32)
        start_c = m.at
        wel = m.take([KT, 2 * D], F32)
        wql = m.take([KT, G3], F32)
        wol = m.take([KT, D], F32)
        sqx = m.take([2, CH], F32)
        rms = m.take([2, CH], F32)
        ss = m.take([2 * KT, B], F32)
        g16 = m.take([KT], F32)
        gam = m.take([3], F32)
        gam2 = m.take([3], F32)

        we_in, wo_in, wo_unit = sem("we_in"), sem("wo_in"), sem("wo_unit")
        wq_in = [sem(f"wq_in{k}") for k in range(KT)]
        sqx_done, ssx_mm, rms_done, rinv_done = sem("sqx_done"), sem("ssx_mm"), sem("rms_done"), sem("rinv_done")
        wq_hi, wq_lo = sem("wq_hi"), sem("wq_lo")
        ss_mm, gam_mm = sem("ss_mm"), sem("gam_mm")
        prep = sem("prep")

        with nc.Block() as block:

            @block.sync
            def _(sp):
                sp.dma_start(wel[:, :, :], wemb).then_inc(we_in, 16)
                for k in range(KT):
                    sp.dma_start(wql[:, k, :], wqkv[:, k, :]).then_inc(wq_in[k], 16)
                sp.dma_start(wol[:, :, :], wout).then_inc(wo_in, 16)

            @block.tensor
            def _(pe):
                for c in range(NCH):
                    if c >= 2:
                        pe.wait_ge(rms_done, c - 1)
                    for k in range(KT):
                        pe.wait_ge(sqx_done, c * KT + k + 1)
                        nc.tensor.matmul(bank[c % 2][:, :], ones[:, :], sqx[:, k % 2, :], start=(k == 0),
                                         stop=(k == KT - 1)).then_inc(ssx_mm, 1)
                nc.tensor.matmul(bank[3][:, 0:3 * NCH], ones[:, :], gsum.rearrange("p c w -> p (c w)"), start=True,
                                 stop=True).then_inc(gam_mm, 1)
                pe.wait_ge(we_in, 16)
                SS = bank[2][:, 0:2 * KT * B].rearrange("p (m b) -> p m b", b=B)
                for mt in range(2 * KT):
                    for k in range(KT):
                        mm = nc.tensor.matmul(SS[:, mt, :], wel[:, k, mt * P:(mt + 1) * P], cond[:, k, :],
                                              start=(k == 0), stop=(k == KT - 1))
                mm.then_inc(ss_mm, 1)

            @block.scalar
            def _(act):
                A = nc.scalar
                for c in range(NCH):
                    for k in range(KT):
                        n = c * KT + k
                        if n >= 2:
                            act.wait_ge(ssx_mm, n - 1)
                        A.activation(tb(sqx[:, k % 2, :]), chunk_of_states(c, k), ACT.Square).then_inc(sqx_done, 1)
                    act.wait_ge(ssx_mm, c * KT + KT)
                    if c >= 2:
                        act.wait_ge(rinv_done, c - 1)
                    A.activation(rms[:, c % 2, :], bank[c % 2][:, :], ACT.Sqrt, scale=1 / D,
                                 bias=epsb[:, :]).then_inc(rms_done, 1)
                for k in range(KT):
                    act.wait_ge(wq_in[k], 16)
                    A.activation(wqs[:, 0, k, :], wql[:, k, :], ACT.Copy, scale=SW).then_inc(wq_hi, 1)
                act.wait_ge(wo_unit, KT)
                A.activation(wos[:, 0], wol[:, :, :], ACT.Copy, scale=SW).then_inc(wq_hi, 1)

            @block.vector
            def _(dve):
                V = nc.vector
                for c in range(NCH):
                    dve.wait_ge(rms_done, c + 1)
                    V.reciprocal(rinv[:, c * CH:(c + 1) * CH], rms[:, c % 2, :]).then_inc(rinv_done, 1)
                dve.wait_ge(wo_in, 16)
                for k in range(KT):
                    V.tensor_tensor(wol[:, k, k * P:(k + 1) * P], wol[:, k, k * P:(k + 1) * P], ident,
                                    ALU.add).then_inc(wo_unit, 1)
                dve.wait_ge(gam_mm, 1)
                V.tensor_reduce(gam[:, :], bank[3][:, 0:3 * NCH].rearrange("p (c w) -> p w c", w=3), AX.X,
                                ALU.add).then_inc(prep, 1)
                dve.wait_ge(prep, 1)
                V.tensor_scalar(gam2[:, :], gam[:, :], 1 / WN, 1e-8, ALU.mult, ALU.add).then_inc(prep, 1)
                dve.wait_ge(prep, 2)
                V.tensor_scalar(thr[:, 0, :], gam2[:, :], 0.5, None, ALU.mult)
                V.tensor_scalar(thr[:, 1, :], gam2[:, :], -0.5, None, ALU.mult)
                V.tensor_scalar(g16[:, :], av[:, 2 * KT:3 * KT], SX, None, ALU.mult)
                V.tensor_tensor(gg[:, :], gq[:, 0, :], gq[:, 1, :], ALU.mult).then_inc(prep, 1)
                dve.wait_ge(ss_mm, 1)
                V.tensor_tensor(ss[:, :, :], bank[2][:, 0:2 * KT * B].rearrange("p (m b) -> p m b", b=B),
                                av[:, 0:2 * KT].unsqueeze(2).broadcast_to((P, 2 * KT, B)), ALU.add).then_inc(prep, 1)
                dve.wait_ge(prep, 4)
                V.scalar_tensor_tensor(ada[:, 0], ss[:, 0:KT, :], 1.0,
                                       g16[:, :].unsqueeze(2).broadcast_to((P, KT, B)), ALU.add, ALU.mult)
                V.tensor_scalar(ada[:, 1], ss[:, KT:2 * KT, :], SX, None, ALU.mult).then_inc(prep, 1)
                for k in range(KT):
                    dve.wait_ge(wq_hi, k + 1)
                    V.scalar_tensor_tensor(wqs[:, 1, k, :], wql[:, k, :], SW, wqs[:, 0, k, :], ALU.mult,
                                           ALU.subtract).then_inc(wq_lo, 1)
                dve.wait_ge(wq_hi, KT + 1)
                V.scalar_tensor_tensor(wos[:, 1], wol[:, :, :], SW, wos[:, 0], ALU.mult,
                                       ALU.subtract).then_inc(wq_lo, 1)

        m = Mem(arena, start_c)
        xnf = m.take([KT, S], F32)
        xn = m.take([2, KT, S], F16)
        qkr = m.take([4, D], F32)
        sqk = m.take([2, D], F32)
        ssk = m.take([4, H], F32)
        rmsk = m.take([4, H], F32)
        rk = m.take([4, H], F32)
        stk = m.take([4, H, 3 * DH], F16)
        qs = m.take([H, S], F16)
        ks = m.take([H, S], F16)
        vr = m.take([2, D], F32)
        vh = m.take([2, H, DH + 1], F16)
        vl = m.take([2, H, DH + 1], F16)
        mxs = m.take([2, H], F32)
        mT = m.take([P], F16)
        pf = m.take([3, 2 * S], F32)
        ph = m.take([3, 2, S], F16)
        pl = m.take([3, 2, S], F16)
        rc = m.take([2, 4], F32)
        of = m.take([2, H, DH], F32)
        oTp = m.take([2, KT, S], F16)

        KC = SX * SX
        SPLIT = (1, 0, 3, 2)
        PROJECT_AT = {0: 0, 1: 1, 2: 2, 3: 3, 5: 4, 7: 5}
        ROOT_AT = 4
        NORM_AT = {4: (0,), 5: (1, 2, 3)}
        SPLIT_AT = {5: (0, 1), 6: (2, 3)}
        LOW_AT = {6: (0, 1), 7: (2, 3)}
        STACK_AT = {8: (0,), 9: (1,), 10: (2,), 13: (3,)}
        MAX_AT = {9: (0, 1), 10: (2, 3), 11: (4, 5, 6), 12: (7, 8), 13: (9, 10), 14: (11, 12), 15: (13, 14)}

        vzero = sem("vzero")
        xnt_done, xnf_done, xn_hi, xn_lo = sem("xnt_done"), sem("xnf_done"), sem("xn_hi"), sem("xn_lo")
        qkv_mm, qkv_out, sqk_done, ssk_done = sem("qkv_mm"), sem("qkv_out"), sem("sqk_done"), sem("ssk_done")
        rmsk_done, rk_done, qk_unit, q_gain = sem("rmsk_done"), sem("rk_done"), sem("qk_unit"), sem("q_gain")
        qk_hi, qk_lo = sem("qk_hi"), sem("qk_lo")
        qs_mm, ks_mm, qs_done, ks_done = sem("qs_mm"), sem("ks_mm"), sem("qs_done"), sem("ks_done")
        s_mm, max_done, mT_mm, mT_done, mrow_in = (sem("s_mm"), sem("max_done"), sem("mT_mm"), sem("mT_done"),
                                                   sem("mrow_in"))
        st_mm, exp_done, ph_done, pl_done, av_head = (sem("st_mm"), sem("exp_done"), sem("ph_done"), sem("pl_done"),
                                                      sem("av_head"))
        rc_done, o_done = sem("rc_done"), sem("o_done")
        vh_done, v_done = sem("vh_done"), sem("v_done")
        oT_mm, oTh_done, oTl_done, wo_mm, o2_hi, o2_lo = (sem("oT_mm"), sem("oTh_done"), sem("oTl_done"), sem("wo_mm"),
                                                          sem("o2_hi"), sem("o2_lo"))

        def heads_of(a):
            return a.rearrange("p (h d) -> p h d", h=H)

        def O_bank(q4):
            return bank[q4 % 2][:, 0:2 * 4 * (DH + 1)].rearrange("p (q h d) -> p q h d", q=2, h=4)

        with nc.Block() as block:

            @block.sync
            def _(sp):
                def load_max(b):
                    sp.wait_ge(mT_done, b + 1)
                    for qt in range(2):
                        sp.dma_start(qs[96:97, :, qt * P:(qt + 1) * P], mT[16 * qt:16 * qt + 16, :])\
                            .then_inc(mrow_in, 16)

                load_max(0)
                with sp.Fori(0, B - 1) as b:
                    load_max(b + 1)

            @block.tensor
            def _(pe):
                def project(b, i, first=False):
                    if i == 0:
                        pe.wait_ge(xn_lo, b + 1)
                    if i < 2 and not first:
                        pe.wait_ge(o2_lo, 2 * b + i - 1)
                    elif i >= 2:
                        pe.wait_ge(qkv_out, 6 * b + i - 1)
                    half = i // 2 if i < 4 else i - 4
                    col = (i % 2 if i < 4 else 2) * D
                    n = 0
                    for w_, x_ in ((0, 0), (0, 1), (1, 0)):
                        for k in range(KT):
                            mm = nc.tensor.matmul(bank[5 + i % 2][:, :], xn[:, x_, k, half * P:(half + 1) * P],
                                                  wqs[:, w_, k, col:col + D], start=(n == 0), stop=(n == 3 * KT - 1))
                            n += 1
                    mm.then_inc(qkv_mm, 1)

                def stack(b, g):
                    for a, done, mms in ((0, qs_done, qs_mm), (1, ks_done, ks_mm)):
                        if g == 0:
                            pe.wait_ge(qk_lo, 4 * b + 4)
                            pe.wait_ge(qkv_out, 6 * b + 5 + a)
                        else:
                            pe.wait_ge(done, 4 * b + g)
                        T16 = bank[5 + a].bitcast(F16).rearrange("p (h s) -> p h s", h=4)
                        for h in range(4):
                            for half in range(2):
                                mm = nc.tensor.transpose(T16[0:96, h, half * P:(half + 1) * P],
                                                         stk[:, 2 * half + a, 4 * g + h, :], id1[:, :])
                        mm.then_inc(mms, 1)

                def scores(b, h, first=False):
                    if h % 4 == 0:
                        pe.wait_ge(qs_done, 4 * b + h // 4 + 1)
                        pe.wait_ge(ks_done, 4 * b + h // 4 + 1)
                    if h >= 2:
                        pe.wait_ge(max_done, H * b + h - 1)
                    elif h == 1 and not first:
                        pe.wait_ge(mT_done, b)
                    for qt in range(2):
                        mm = nc.tensor.matmul(bank[4 + 3 * (h % 2)][:, qt * S:(qt + 1) * S],
                                              qs[0:96, h, qt * P:(qt + 1) * P], ks[0:96, h, :], start=True, stop=True)
                    mm.then_inc(s_mm, 1)

                def turn_max(b):
                    pe.wait_ge(max_done, H * b + H)
                    nc.tensor.transpose(bank[7][0:32, 0:P], mxs.rearrange("p q h -> p (q h)"), ident)\
                        .then_inc(mT_mm, 1)

                def scores_t(b, h, first=False):
                    if h == 0:
                        pe.wait_ge(mrow_in, 32 * (b + 1))
                    if h >= 2:
                        pe.wait_ge(exp_done, H * b + h - 1)
                    elif not first:
                        pe.wait_ge(exp_done, H * b)
                    for kt in range(2):
                        mm = nc.tensor.matmul(bank[2 + h % 2][:, kt * S:(kt + 1) * S], ks[0:97, h, kt * P:(kt + 1) * P],
                                              qs[0:97, h, :], start=True, stop=True)
                    mm.then_inc(st_mm, 1)

                def values(b, h):
                    if h == 0:
                        pe.wait_ge(v_done, 2 * b + 2)
                    if h % 4 == 0:
                        pe.wait_ge(oTl_done, 4 * b + h // 4 + 1)
                    pe.wait_ge(pl_done, H * b + h + 1)
                    for qt in range(2):
                        n = 0
                        for kt in range(2):
                            for p_, v_ in ((ph, vh), (ph, vl), (pl, vh)):
                                mm = nc.tensor.matmul(O_bank(h // 4)[:, qt, h % 4, :],
                                                      p_[:, h % 3, kt, qt * P:(qt + 1) * P], v_[:, kt, h, :],
                                                      start=(n == 0), stop=(n == 5))
                                n += 1
                    mm.then_inc(av_head, 1)

                def turn_out(b, q4):
                    pe.wait_ge(o_done, 4 * b + q4 + 1)
                    for qt in range(2):
                        mm = nc.tensor.transpose(bank[q4 % 2][:, qt * P:(qt + 1) * P],
                                                 of[:, qt, 4 * q4:4 * q4 + 4, :].rearrange("p h d -> p (h d)"), ident)
                    mm.then_inc(oT_mm, 1)

                def project_out(b, jp, last):
                    if jp == 0:
                        pe.wait_ge(oTl_done, 4 * b + 6)
                    pe.wait_ge((qs_done, ks_done)[jp], 4 * b + (4 if last else 8))
                    for a in range(2):
                        j = 2 * jp + a
                        n = 0
                        for w_, x_ in ((0, 0), (0, 1), (1, 0)):
                            for k in range(KT):
                                mm = nc.tensor.matmul(bank[5 + jp][:, a * S:(a + 1) * S],
                                                      wos[:, w_, k, j * P:(j + 1) * P], oTp[:, x_, k, :],
                                                      start=(n == 0), stop=(n == 3 * KT - 1))
                                n += 1
                    mm.then_inc(wo_mm, 1)

                def batch(b, last):
                    for h in range(H):
                        if h + 2 < H:
                            scores_t(b, h + 2)
                        if h % 4 == 1 and h > 4:
                            turn_out(b, h // 4 - 1)
                        if not last:
                            if h in PROJECT_AT:
                                project(b + 1, PROJECT_AT[h])
                            for g in STACK_AT.get(h, ()):
                                stack(b + 1, g)
                            for i in MAX_AT.get(h, ()):
                                scores(b + 1, i)
                        values(b, h)
                    if not last:
                        scores(b + 1, 15)
                    turn_out(b, 3)
                    if not last:
                        turn_max(b + 1)
                    project_out(b, 0, last)
                    if not last:
                        scores_t(b + 1, 0)
                        scores_t(b + 1, 1)
                    project_out(b, 1, last)

                for i in range(6):
                    project(0, i, True)
                for g in range(4):
                    stack(0, g)
                pe.wait_ge(vzero, 1)
                for h in range(H):
                    scores(0, h, True)
                pe.wait_ge(vzero, 4)
                turn_max(0)
                scores_t(0, 0, True)
                scores_t(0, 1, True)
                with pe.Fori(0, B - 1) as b:
                    batch(b, False)
                batch(B - 1, True)

            @block.scalar
            def _(act):
                A = nc.scalar

                def norm_x(b):
                    act.wait_ge(xnt_done, b + 1)
                    for k in range(KT):
                        A.activation(xnf[:, k, :], xnf[:, k, :], ACT.Identity, scale=ada[:, 0, k, bass.ds(b, 1)],
                                     bias=ada[:, 1, k, bass.ds(b, 1)]).then_inc(xnf_done, 1)
                    act.wait_ge(xnf_done, KT * b + KT)
                    A.activation(xn[:, 0], xnf[:, :, :], ACT.Copy).then_inc(xn_hi, 1)

                def take_out(b, i):
                    act.wait_ge(qkv_mm, 6 * b + i + 1)
                    A.activation(qkr[:, i, :] if i < 4 else vr[:, i - 4, :], bank[5 + i % 2][:, :], ACT.Copy,
                                 scale=1 / SWX if i < 4 else 1 / SW).then_inc(qkv_out, 1)

                def root(b):
                    act.wait_ge(ssk_done, 4 * b + 4)
                    A.activation(rmsk[:, :, :], ssk[:, :, :], ACT.Sqrt, scale=1 / DH, bias=epsb[:, :])\
                        .then_inc(rmsk_done, 1)

                def high_qk(b, n):
                    i = SPLIT[n]
                    if i % 2:
                        act.wait_ge(qk_unit, 4 * b + i + 1)
                    else:
                        act.wait_ge(q_gain, 2 * b + i // 2 + 1)
                    A.activation(stk[:, i, :, 0:DH], heads_of(qkr[:, i, :]), ACT.Copy).then_inc(qk_hi, 1)

                def stack(b, g):
                    act.wait_ge(ks_mm, 4 * b + g + 1)
                    A.activation(ks[0:96, 4 * g:4 * g + 4, :].rearrange("p h s -> p (h s)"),
                                 bank[6].bitcast(F16)[0:96, :], ACT.Copy).then_inc(ks_done, 1)

                def turn_max(b):
                    act.wait_ge(mT_mm, b + 1)
                    A.activation(mT[0:32, :], bank[7][0:32, 0:P], ACT.Copy, scale=-1 / KC).then_inc(mT_done, 1)

                def high_v(b):
                    for vt in range(2):
                        act.wait_ge(qkv_out, 6 * b + 5 + vt)
                        A.activation(vh[:, vt, :, 0:DH], heads_of(vr[:, vt, :]), ACT.Copy).then_inc(vh_done, 1)

                def softmax(b, h):
                    act.wait_ge(st_mm, H * b + h + 1)
                    if h >= 3:
                        act.wait_ge(pl_done, H * b + h - 2)
                    A.activation(pf[:, h % 3, :], bank[2 + h % 2][:, :], ACT.Exp, scale=DH ** -0.5 / KC)\
                        .then_inc(exp_done, 1)
                    act.wait_ge(exp_done, H * b + h + 1)
                    if h >= 3:
                        act.wait_ge(av_head, H * b + h - 2)
                    A.activation(ph[:, h % 3].rearrange("p k s -> p (k s)"), pf[:, h % 3, :], ACT.Copy)\
                        .then_inc(ph_done, 1)

                def high_out(b, q4):
                    act.wait_ge(oT_mm, 4 * b + q4 + 1)
                    A.activation(oTp[:, 0, q4, :], bank[q4 % 2][:, 0:S], ACT.Copy).then_inc(oTh_done, 1)

                def batch(b, last, more):
                    softmax(b, 0)
                    for h in range(H):
                        if h + 1 < H:
                            softmax(b, h + 1)
                        if h % 4 == 1 and h > 4:
                            high_out(b, h // 4 - 1)
                        if not last:
                            if h in PROJECT_AT:
                                take_out(b + 1, PROJECT_AT[h])
                            if h == ROOT_AT:
                                root(b + 1)
                            for n in SPLIT_AT.get(h, ()):
                                high_qk(b + 1, n)
                            for g in STACK_AT.get(h, ()):
                                stack(b + 1, g)
                    high_out(b, 3)
                    if not last:
                        turn_max(b + 1)
                        high_v(b + 1)
                    if more:
                        norm_x(b + 2)
                    for jp in range(2):
                        act.wait_ge(wo_mm, 2 * b + jp + 1)
                        A.activation(o2p[:, 0, 2 * jp:2 * jp + 2, bass.ts(b, S)],
                                     bank[5 + jp].rearrange("p (a s) -> p a s", a=2), ACT.Copy,
                                     scale=1 / SW).then_inc(o2_hi, 1)

                norm_x(0)
                for i in range(6):
                    take_out(0, i)
                root(0)
                for n in range(4):
                    high_qk(0, n)
                for g in range(4):
                    stack(0, g)
                turn_max(0)
                act.wait_ge(vzero, 4)
                high_v(0)
                norm_x(1)
                with act.Fori(0, B - 2) as b:
                    batch(b, False, True)
                batch(B - 2, False, False)
                batch(B - 1, True, False)

            @block.vector
            def _(dve):
                V = nc.vector

                def norm_x(b):
                    x1 = hx.rearrange("p t (k b) -> p b k t", k=KT)[:, b]
                    r = rinv.rearrange("p (t b) -> p b t", b=B)[:, b].unsqueeze(1).broadcast_to((P, KT, S))
                    V.tensor_tensor(xnf[:, :, :], x1, r, ALU.mult).then_inc(xnt_done, 1)
                    dve.wait_ge(xn_hi, b + 1)
                    V.tensor_tensor(xn[:, 1], xnf[:, :, :], xn[:, 0], ALU.subtract).then_inc(xn_lo, 1)

                def sum_squares(b, i):
                    dve.wait_ge(sqk_done, 4 * b + i + 1)
                    V.tensor_reduce(ssk[:, i, :], heads_of(sqk[:, i % 2, :]), AX.X, ALU.add).then_inc(ssk_done, 1)

                def invert(b):
                    dve.wait_ge(rmsk_done, b + 1)
                    V.reciprocal(rk[:, :, :], rmsk[:, :, :]).then_inc(rk_done, 1)
                    dve.wait_ge(rk_done, b + 1)

                def normalise_qk(b, i):
                    V.scalar_tensor_tensor(heads_of(qkr[:, i, :]), heads_of(qkr[:, i, :]), SX,
                                           rk[:, i, :].unsqueeze(2).broadcast_to((P, H, DH)), ALU.mult,
                                           ALU.mult).then_inc(qk_unit, 1)

                def low_qk(b, n):
                    i = SPLIT[n]
                    lo, again = (1, 2) if i % 2 == 0 else (2, 1)
                    dve.wait_ge(qk_hi, 4 * b + n + 1)
                    V.tensor_copy(stk[:, i, :, again * DH:(again + 1) * DH], stk[:, i, :, 0:DH])
                    V.tensor_tensor(stk[:, i, :, lo * DH:(lo + 1) * DH], heads_of(qkr[:, i, :]), stk[:, i, :, 0:DH],
                                    ALU.subtract).then_inc(qk_lo, 1)

                def stack(b, g):
                    dve.wait_ge(qs_mm, 4 * b + g + 1)
                    V.tensor_copy(qs[0:96, 4 * g:4 * g + 4, :].rearrange("p h s -> p (h s)"),
                                  bank[5].bitcast(F16)[0:96, :]).then_inc(qs_done, 1)

                def maximum(b, h):
                    dve.wait_ge(s_mm, H * b + h + 1)
                    V.tensor_reduce(mxs[:, :, h], bank[4 + 3 * (h % 2)].rearrange("p (q s) -> p q s", q=2), AX.X,
                                    ALU.max).then_inc(max_done, 1)

                def low_v(b):
                    for vt in range(2):
                        dve.wait_ge(vh_done, 2 * b + vt + 1)
                        V.tensor_tensor(vl[:, vt, :, 0:DH], heads_of(vr[:, vt, :]), vh[:, vt, :, 0:DH],
                                        ALU.subtract).then_inc(v_done, 1)

                def low_p(b, h):
                    dve.wait_ge(ph_done, H * b + h + 1)
                    V.tensor_tensor(pl[:, h % 3].rearrange("p k s -> p (k s)"), pf[:, h % 3, :],
                                    ph[:, h % 3].rearrange("p k s -> p (k s)"), ALU.subtract).then_inc(pl_done, 1)

                def normalise(b, q4):
                    O = O_bank(q4)
                    dve.wait_ge(av_head, H * b + 4 * q4 + 4)
                    V.reciprocal(rc[:, :, :], O[:, :, :, DH]).then_inc(rc_done, 1)
                    dve.wait_ge(rc_done, 4 * b + q4 + 1)
                    V.tensor_tensor(of[:, :, 4 * q4:4 * q4 + 4, :], O[:, :, :, 0:DH],
                                    rc[:, :, :].unsqueeze(3).broadcast_to((P, 2, 4, DH)), ALU.mult).then_inc(o_done, 1)

                def low_out(b, q4):
                    dve.wait_ge(oTh_done, 4 * b + q4 + 1)
                    V.tensor_tensor(oTp[:, 1, q4, :], bank[q4 % 2][:, 0:S], oTp[:, 0, q4, :],
                                    ALU.subtract).then_inc(oTl_done, 1)

                def batch(b, last, more):
                    low_p(b, 0)
                    for h in range(H):
                        if h + 1 < H:
                            low_p(b, h + 1)
                        if h % 4 == 0 and h > 0:
                            normalise(b, h // 4 - 1)
                        if h % 4 == 1 and h > 4:
                            low_out(b, h // 4 - 1)
                        if not last:
                            if 0 < h < 5:
                                sum_squares(b + 1, h - 1)
                            if h == ROOT_AT:
                                invert(b + 1)
                            for i in NORM_AT.get(h, ()):
                                normalise_qk(b + 1, i)
                            for n in LOW_AT.get(h, ()):
                                low_qk(b + 1, n)
                            for g in STACK_AT.get(h, ()):
                                stack(b + 1, g)
                            for i in MAX_AT.get(h, ()):
                                maximum(b + 1, i)
                    normalise(b, 3)
                    if not last:
                        maximum(b + 1, 15)
                    low_out(b, 3)
                    if not last:
                        low_v(b + 1)
                    if more:
                        norm_x(b + 2)
                    for jp in range(2):
                        dve.wait_ge(o2_hi, 2 * b + jp + 1)
                        V.scalar_tensor_tensor(o2p[:, 1, 2 * jp:2 * jp + 2, bass.ts(b, S)],
                                               bank[5 + jp].rearrange("p (a s) -> p a s", a=2), 1 / SW,
                                               o2p[:, 0, 2 * jp:2 * jp + 2, bass.ts(b, S)], ALU.mult,
                                               ALU.subtract).then_inc(o2_lo, 1)

                V.memset(ks[96:97, :, :], KC).then_inc(vzero, 1)
                V.memset(mxs[:, :, :], 0.0).then_inc(vzero, 1)
                V.memset(vh[:, :, :, DH:DH + 1], 1.0).then_inc(vzero, 1)
                V.memset(vl[:, :, :, DH:DH + 1], 0.0).then_inc(vzero, 1)
                V.memset(rk[:, :, :], 0.0).then_inc(o2_lo, 2)
                V.memset(rc[:, :, :], 0.0).then_inc(oTl_done, 2)
                norm_x(0)
                for i in range(4):
                    sum_squares(0, i)
                invert(0)
                for i in range(4):
                    normalise_qk(0, i)
                for n in range(4):
                    low_qk(0, n)
                for g in range(4):
                    stack(0, g)
                for h in range(H):
                    maximum(0, h)
                low_v(0)
                norm_x(1)
                with dve.Fori(0, B - 2) as b:
                    batch(b, False, True)
                batch(B - 2, False, False)
                batch(B - 1, True, False)

            @block.gpsimd
            def _(pool):
                G = nc.gpsimd

                def batch(b):
                    for i in range(4):
                        pool.wait_ge(qkv_out, 6 * b + i + 1)
                        if i >= 2:
                            pool.wait_ge(ssk_done, 4 * b + i - 1)
                        G.tensor_tensor(sqk[:, i % 2, :], qkr[:, i, :], qkr[:, i, :], ALU.mult).then_inc(sqk_done, 1)
                    for i in (0, 2):
                        pool.wait_ge(qk_unit, 4 * b + i + 1)
                        G.tensor_tensor(heads_of(qkr[:, i, :]), heads_of(qkr[:, i, :]),
                                        gg[:, :].unsqueeze(1).broadcast_to((P, H, DH)), ALU.mult).then_inc(q_gain, 1)

                batch(0)
                with pool.Fori(0, B - 1) as b:
                    batch(b + 1)

        m = Mem(arena, base)
        assert m.take([2, KT, NTOK], F16).shape == o2p.shape
        w12 = m.take([HM, 2, KT, P], F16)
        w3q = m.take([HM, D], F16)
        tl = m.take([3, 3 * D], F32)
        neg = m.take([2, 3 * D], F16)
        sgd = m.take([2, CH], F32)
        hdf = m.take([2, CH], F32)
        hdp = m.take([2, HM, CH], F16)
        yo = m.take([2, CH], F32)

        t_in = [sem(f"t_in{i}") for i in range(3)]
        neg_done, q_done = sem("neg_done"), sem("q_done")
        up_mm, sgd_done, hdf_done, hdp_hi, hdp_lo = (sem("up_mm"), sem("sgd_done"), sem("hdf_done"), sem("hdp_hi"),
                                                     sem("hdp_lo"))
        y_mm, y_done, y_out = sem("y_mm"), sem("y_done"), two("y_out")

        with nc.Block() as block:

            @block.sync
            def _(sp):
                for mt in range(HM):
                    if mt >= 3:
                        sp.wait_ge(q_done, 3 * (mt - 2))
                    for i, w in enumerate((w1T, w2T)):
                        sp.dma_start(tl[:, mt % 3, i * D:(i + 1) * D], w[:, mt].rearrange("p k h -> p (k h)"))\
                            .then_inc(t_in[mt % 3], 16)
                    sp.dma_start(tl[:, mt % 3, 2 * D:3 * D], w3T[:, mt, :]).then_inc(t_in[mt % 3], 16)
                with sp.Fori(0, NCH) as c:
                    for j in range(KT):
                        sp.wait_ge(y_done, c * KT + j + 1)
                        sp.dma_start(out[:, j, bass.ts(c, CH)], yo[:, j % 2, :]).then_inc(y_out[j % 2], 16)
                sp.wait_ge(y_out[0], 8 * KT * NCH)
                sp.wait_ge(y_out[1], 8 * KT * NCH)

            @block.gpsimd
            def _(pool):
                for mt in range(HM):
                    pool.wait_ge(t_in[mt % 3], 48 * (mt // 3 + 1))
                    if mt >= 2:
                        pool.wait_ge(q_done, 3 * (mt - 1))
                    for i in range(3):
                        nc.gpsimd.tensor_scalar(neg[:, mt % 2, i * D:(i + 1) * D], tl[:, mt % 3, i * D:(i + 1) * D],
                                                thr[:, 1, i:i + 1], None, ALU.is_lt).then_inc(neg_done, 1)

            @block.tensor
            def _(pe):
                def chunk(c, first):
                    for mt in range(HM):
                        if first:
                            pe.wait_ge(q_done, 3 * mt + 3)
                        if mt < 2:
                            pe.wait_ge(hdf_done, c * HM + mt)
                        else:
                            pe.wait_ge(hdf_done, c * HM + mt - 1)
                        for a in range(2):
                            n = 0
                            for part in range(2):
                                for k in range(KT):
                                    mm = nc.tensor.matmul(bank[2 * a + mt % 2][:, :], w12[:, mt, a, k, :],
                                                          o2p[:, part, k, bass.ts(c, CH)], start=(n == 0),
                                                          stop=(n == 2 * KT - 1))
                                    n += 1
                        mm.then_inc(up_mm, 1)
                    pe.wait_ge(hdp_lo, c * HM + HM)
                    for j in range(KT):
                        if j < 2:
                            pe.wait_ge(y_done, c * KT + j)
                        else:
                            pe.wait_ge(y_done, c * KT + j - 1)
                        n = 0
                        for mt in range(HM):
                            for part in range(2):
                                mm = nc.tensor.matmul(bank[4 + j % 2][:, :], w3q[:, mt, j * P:(j + 1) * P],
                                                      hdp[:, part, mt, :], start=(n == 0), stop=(n == 2 * HM - 1))
                                n += 1
                        mm.then_inc(y_mm, 1)

                chunk(0, True)
                with pe.Fori(1, NCH) as c:
                    chunk(c, False)

            @block.scalar
            def _(act):
                A = nc.scalar

                def chunk(c, first):
                    for mt in range(HM + 1):
                        if mt < HM:
                            act.wait_ge(up_mm, c * HM + mt + 1)
                            A.activation(sgd[:, mt % 2, :], bank[mt % 2][:, :], ACT.Sigmoid, scale=1 / SX)\
                                .then_inc(sgd_done, 1)
                        if mt > 0:
                            act.wait_ge(hdf_done, c * HM + mt)
                            if mt == 1 and not first:
                                act.wait_ge(y_mm, c * KT)
                            A.activation(hdp[:, 0, mt - 1, :], hdf[:, (mt - 1) % 2, :], ACT.Copy).then_inc(hdp_hi, 1)

                chunk(0, True)
                with act.Fori(1, NCH) as c:
                    chunk(c, False)

            @block.vector
            def _(dve):
                V = nc.vector

                def quantise(mt):
                    for i in range(3):
                        dve.wait_ge(neg_done, 3 * mt + i + 1)
                        dst = w12[:, mt, i].rearrange("p k h -> p (k h)") if i < 2 else w3q[:, mt, :]
                        V.scalar_tensor_tensor(dst, tl[:, mt % 3, i * D:(i + 1) * D], thr[:, 0, i:i + 1],
                                               neg[:, mt % 2, i * D:(i + 1) * D], ALU.is_gt,
                                               ALU.subtract).then_inc(q_done, 1)

                def chunk(c, first):
                    for mt in range(HM + 1):
                        if first and mt + 2 < HM:
                            quantise(mt + 2)
                        if mt < HM:
                            dve.wait_ge(hdp_lo, c * HM + (mt - 1 if mt >= 2 else 0))
                            dve.wait_ge(sgd_done, c * HM + mt + 1)
                            V.scalar_tensor_tensor(hdf[:, mt % 2, :], bank[2 + mt % 2][:, :], 1 / SX,
                                                   sgd[:, mt % 2, :], ALU.mult, ALU.mult).then_inc(hdf_done, 1)
                        if mt > 0:
                            dve.wait_ge(hdp_hi, c * HM + mt)
                            V.tensor_tensor(hdp[:, 1, mt - 1, :], hdf[:, (mt - 1) % 2, :], hdp[:, 0, mt - 1, :],
                                            ALU.subtract).then_inc(hdp_lo, 1)
                    for j in range(KT):
                        dve.wait_ge(y_mm, c * KT + j + 1)
                        if not first or j >= 2:
                            dve.wait_ge(y_out[j % 2], (c * 2 + j // 2) * 16)
                        x1 = hx.rearrange("p t (k b) -> p k b t", k=KT)[:, j, bass.ts(c, 2), :]
                        V.tensor_tensor(yo[:, j % 2, :].rearrange("p (b t) -> p b t", b=2),
                                        bank[4 + j % 2].rearrange("p (b t) -> p b t", b=2), x1,
                                        ALU.add).then_inc(y_done, 1)

                quantise(0)
                quantise(1)
                chunk(0, True)
                with dve.Fori(1, NCH) as c:
                    chunk(c, False)


NAMES = ["xT", "condT", "wih", "whh", "bias", "wr", "wgu", "wdn", "wemb", "avec", "gqk", "wqkv", "wout",
         "w1f", "w2f", "w3f", "w1T", "w2T", "w3T", "consts"]


def kernel(**inputs):
    import numpy as np
    import concourse.bacc as bacc
    from concourse.bass_utils import run_bass_kernel_spmd

    i = {k: np.asarray(v) for k, v in inputs.items()}

    def rows(w):
        return w.reshape(KT, P, -1).transpose(1, 0, 2)

    a = {}
    a["xT"] = rows(i["x"].transpose(2, 1, 0).reshape(D, NTOK))
    a["condT"] = rows(i["cond_2048"].T)
    a["wih"], a["whh"] = rows(i["L0_cond_W_ih"]), rows(i["L0_cond_W_hh"])
    a["bias"] = np.stack([i["L0_cond_b_ih"].reshape(GM, P).T, i["L0_cond_b_hh"].reshape(GM, P).T], 1)
    a["wr"] = rows(i["L0_ffn_w_gate_router"].T)
    gate = i["L0_ffn_w_gate_proj"].reshape(E * F, D).T.reshape(KT, P, FM, P)
    up = i["L0_ffn_w_up_proj"].reshape(E * F, D).T.reshape(KT, P, FM, P)
    a["wgu"] = np.stack([gate, up]).transpose(2, 3, 0, 1, 4)
    a["wdn"] = i["L0_ffn_w_down_proj"].transpose(0, 2, 1).reshape(FM, P, D).transpose(1, 0, 2)
    a["wemb"] = rows(i["L1_cond_W_emb"])
    a["avec"] = np.concatenate([i["L1_cond_b_emb"].reshape(2 * KT, P).T, i["L1_cond_g_norm"].reshape(KT, P).T], 1)
    a["gqk"] = np.tile(np.stack([i["L1_cond_g_q"], i["L1_cond_g_k"]]), (P, 1, 1))
    a["wqkv"], a["wout"] = rows(i["L1_cond_W_qkv"]), rows(i["L1_cond_W_out"])
    for n in "123":
        a[f"w{n}f"] = i[f"L1_ffn_w{n}"].reshape(P, -1)
    a["w1T"] = i["L1_ffn_w1"].T.reshape(KT, P, HM, P).transpose(1, 2, 0, 3)
    a["w2T"] = i["L1_ffn_w2"].T.reshape(KT, P, HM, P).transpose(1, 2, 0, 3)
    a["w3T"] = i["L1_ffn_w3"].T.reshape(HM, P, D).transpose(1, 0, 2)
    c = np.zeros((P, 264 + FM * P), np.float32)
    c[:, 0:128] = np.eye(P)
    c[:, 128:256] = np.kron(np.eye(P // DH), np.ones((DH, DH)))
    c[:, 256:264] = np.arange(E)
    for f in range(FM * P):
        c[f // F, 264 + f] = 1.0
        c[E + f // F, 264 + f] = 1.0
    a["consts"] = c

    nc = bacc.Bacc("TRN2", target_bir_lowering=False, num_devices=1)
    arrays, args = {}, []
    for name in NAMES:
        v = np.ascontiguousarray(a[name])
        arrays[f"in_{name}"] = v
        args.append(nc.dram_tensor(f"in_{name}", v.shape, mybir.dt.from_np(v.dtype), kind="ExternalInput").ap())
    y = nc.dram_tensor("out_y", (P, KT, NTOK), F32, kind="ExternalOutput").ap()
    mixed_net_kernel(nc, *args, y)
    r = run_bass_kernel_spmd(nc, [arrays], core_ids=[0])
    got = r.results[0]["out_y"]
    return np.ascontiguousarray(got.reshape(P, KT, B, T).transpose(2, 3, 1, 0).reshape(B, T, D))
```

```python
from contextlib import ExitStack

import concourse.bass as bass
from concourse import mybir

F32 = mybir.dt.float32
F16 = mybir.dt.float16
U32 = mybir.dt.uint32
ACT = mybir.ActivationFunctionType
ALU = mybir.AluOpType
AX = mybir.AxisListType

P = 128
D = 512
KT = D // P
T = 256
B = 8
NTOK = T * B
CH = 512
NCH = NTOK // CH
TC = CH // B
G3 = 3 * D
GM = G3 // P
E = 8
F = 192
FM = E * F // P
H = 16
DH = D // H
HF = 1408
HM = HF // P
WN = HF * D

SW = 64.0
SX = 16.0
SWX = SW * SX

UN = 16
ARENA = 200 * 1024


class Mem:

    def __init__(self, arena, start):
        self.arena, self.at = arena, start

    def take(self, shape, dt, parts=P):
        n = 1
        for s in shape:
            n *= s
        size = n * (2 if dt == F16 else 4)
        size = (size + 31) // 32 * 32
        a = self.arena[0:parts, self.at // 4:(self.at + size) // 4]
        self.at += size
        assert self.at <= ARENA, self.at
        a = a.bitcast(dt) if dt != F32 else a
        a = a[:, 0:n]
        if len(shape) > 1:
            names = "abcdef"[:len(shape)]
            a = a.rearrange("p (%s) -> p %s" % (" ".join(names), " ".join(names)),
                            **{c: s for c, s in zip(names, shape)})
        return a


def gru_order():
    RZ, N, ALL = (0, 1), (2,), (0, 1, 2)

    def block(ks, js, gates):
        return [(k, j, gates) for j in js for k in ks]

    return (block((0, 1), (0, 1), ALL) + block((0, 1), (2,), RZ) + block((2, 3), (0, 1), RZ)
            + block((2, 3), (0, 1), N) + block((0, 1), (3,), RZ) + block((2, 3), (2, 3), RZ)
            + block((0, 1, 2, 3), (2, 3), N))


def mixed_net_kernel(nc, xT, condT, wih, whh, bias, wr, wgu, wdn, wemb, avec, gqk, wqkv, wout,
                     w1f, w2f, w3f, w1T, w2T, w3T, consts, out):
    with ExitStack() as ctx:
        def sb(name, shape, dt):
            return ctx.enter_context(nc.sbuf_tensor(name, shape, dt))

        def sem(name):
            return ctx.enter_context(nc.semaphore(name))

        def two(name):
            return [sem(name + "_0"), sem(name + "_1")]

        bank = [ctx.enter_context(nc.psum_tensor(f"bank{i}", [P, 512], F32)) for i in range(8)]
        arena = sb("arena", [P, ARENA // 4], F32)

        cst = sb("cst", [P, P + E], F32)
        ident = cst[:, 0:128]
        iota = cst[:, P:P + E]
        ones = sb("ones", [P, 128], F32)
        id1 = sb("id1", [P, 128], F16)
        id16 = sb("id16", [P, 128], F16)
        sel = sb("sel", [P, FM, 128], F16)
        bia = sb("bia", [P, 2, GM], F32)
        bgi = sb("bgi", [P, GM], F32)
        ss = sb("ss", [P, 2 * KT, B], F32)
        g16 = sb("g16", [P, KT], F32)
        gam = sb("gam", [P, 3], F32)
        gam2 = sb("gam2", [P, 3], F32)
        bhn = sb("bhn", [P, 2, 4, B], F16)
        bhf = sb("bhf", [P, 4, B], F32)
        cond = sb("cond", [P, KT, B], F32)
        gsum = sb("gsum", [P, NCH, 3], F32)
        thr = sb("thr", [P, 2, 3], F32)
        av = sb("av", [P, 3 * KT], F32)
        gq = sb("gq", [P, 2, DH], F32)
        gg = sb("gg", [P, DH], F32)
        ada = sb("ada", [P, 2, KT, B], F32)
        epsb = sb("epsb", [P, 1], F32)
        wrs = sb("wrs", [P, KT, 2, E], F16)
        wrf = sb("wrf", [P, KT, E], F32)

        top = Mem(arena, 0)
        hx = top.take([T, KT * B], F32)
        base = top.at

        raw_top = ARENA - 4 * 3 * (2 * KT * P + D)
        mr = Mem(arena, raw_top)
        gul = mr.take([3, 2 * KT * P], F32)
        dnl = mr.take([3, D], F32)
        raw2_in = [sem(f"raw2_in{i}") for i in range(3)]

        def load_experts(sp, mt):
            sp.dma_start(gul[:, mt % 3, :], wgu[:, mt].rearrange("p a k f -> p (a k f)")).then_inc(raw2_in[mt % 3], 16)
            sp.dma_start(dnl[:, mt % 3, :], wdn[:, mt, :]).then_inc(raw2_in[mt % 3], 16)

        m = Mem(arena, base)
        wihs = m.take([2, KT, GM, P], F16)
        whhs = m.take([2, KT, GM, P], F16)
        girz = m.take([TC + 1, 2, 2 * KT * B], F16)
        gin = m.take([TC + 1, KT * B], F32)
        xc = m.take([KT, CH], F32)
        xs = m.take([2, KT, CH], F16)
        raw = m.take([4, G3], F32)
        tmp = m.take([2, CH], F32)
        wal = m.take([3, WN // P // NCH], F32)
        cstage = m.take([FM * 128], F32)
        mv = m.take([2, KT, 4, B], F16)
        H16 = m.take([KT * B], F32)
        rzp = m.take([2, 32], F32)
        rz = m.take([2, 32], F32)
        n5 = m.take([32, 5], F32)
        npre = m.take([32], F32)
        nn = m.take([32], F32)
        om = m.take([32], F32)
        zh = m.take([32], F32)
        uf = m.take([32], F32)

        assert m.at <= raw_top
        ORDER = gru_order()
        PZ = [bank[g][:, 0:128].rearrange("p (a g c) -> p a g c", a=4, g=2) for g in range(2)]
        PN = [bank[2 + g][:, 0:64].rearrange("p (a c) -> p a c", a=4) for g in range(2)]
        HALF = [slice(0, 16), slice(16, 32)]

        small_in = sem("small_in")
        raw_in = [sem(f"raw_in{i}") for i in range(4)]
        sel_in = sem("sel_in")
        x_in = sem("x_in")
        wal_in = sem("wal_in")
        wal_used = sem("wal_used")
        consts_done = sem("consts_done")
        w_hi = sem("w_hi")
        w_lo = sem("w_lo")
        x_hi = sem("x_hi")
        x_lo = sem("x_lo")
        gi_mm = sem("gi_mm")
        gi_evac = sem("gi_evac")
        gi_hi = sem("gi_hi")
        gi_lo = sem("gi_lo")
        h_init = sem("h_init")
        pads = sem("pads")
        pad_row = sem("pad_row")
        rz_mm, n_mm = two("rz_mm"), two("n_mm")
        rz_pre, n_read = two("rz_pre"), two("n_read")
        rz_act, n_pre, n_act = two("rz_act"), two("n_pre"), two("n_act")
        om_ready = two("om_ready")
        u_f32, u_hi, u_ready = two("u_f32"), two("u_hi"), two("u_ready")
        zh_hi, zh_f32, zh_ready = two("zh_hi"), two("zh_f32"), two("zh_ready")
        gin_staged = sem("gin_staged")
        h_new = sem("h_new")
        h_kept = sem("h_kept")

        with nc.Block() as block:

            @block.sync
            def _(sp):
                sp.dma_start(cst[:, :], consts[:, 0:P + E]).then_inc(small_in, 16)
                sp.dma_start(bia[:, :, :], bias).then_inc(small_in, 16)
                sp.dma_start(cond[:, :, :], condT).then_inc(small_in, 16)
                sp.dma_start(av[:, :], avec).then_inc(small_in, 16)
                sp.dma_start(gq[:, :, :], gqk).then_inc(small_in, 16)
                sp.dma_start(wrf[:, :, :], wr).then_inc(small_in, 16)
                sp.dma_start(xc[:, :, :], xT[:, :, 0:CH]).then_inc(x_in, 16)
                for i in range(2 * KT):
                    if i >= 4:
                        sp.wait_ge(w_lo, i - 3)
                    src = wih if i < KT else whh
                    sp.dma_start(raw[:, i % 4, :], src[:, i % KT, :]).then_inc(raw_in[i % 4], 16)
                sp.dma_start(cstage[:, :], consts[:, P + E:P + E + FM * P]).then_inc(sel_in, 16)

                def load_w_quarter(c):
                    for i, w in enumerate((w1f, w2f, w3f)):
                        n = WN // P // NCH
                        sp.dma_start(wal[:, i, :], w[:, bass.ts(c, n)]).then_inc(wal_in, 16)

                load_w_quarter(0)
                with sp.Fori(1, NCH) as c:
                    sp.wait_ge(x_lo, c * KT)
                    sp.dma_start(xc[:, :, :], xT[:, :, bass.ts(c, CH)]).then_inc(x_in, 16)
                    sp.wait_ge(wal_used, c)
                    load_w_quarter(c)
                for mt in range(3):
                    load_experts(sp, mt)

            @block.tensor
            def _(pe):
                def project_x(c, first):
                    for group in range(GM // 4):
                        for k in range(KT):
                            if group == 0:
                                pe.wait_ge(x_lo, c * KT + k + 1)
                                if first:
                                    pe.wait_ge(w_lo, k + 1)
                            for i in range(4):
                                mt = 4 * group + i
                                if k == 0 and not (first and group == 0):
                                    pe.wait_ge(gi_evac, c * GM + mt - 3)
                                for n, (wp, xp) in enumerate(((0, 0), (0, 1), (1, 0))):
                                    mm = nc.tensor.matmul(bank[4 + i][:, :], wihs[:, wp, k, mt, :], xs[:, xp, k, :],
                                                          start=(k == 0 and n == 0), stop=(k == KT - 1 and n == 2))
                                if k == KT - 1:
                                    mm.then_inc(gi_mm, 1)

                def step(n1, n2, s, it):
                    left = {}
                    for k, j, gates in ORDER:
                        for g in gates:
                            left[(j // 2, g == 2)] = left.get((j // 2, g == 2), 0) + 1
                    opened, seen = set(), set()
                    for k, j, gates in ORDER:
                        half, khalf = j // 2, k // 2
                        if gates != (2,) and (half, 0) not in opened:
                            opened.add((half, 0))
                            pe.wait_ge(rz_pre[half], n1)
                            x_part = girz[:, it].rearrange("p a (g c) -> p a g c", g=2)[:, :, :, HALF[half]]
                            nc.tensor.matmul(PZ[half][:, 0:2], id16[:, :], x_part, start=True, stop=False,
                                             skip_group_check=True)
                        if 2 in gates and (half, 1) not in opened:
                            opened.add((half, 1))
                            pe.wait_ge(n_read[half], n1)
                            b_part = bhn.rearrange("p a k b -> p a (k b)")[:, :, HALF[half]]
                            nc.tensor.matmul(PN[half][:, 0:2], id16[:, :], b_part, start=True, stop=False,
                                             skip_group_check=True)
                        if khalf not in seen:
                            seen.add(khalf)
                            pe.wait_ge(zh_ready[khalf], n1)
                            pe.wait_ge(u_ready[khalf], n1)
                        o = (j % 2) * B
                        for g in gates:
                            for part in range(2):
                                dst = PZ[half][:, :, g, o:o + B] if g < 2 else PN[half][:, :, o:o + B]
                                mm = nc.tensor.matmul(dst, whhs[:, part, k, g * KT + j, :], mv[:, 1 - s % 2, k],
                                                      start=False, stop=False, skip_group_check=True)
                            left[(half, g == 2)] -= 1
                            if left[(half, g == 2)] == 0:
                                mm.then_inc((n_mm if g == 2 else rz_mm)[half], 1)

                pe.wait_ge(consts_done, 4)

                def steps(c):
                    pe.wait_ge(w_lo, 2 * KT)
                    pe.wait_ge(h_init, 4)
                    with pe.Fori(0, TC // UN) as i:
                        n = [pe.snap(c * TC + i * UN + s + 1) for s in range(UN + 1)]
                        pe.wait_ge(gi_lo, c * 8 + 8)
                        for s in range(UN):
                            step(n[s], n[s + 1], s, i * UN + s)

                project_x(0, True)
                with pe.Fori(0, NCH - 1) as c:
                    steps(c)
                    project_x(c + 1, False)
                steps(NCH - 1)

            @block.scalar
            def _(act):
                A = nc.scalar
                act.wait_ge(small_in, 6 * 16)
                A.activation(id1[:, :], ident, ACT.Copy).then_inc(consts_done, 1)
                A.activation(id16[:, :], ident, ACT.Copy, scale=SX).then_inc(consts_done, 1)
                A.activation(H16[:, :], cond.rearrange("p a b -> p (a b)"), ACT.Copy, scale=SX).then_inc(h_init, 1)
                A.activation(mv[:, 1, :, 0, :], cond[:, :, :], ACT.Copy, scale=SX).then_inc(h_init, 1)
                for i in range(2 * KT):
                    act.wait_ge(raw_in[i % 4], 16 * (i // 4 + 1))
                    w = wihs if i < KT else whhs
                    A.activation(w[:, 0, i % KT].rearrange("p a b -> p (a b)"), raw[:, i % 4, :], ACT.Copy,
                                 scale=SW).then_inc(w_hi, 1)
                    if i == 0:
                        act.wait_ge(x_in, 16)
                        for k in range(KT):
                            A.activation(xs[:, 0, k, :], xc[:, k, :], ACT.Copy, scale=SX).then_inc(x_hi, 1)
                act.wait_ge(consts_done, 4)
                act.wait_ge(pad_row, 1)
                act.wait_ge(sel_in, 16)
                A.activation(sel.rearrange("p a b -> p (a b)"), cstage[:, :], ACT.Copy)

                def step(n1, n2, s, it):
                    for g in range(2):
                        act.wait_ge(rz_pre[g], n2)
                        A.activation(rz[:, :, HALF[g]], rzp[:, :, HALF[g]], ACT.Sigmoid,
                                     scale=1 / SWX).then_inc(rz_act[g], 1)
                        act.wait_ge(n_pre[g], n1)
                        A.activation(nn[:, HALF[g]], npre[:, HALF[g]], ACT.Tanh, scale=1 / SWX).then_inc(n_act[g], 1)
                    A.activation(n5[:, :, 4], gin[:, it + 1], ACT.Copy).then_inc(gin_staged, 1)

                def read_projections(c):
                    for mt in range(GM):
                        act.wait_ge(gi_mm, c * GM + mt + 1)
                        if mt < 8:
                            if mt < 2:
                                act.wait_ge(gi_lo, c * 8 + mt)
                            else:
                                act.wait_ge(gi_lo, c * 8 + (mt - 1))
                            A.activation(tmp[:, mt % 2, :], bank[4 + mt % 4][:, :], ACT.Identity,
                                         scale=1 / SX, bias=bgi[:, mt:mt + 1]).then_inc(gi_evac, 1)
                        else:
                            j = mt - 8
                            A.activation(gin[:, 0:TC, j * B:(j + 1) * B],
                                         bank[4 + mt % 4].rearrange("p (t b) -> p t b", b=B), ACT.Identity,
                                         bias=bgi[:, mt:mt + 1]).then_inc(gi_evac, 1)
                    act.wait_ge(gi_evac, c * GM + GM)
                    A.activation(n5[:, :, 4], gin[:, 0], ACT.Copy).then_inc(gin_staged, 1)

                def steps(c):
                    with act.Fori(0, TC // UN) as i:
                        n = [act.snap(c * TC + i * UN + s + 1) for s in range(UN + 1)]
                        for s in range(UN):
                            step(n[s], n[s + 1], s, i * UN + s)

                read_projections(0)
                with act.Fori(0, NCH - 1) as c:
                    steps(c)
                    act.wait_ge(x_in, c * 16 + 32)
                    for k in range(KT):
                        A.activation(xs[:, 0, k, :], xc[:, k, :], ACT.Copy, scale=SX).then_inc(x_hi, 1)
                    read_projections(c + 1)
                steps(NCH - 1)

            @block.vector
            def _(dve):
                V = nc.vector
                V.memset(ones[:, :], 1.0).then_inc(consts_done, 1)
                V.memset(epsb[:, :], 1e-6)
                dve.wait_ge(small_in, 6 * 16)
                V.tensor_tensor(bgi[:, 0:8], bia[:, 0, 0:8], bia[:, 1, 0:8], ALU.add).then_inc(pads, 1)
                dve.wait_ge(pads, 1)
                V.tensor_scalar(bgi[:, 0:8], bgi[:, 0:8], SW, None, ALU.mult)
                V.tensor_scalar(bgi[:, 8:12], bia[:, 0, 8:12], SWX, None, ALU.mult)
                V.tensor_scalar(bhf[:, :, :], bia[:, 1, 8:12].unsqueeze(2).broadcast_to((P, 4, B)), SW, None,
                                ALU.mult).then_inc(pads, 1)
                dve.wait_ge(pads, 2)
                V.tensor_copy(bhn[:, 0], bhf[:, :, :]).then_inc(pads, 1)
                dve.wait_ge(pads, 3)
                V.tensor_tensor(bhn[:, 1], bhf[:, :, :], bhn[:, 0], ALU.subtract).then_inc(consts_done, 1)
                V.memset(mv[:, 1, :, 2:4, :], 0.0).then_inc(h_init, 1)
                dve.wait_ge(h_init, 3)
                V.tensor_tensor(mv[:, 1, :, 1, :], H16.rearrange("p (k b) -> p k b", k=KT), mv[:, 1, :, 0, :],
                                ALU.subtract).then_inc(h_init, 1)
                for i in range(2 * KT):
                    dve.wait_ge(w_hi, i + 1)
                    w = wihs if i < KT else whhs
                    V.scalar_tensor_tensor(w[:, 1, i % KT].rearrange("p a b -> p (a b)"), raw[:, i % 4, :], SW,
                                           w[:, 0, i % KT].rearrange("p a b -> p (a b)"), ALU.mult,
                                           ALU.subtract).then_inc(w_lo, 1)
                    if i == 0:
                        for k in range(KT):
                            dve.wait_ge(x_hi, k + 1)
                            V.scalar_tensor_tensor(xs[:, 1, k, :], xc[:, k, :], SX, xs[:, 0, k, :], ALU.mult,
                                                   ALU.subtract).then_inc(x_lo, 1)

                def halves(a):
                    return a.rearrange("p (j c) -> p j c", j=2)

                def step(n1, n2, s):
                    u_parts = [mv[:, s % 2, 2 * g:2 * g + 2] for g in range(2)]

                    def sum_rz(g):
                        dve.wait_ge(rz_mm[g], n1)
                        if g == 0:
                            dve.wait_ge(h_new, n1)
                        V.tensor_reduce(rzp[:, :, HALF[g]], PZ[g].rearrange("p a g c -> p g c a"), AX.X,
                                        ALU.add).then_inc(rz_pre[g], 1)

                    def times_r(g):
                        dve.wait_ge(rz_act[g], n1)
                        dve.wait_ge(n_mm[g], n1)
                        V.tensor_tensor(n5[:, HALF[g], 0:4], PN[g].rearrange("p a c -> p c a"),
                                        rz[:, 0, HALF[g]].unsqueeze(2).broadcast_to((P, 16, 4)),
                                        ALU.mult).then_inc(n_read[g], 1)

                    def one_minus_z(g):
                        V.tensor_scalar(om[:, HALF[g]], rz[:, 1, HALF[g]], -SX, SX, ALU.mult,
                                        ALU.add).then_inc(om_ready[g], 1)

                    def sum_n(g):
                        dve.wait_ge(n_read[g], n2)
                        V.tensor_reduce(npre[:, HALF[g]], n5[:, HALF[g]], AX.X, ALU.add).then_inc(n_pre[g], 1)

                    def form_u(g):
                        dve.wait_ge(n_act[g], n1)
                        V.tensor_tensor(uf[:, HALF[g]], nn[:, HALF[g]], om[:, HALF[g]], ALU.mult).then_inc(u_f32[g], 1)
                        V.tensor_tensor(u_parts[g][:, :, 2], halves(nn[:, HALF[g]]), halves(om[:, HALF[g]]),
                                        ALU.mult).then_inc(u_hi[g], 1)

                    def low_u(g):
                        dve.wait_ge(u_hi[g], n1)
                        V.tensor_tensor(u_parts[g][:, :, 3], halves(uf[:, HALF[g]]), u_parts[g][:, :, 2],
                                        ALU.subtract).then_inc(u_ready[g], 1)

                    sum_rz(0)
                    times_r(0)
                    one_minus_z(0)
                    sum_n(0)
                    sum_rz(1)
                    form_u(0)
                    times_r(1)
                    low_u(0)
                    one_minus_z(1)
                    sum_n(1)
                    form_u(1)
                    low_u(1)

                def split_projections(c):
                    for mt in range(8):
                        g0, j = mt // 4, mt % 4
                        col = slice(g0 * 32 + j * B, g0 * 32 + (j + 1) * B)
                        src = tmp[:, mt % 2, :].rearrange("p (t b) -> p t b", b=B)
                        dve.wait_ge(gi_evac, c * GM + mt + 1)
                        V.tensor_copy(girz[:, 0:TC, 0, col], src).then_inc(gi_hi, 1)
                        dve.wait_ge(gi_hi, c * 8 + mt + 1)
                        V.tensor_tensor(girz[:, 0:TC, 1, col], src, girz[:, 0:TC, 0, col],
                                        ALU.subtract).then_inc(gi_lo, 1)
                    dve.wait_ge(wal_in, c * 48 + 48)
                    V.tensor_reduce(gsum[:, c, :], wal[:, :, :], AX.X, ALU.add,
                                    apply_absolute_value=True).then_inc(wal_used, 1)
                    dve.wait_ge(gin_staged, c * (TC + 1) + 1)

                def steps(c):
                    with dve.Fori(0, TC // UN) as i:
                        n = [dve.snap(c * TC + i * UN + s + 1) for s in range(UN + 1)]
                        for s in range(UN):
                            step(n[s], n[s + 1], s)

                for g in range(2):
                    V.memset(om[:, HALF[g]], 0.0).then_inc(rz_pre[g], 1)
                    V.memset(npre[:, HALF[g]], 0.0).then_inc(n_read[g], 1)
                    V.memset(uf[:, HALF[g]], 0.0).then_inc(u_ready[g], 1)
                split_projections(0)
                with dve.Fori(0, NCH - 1) as c:
                    steps(c)
                    for k in range(KT):
                        dve.wait_ge(x_hi, c * KT + KT + k + 1)
                        V.scalar_tensor_tensor(xs[:, 1, k, :], xc[:, k, :], SX, xs[:, 0, k, :], ALU.mult,
                                               ALU.subtract).then_inc(x_lo, 1)
                    split_projections(c + 1)
                steps(NCH - 1)

            @block.gpsimd
            def _(pool):
                G = nc.gpsimd

                def halves(a):
                    return a.rearrange("p (j c) -> p j c", j=2)

                G.memset(gin[:, TC], 0.0).then_inc(pad_row, 1)
                pool.wait_ge(h_init, 4)
                for g in range(2):
                    G.memset(zh[:, HALF[g]], 0.0).then_inc(zh_ready[g], 1)
                pool.wait_ge(zh_ready[0], 1)
                pool.wait_ge(zh_ready[1], 1)
                G.memset(zh[:, :], 0.0).then_inc(h_new, 1)

                def step(n1, n2, s, t):
                    for g in range(2):
                        z_parts = mv[:, s % 2, 2 * g:2 * g + 2]
                        pool.wait_ge(rz_act[g], n1)
                        if g == 0:
                            pool.wait_ge(h_new, n1)
                        G.tensor_tensor(z_parts[:, :, 0], halves(rz[:, 1, HALF[g]]), halves(H16[:, HALF[g]]),
                                        ALU.mult).then_inc(zh_hi[g], 1)
                        G.tensor_tensor(zh[:, HALF[g]], rz[:, 1, HALF[g]], H16[:, HALF[g]],
                                        ALU.mult).then_inc(zh_f32[g], 1)
                        pool.wait_ge(zh_hi[g], n1)
                        pool.wait_ge(zh_f32[g], n1)
                        G.tensor_tensor(z_parts[:, :, 1], halves(zh[:, HALF[g]]), z_parts[:, :, 0],
                                        ALU.subtract).then_inc(zh_ready[g], 1)
                    pool.wait_ge(u_f32[0], n1)
                    pool.wait_ge(u_f32[1], n1)
                    G.tensor_tensor(H16[:, :], uf[:, :], zh[:, :], ALU.add).then_inc(h_new, 1)
                    pool.wait_ge(h_new, n2)
                    G.tensor_copy(hx[:, t], H16[:, :]).then_inc(h_kept, 1)

                with pool.Fori(0, NCH) as c:
                    with pool.Fori(0, TC // UN) as i:
                        n = [pool.snap(c * TC + i * UN + s + 1) for s in range(UN + 1)]
                        for s in range(UN):
                            step(n[s], n[s + 1], s, c * TC + i * UN + s)

        m = Mem(arena, base)
        wgus = m.take([2, FM, 2, KT, P], F16)
        wdns = m.take([2, FM, D], F16)
        hc = m.take([2, KT, CH], F16)
        hid = m.take([2, FM, CH], F16)
        xr = m.take([KT, CH], F32)
        sg = m.take([2, CH], F32)
        ga = m.take([CH], F32)
        gb = m.take([CH], F32)
        hf = m.take([2, CH], F32)
        wT = m.take([CH], F16)
        sc = m.take([4, E], F32)
        mx = m.take([4, 8], F32)
        ix = m.take([4, 8], F32).bitcast(U32)
        ixf = m.take([4, 2], F32)
        dif = m.take([4, 2], F32)
        pr = m.take([4, 2], F32)
        w1st = m.take([4, E], F32)
        w2nd = m.take([4, E], F32)
        wgt = m.take([4, E], F32)
        wp = m.take([4, 2 * E], F16)

        mc = Mem(arena, base)
        wqs = mc.take([2, KT, G3], F16)
        wos = mc.take([2, KT, D], F16)
        rinv = mc.take([NTOK], F32)
        start_c = mc.at
        wol = mc.take([KT, D], F32)
        end_wgus = base + 2 * FM * 2 * KT * P * 2
        assert mc.at <= end_wgus
        wel = Mem(arena, raw_top).take([KT, 2 * D], F32)
        sqx = hc.bitcast(F32).rearrange("p a k (c t) -> p (a k c t)", c=1).rearrange("p (k t) -> p k t", k=KT)
        wql = m.take([KT, G3], F32)
        assert m.at <= raw_top
        rms = sg

        we_in, wo_in, wo_unit = sem("we_in"), sem("wo_in"), sem("wo_unit")
        wq_in = [sem(f"wq_in{k}") for k in range(KT)]
        sqx_done, add_done, sumx_done, ssx_mm = sem("sqx_done"), sem("add_done"), sem("sumx_done"), sem("ssx_mm")
        rms_done, rinv_done = sem("rms_done"), sem("rinv_done")
        wq_hi, wq_lo = sem("wq_hi"), sem("wq_lo")
        ss_mm, gam_mm, prep = sem("ss_mm"), sem("gam_mm"), sem("prep")

        xr_in = sem("xr_in")
        wr_done, wT_zero = sem("wr_done"), sem("wT_zero")
        gu_hi, gu_lo = sem("gu_hi"), sem("gu_lo")
        hc_hi, hc_lo = sem("hc_hi"), sem("hc_lo")
        score_mm, scores = sem("score_mm"), sem("scores")
        top8, top_ix, top_dif, probs = sem("top8"), sem("top_ix"), sem("top_dif"), sem("probs")
        ixf_done = sem("ixf_done")
        wts_a, wts, wp_hi, wp_done = sem("wts_a"), sem("wts"), sem("wp_hi"), sem("wp_done")
        wT_mm, wT_done = sem("wT_mm"), sem("wT_done")
        gate_mm, sig_done, ga_done, gb_done = sem("gate_mm"), sem("sig_done"), sem("ga_done"), sem("gb_done")
        wb_mm, hf_done, hid_hi, hid_lo = sem("wb_mm"), sem("hf_done"), sem("hid_hi"), sem("hid_lo")
        down_mm, down_out = sem("down_mm"), sem("down_out")

        def chunk_of_states(c, k):
            return hx[:, bass.ts(c, TC), k * B:(k + 1) * B]

        def tb(a):
            return a.rearrange("p (t b) -> p t b", b=B)

        with nc.Block() as block:

            @block.sync
            def _(sp):
                sp.dma_start(xr[:, :, :], xT[:, :, 0:CH]).then_inc(xr_in, 16)
                for mt in range(3, FM):
                    sp.wait_ge(gu_lo, 2 * (mt - 2))
                    load_experts(sp, mt)
                for k in range(KT):
                    sp.dma_start(wql[:, k, :], wqkv[:, k, :]).then_inc(wq_in[k], 16)
                with sp.Fori(1, NCH) as c:
                    sp.wait_ge(down_out, c * KT)
                    sp.dma_start(xr[:, :, :], xT[:, :, bass.ts(c, CH)]).then_inc(xr_in, 16)
                sp.wait_ge(gu_lo, 2 * FM)
                sp.dma_start(wel[:, :, :], wemb).then_inc(we_in, 16)
                sp.wait_ge(gate_mm, NCH * FM)
                sp.dma_start(wol[:, :, :], wout).then_inc(wo_in, 16)

            @block.tensor
            def _(pe):
                pe.wait_ge(wr_done, 2)
                pe.wait_ge(wT_zero, 1)

                def sum_x(c):
                    if c >= 2:
                        pe.wait_ge(rms_done, c - 1)
                    pe.wait_ge(sumx_done, c + 1)
                    mm = nc.tensor.matmul(bank[c % 2][:, :], ones[:, :], sqx[:, 0, :], start=True, stop=(c < NCH - 1))
                    if c == NCH - 1:
                        pe.wait_ge(sqx_done, NCH * KT)
                        mm = nc.tensor.matmul(bank[c % 2][:, :], ones[:, :], sqx[:, KT - 1, :], start=False, stop=True)
                    mm.then_inc(ssx_mm, 1)

                def scale_and_shift():
                    pe.wait_ge(we_in, 16)
                    SS = bank[2][:, 0:2 * KT * B].rearrange("p (m b) -> p m b", b=B)
                    for mt in range(2 * KT):
                        for k in range(KT):
                            mm = nc.tensor.matmul(SS[:, mt, :], wel[:, k, mt * P:(mt + 1) * P], cond[:, k, :],
                                                  start=(k == 0), stop=(k == KT - 1))
                    mm.then_inc(ss_mm, 1)

                def spread_weights(c, mt):
                    pe.wait_ge(hf_done, c * FM + mt)
                    nc.tensor.matmul(bank[6][:, :], sel[:, mt, :], wT[:, :], start=True, stop=True)\
                        .then_inc(wb_mm, 1)

                def chunk(c, first, last):
                    pe.wait_ge(hc_lo, c * KT + KT)
                    SC = bank[7][:, 0:64].rearrange("p (s e) -> p s e", s=4)
                    for st in range(4):
                        n = 0
                        for part in range(2):
                            for k in range(KT):
                                mm = nc.tensor.matmul(SC[:, st, :], hc[:, part, k, st * P:(st + 1) * P],
                                                      wrs[:, k].rearrange("p a e -> p (a e)"),
                                                      start=(n == 0), stop=(n == 2 * KT - 1))
                                n += 1
                    mm.then_inc(score_mm, 1)
                    for mt in range(FM):
                        if first:
                            pe.wait_ge(gu_lo, 2 * mt + 2)
                        if mt < 2:
                            pe.wait_ge(gb_done, c * FM + mt)
                        else:
                            pe.wait_ge(gb_done, c * FM + (mt - 1))
                        for a in range(2):
                            n = 0
                            for w_, h_ in ((0, 0), (0, 1), (1, 0)):
                                for k in range(KT):
                                    mm = nc.tensor.matmul(bank[2 * a + mt % 2][:, :], wgus[:, w_, mt, a, k, :],
                                                          hc[:, h_, k, :], start=(n == 0), stop=(n == 3 * KT - 1))
                                    n += 1
                        mm.then_inc(gate_mm, 1)
                        if mt == 1:
                            pe.wait_ge(wp_done, c + 1)
                            WT = bank[7].bitcast(F16)[0:2 * E, 0:CH]
                            for st in range(4):
                                mm = nc.tensor.transpose(WT[:, st * P:(st + 1) * P], wp[:, st, :], id1[:, :])
                            mm.then_inc(wT_mm, 1)
                            pe.wait_ge(wT_done, c + 1)
                        if mt > 0:
                            spread_weights(c, mt - 1)
                    spread_weights(c, FM - 1)
                    pe.wait_ge(hid_lo, c * FM + FM - 2)
                    for j in range(KT):
                        if j < 2:
                            pe.wait_ge(down_out, c * KT + j)
                        else:
                            pe.wait_ge(down_out, c * KT + (j - 1))
                        n = 0
                        for mt in range(FM):
                            if j == 0 and mt >= FM - 2:
                                pe.wait_ge(hid_lo, c * FM + mt + 1)
                            for w_, h_ in ((0, 0), (0, 1), (1, 0)):
                                mm = nc.tensor.matmul(bank[4 + j % 2][:, :], wdns[:, w_, mt, j * P:(j + 1) * P],
                                                      hid[:, h_, mt, :], start=(n == 0), stop=(n == 3 * FM - 1))
                                n += 1
                        mm.then_inc(down_mm, 1)
                        if last:
                            if j == 0:
                                nc.tensor.matmul(bank[3][:, 0:3 * NCH], ones[:, :], gsum.rearrange("p c w -> p (c w)"),
                                                 start=True, stop=True).then_inc(gam_mm, 1)
                            sum_x(j)
                    if last:
                        scale_and_shift()

                chunk(0, True, False)
                with pe.Fori(1, NCH - 1) as c:
                    chunk(c, False, False)
                chunk(NCH - 1, False, True)

            @block.scalar
            def _(act):
                A = nc.scalar

                def split_states(c):
                    for k in range(KT):
                        A.activation(tb(hc[:, 0, k, :]), chunk_of_states(c, k), ACT.Copy).then_inc(hc_hi, 1)

                def split_weights(mt):
                    act.wait_ge(raw2_in[mt % 3], 32 * (mt // 3 + 1))
                    A.activation(wgus[:, 0, mt].rearrange("p a k f -> p (a k f)"), gul[:, mt % 3, :], ACT.Copy,
                                 scale=SW).then_inc(gu_hi, 1)
                    A.activation(wdns[:, 0, mt, :], dnl[:, mt % 3, :], ACT.Copy, scale=SW).then_inc(gu_hi, 1)

                def chunk(c, first, last):
                    act.wait_ge(top_dif, 2 * c + 2)
                    A.activation(pr[:, :, :], dif[:, :, :], ACT.Sigmoid, scale=1 / SWX).then_inc(probs, 1)
                    for mt in range(FM + 1):
                        if first and mt + 2 < FM:
                            split_weights(mt + 2)
                        if mt < FM:
                            act.wait_ge(gate_mm, c * FM + mt + 1)
                            A.activation(sg[:, mt % 2, :], bank[mt % 2][:, :], ACT.Sigmoid, scale=1 / SWX)\
                                .then_inc(sig_done, 1)
                        if mt == 1:
                            act.wait_ge(wT_mm, c + 1)
                            A.activation(wT[0:2 * E, :], bank[7].bitcast(F16)[0:2 * E, 0:CH], ACT.Copy)\
                                .then_inc(wT_done, 1)
                        if mt >= 1:
                            act.wait_ge(hf_done, c * FM + mt)
                            if mt == 1:
                                act.wait_ge(down_mm, c * KT)
                            A.activation(hid[:, 0, mt - 1, :], hf[:, (mt - 1) % 2, :], ACT.Copy).then_inc(hid_hi, 1)
                    if not last:
                        split_states(c + 1)
                    else:
                        prepare()

                def squares(c, ks):
                    for k in ks:
                        if c == NCH - 1:
                            act.wait_ge(down_out, c * KT + k + 1)
                        A.activation(tb(sqx[:, k, :]), chunk_of_states(c, k), ACT.Square).then_inc(sqx_done, 1)

                def roots(c):
                    act.wait_ge(ssx_mm, c + 1)
                    if c >= 2:
                        act.wait_ge(rinv_done, c - 1)
                    A.activation(rms[:, c % 2, :], bank[c % 2][:, :], ACT.Sqrt, scale=1 / D,
                                 bias=epsb[:, :]).then_inc(rms_done, 1)

                def prepare():
                    squares(0, range(KT))
                    for k in range(KT):
                        act.wait_ge(wq_in[k], 16)
                        A.activation(wqs[:, 0, k, :], wql[:, k, :], ACT.Copy, scale=SW).then_inc(wq_hi, 1)
                    for c in range(1, NCH):
                        act.wait_ge(ssx_mm, c)
                        squares(c, range(KT if c < NCH - 1 else KT - 1))
                        roots(c - 1)
                        if c == 1:
                            act.wait_ge(wo_unit, KT)
                            A.activation(wos[:, 0], wol[:, :, :], ACT.Copy, scale=SW).then_inc(wq_hi, 1)
                    squares(NCH - 1, (KT - 1,))
                    roots(NCH - 1)

                A.activation(wrs[:, :, 0, :], wrf[:, :, :], ACT.Copy, scale=SW).then_inc(wr_done, 1)
                split_states(0)
                split_weights(0)
                split_weights(1)
                chunk(0, True, False)
                with act.Fori(1, NCH - 1) as c:
                    chunk(c, False, False)
                chunk(NCH - 1, False, True)

            @block.vector
            def _(dve):
                V = nc.vector

                def split_states(c):
                    for k in range(KT):
                        dve.wait_ge(hc_hi, c * KT + k + 1)
                        V.tensor_tensor(tb(hc[:, 1, k, :]), chunk_of_states(c, k), tb(hc[:, 0, k, :]),
                                        ALU.subtract).then_inc(hc_lo, 1)

                def split_weights(mt):
                    dve.wait_ge(gu_hi, 2 * mt + 1)
                    V.scalar_tensor_tensor(wgus[:, 1, mt].rearrange("p a k f -> p (a k f)"), gul[:, mt % 3, :], SW,
                                           wgus[:, 0, mt].rearrange("p a k f -> p (a k f)"), ALU.mult,
                                           ALU.subtract).then_inc(gu_lo, 1)
                    dve.wait_ge(gu_hi, 2 * mt + 2)
                    V.scalar_tensor_tensor(wdns[:, 1, mt, :], dnl[:, mt % 3, :], SW, wdns[:, 0, mt, :], ALU.mult,
                                           ALU.subtract).then_inc(gu_lo, 1)

                def route(c):
                    dve.wait_ge(score_mm, c + 1)
                    V.tensor_reduce(sc[:, :, :], bank[7][:, 0:64].rearrange("p (s a e) -> p s e a", s=4, a=2), AX.X,
                                    ALU.add).then_inc(scores, 1)
                    dve.wait_ge(hc_lo, KT)
                    dve.wait_ge(scores, c + 1)
                    for st in range(4):
                        V.max(mx[:, st, :], sc[:, st, :]).then_inc(top8, 1)
                    dve.wait_ge(top8, 4 * c + 4)
                    V.tensor_tensor(dif[:, :, 0], mx[:, :, 0], mx[:, :, 1], ALU.subtract).then_inc(top_dif, 1)
                    V.tensor_tensor(dif[:, :, 1], mx[:, :, 1], mx[:, :, 0], ALU.subtract).then_inc(top_dif, 1)
                    for st in range(4):
                        V.max_index(ix[:, st, :], mx[:, st, :], sc[:, st, :]).then_inc(top_ix, 1)
                    dve.wait_ge(top_ix, 4 * c + 4)
                    V.tensor_copy(ixf[:, :, :], ix[:, :, 0:2]).then_inc(ixf_done, 1)
                    dve.wait_ge(ixf_done, c + 1)
                    dve.wait_ge(probs, c + 1)
                    for st in range(4):
                        V.tensor_scalar(w1st[:, st, :], iota, ixf[:, st, 0:1], pr[:, st, 0:1], ALU.is_equal,
                                        ALU.mult).then_inc(wts_a, 1)
                        V.tensor_scalar(w2nd[:, st, :], iota, ixf[:, st, 1:2], pr[:, st, 1:2], ALU.is_equal,
                                        ALU.mult).then_inc(wts_a, 1)
                    dve.wait_ge(wts_a, 8 * c + 8)
                    V.tensor_tensor(wgt[:, :, :], w1st[:, :, :], w2nd[:, :, :], ALU.add).then_inc(wts, 1)
                    dve.wait_ge(wts, c + 1)
                    V.tensor_copy(wp[:, :, 0:E], wgt[:, :, :]).then_inc(wp_hi, 1)
                    dve.wait_ge(wp_hi, c + 1)
                    V.tensor_tensor(wp[:, :, E:2 * E], wgt[:, :, :], wp[:, :, 0:E], ALU.subtract).then_inc(wp_done, 1)

                def down(c, j):
                    dve.wait_ge(down_mm, c * KT + j + 1)
                    V.scalar_tensor_tensor(chunk_of_states(c, j), tb(bank[4 + j % 2][:, :]), 1 / SWX,
                                           tb(xr[:, j, :]), ALU.mult, ALU.add).then_inc(down_out, 1)

                def low_qkv(k):
                    dve.wait_ge(wq_hi, k + 1)
                    V.scalar_tensor_tensor(wqs[:, 1, k, :], wql[:, k, :], SW, wqs[:, 0, k, :], ALU.mult,
                                           ALU.subtract).then_inc(wq_lo, 1)

                def invert_x(c):
                    dve.wait_ge(rms_done, c + 1)
                    V.reciprocal(rinv[:, c * CH:(c + 1) * CH], rms[:, c % 2, :]).then_inc(rinv_done, 1)

                def prepare(j):
                    if j == 0:
                        low_qkv(0)
                        low_qkv(1)
                    if j == 1:
                        low_qkv(2)
                        low_qkv(3)
                        dve.wait_ge(wo_in, 16)
                        for k in range(KT):
                            V.tensor_tensor(wol[:, k, k * P:(k + 1) * P], wol[:, k, k * P:(k + 1) * P], ident,
                                            ALU.add).then_inc(wo_unit, 1)
                        dve.wait_ge(gam_mm, 1)
                        V.tensor_reduce(gam[:, :], bank[3][:, 0:3 * NCH].rearrange("p (c w) -> p w c", w=3), AX.X,
                                        ALU.add).then_inc(prep, 1)
                        dve.wait_ge(prep, 1)
                        V.tensor_scalar(gam2[:, :], gam[:, :], 1 / WN, 1e-8, ALU.mult, ALU.add).then_inc(prep, 1)
                        dve.wait_ge(prep, 2)
                        V.tensor_scalar(thr[:, 0, :], gam2[:, :], 0.5, None, ALU.mult)
                        V.tensor_scalar(thr[:, 1, :], gam2[:, :], -0.5, None, ALU.mult)
                        V.tensor_scalar(g16[:, :], av[:, 2 * KT:3 * KT], SX, None, ALU.mult)
                        V.tensor_tensor(gg[:, :], gq[:, 0, :], gq[:, 1, :], ALU.mult).then_inc(prep, 1)
                    if j == 2:
                        invert_x(0)
                        dve.wait_ge(wq_hi, KT + 1)
                        V.scalar_tensor_tensor(wos[:, 1], wol[:, :, :], SW, wos[:, 0], ALU.mult,
                                               ALU.subtract).then_inc(wq_lo, 1)
                    if j == 3:
                        invert_x(1)
                        invert_x(2)

                def chunk(c, first, last):
                    route(c)
                    for mt in range(FM + 1):
                        if first and mt + 2 < FM:
                            split_weights(mt + 2)
                        if mt < FM:
                            dve.wait_ge(sig_done, c * FM + mt + 1)
                            V.scalar_tensor_tensor(ga[:, :], bank[mt % 2][:, :], 1 / SWX, sg[:, mt % 2, :], ALU.mult,
                                                   ALU.mult).then_inc(ga_done, 1)
                            dve.wait_ge(ga_done, c * FM + mt + 1)
                            V.scalar_tensor_tensor(gb[:, :], bank[2 + mt % 2][:, :], 1 / SW, ga[:, :], ALU.mult,
                                                   ALU.mult).then_inc(gb_done, 1)
                            dve.wait_ge(gb_done, c * FM + mt + 1)
                            dve.wait_ge(wb_mm, c * FM + mt + 1)
                            V.tensor_tensor(hf[:, mt % 2, :], bank[6][:, :], gb[:, :], ALU.mult).then_inc(hf_done, 1)
                        if mt >= 1:
                            dve.wait_ge(hid_hi, c * FM + mt)
                            V.tensor_tensor(hid[:, 1, mt - 1, :], hf[:, (mt - 1) % 2, :], hid[:, 0, mt - 1, :],
                                            ALU.subtract).then_inc(hid_lo, 1)
                    dve.wait_ge(xr_in, 16 * c + 16)
                    for j in range(KT):
                        if j == KT - 1 and not last:
                            split_states(c + 1)
                        if last:
                            prepare(j)
                        down(c, j)
                    if last:
                        invert_x(3)
                        dve.wait_ge(ss_mm, 1)
                        V.tensor_tensor(ss[:, :, :], bank[2][:, 0:2 * KT * B].rearrange("p (m b) -> p m b", b=B),
                                        av[:, 0:2 * KT].unsqueeze(2).broadcast_to((P, 2 * KT, B)),
                                        ALU.add).then_inc(prep, 1)
                        dve.wait_ge(prep, 4)
                        V.scalar_tensor_tensor(ada[:, 0], ss[:, 0:KT, :], 1.0,
                                               g16[:, :].unsqueeze(2).broadcast_to((P, KT, B)), ALU.add, ALU.mult)
                        V.tensor_scalar(ada[:, 1], ss[:, KT:2 * KT, :], SX, None, ALU.mult).then_inc(prep, 1)

                V.memset(wT[:, :], 0.0).then_inc(wT_zero, 1)
                dve.wait_ge(wr_done, 1)
                V.scalar_tensor_tensor(wrs[:, :, 1, :], wrf[:, :, :], SW, wrs[:, :, 0, :], ALU.mult,
                                       ALU.subtract).then_inc(wr_done, 1)
                split_states(0)
                split_weights(0)
                split_weights(1)
                chunk(0, True, False)
                with dve.Fori(1, NCH - 1) as c:
                    chunk(c, False, False)
                chunk(NCH - 1, False, True)

            @block.gpsimd
            def _(pool):
                for c in range(NCH):
                    last = c == NCH - 1
                    pool.wait_ge(sqx_done, c * KT + (KT - 1 if last else KT))
                    nc.gpsimd.tensor_tensor(sqx[:, 0, :], sqx[:, 0, :], sqx[:, 1, :], ALU.add).then_inc(add_done, 1)
                    if not last:
                        nc.gpsimd.tensor_tensor(sqx[:, 2, :], sqx[:, 2, :], sqx[:, 3, :], ALU.add).then_inc(add_done, 1)
                    pool.wait_ge(add_done, 2 * c + (1 if last else 2))
                    nc.gpsimd.tensor_tensor(sqx[:, 0, :], sqx[:, 0, :], sqx[:, 2, :], ALU.add).then_inc(sumx_done, 1)

        S = T
        o2p = Mem(arena, ARENA - 4 * NTOK * KT).take([2, KT, NTOK], F16)
        raw_tl = ARENA - 4 * NTOK * KT - 4 * 9 * D
        tl = Mem(arena, raw_tl).take([3, 3 * D], F32)
        t_in = [sem(f"t_in{i}") for i in range(3)]

        def load_ternary(sp, mt):
            for i, w in enumerate((w1T, w2T)):
                sp.dma_start(tl[:, mt % 3, i * D:(i + 1) * D], w[:, mt].rearrange("p k h -> p (k h)"))\
                    .then_inc(t_in[mt % 3], 16)
            sp.dma_start(tl[:, mt % 3, 2 * D:3 * D], w3T[:, mt, :]).then_inc(t_in[mt % 3], 16)

        w12 = Mem(arena, base).take([HM, 2, KT, P], F16)
        m = Mem(arena, start_c)
        neg = m.take([2, 3 * D], F16)
        w3q = m.take([HM, D], F16)
        assert m.at - start_c <= 4 * KT * S + 4 * KT * S + 16 * D + 8 * D
        sgd = m.take([2, CH], F32)
        hdf = m.take([2, CH], F32)
        hdp = m.take([2, HM, CH], F16)
        yo = m.take([2, CH], F32)
        assert m.at <= raw_tl
        neg_done, q_done = sem("neg_done"), sem("q_done")
        up_mm, sgd_done, hdf_done, hdp_hi, hdp_lo = (sem("up_mm"), sem("sgd_done"), sem("hdf_done"), sem("hdp_hi"),
                                                     sem("hdp_lo"))
        y_mm, y_done, y_out = sem("y_mm"), sem("y_done"), two("y_out")

        def negatives(pool, mt):
            pool.wait_ge(t_in[mt % 3], 48 * (mt // 3 + 1))
            if mt >= 2:
                pool.wait_ge(q_done, 3 * (mt - 1))
            for i in range(3):
                nc.gpsimd.tensor_scalar(neg[:, mt % 2, i * D:(i + 1) * D], tl[:, mt % 3, i * D:(i + 1) * D],
                                        thr[:, 1, i:i + 1], None, ALU.is_lt).then_inc(neg_done, 1)

        def quantise(dve, mt):
            for i in range(3):
                dve.wait_ge(neg_done, 3 * mt + i + 1)
                dst = w12[:, mt, i].rearrange("p k h -> p (k h)") if i < 2 else w3q[:, mt, :]
                nc.vector.scalar_tensor_tensor(dst, tl[:, mt % 3, i * D:(i + 1) * D], thr[:, 0, i:i + 1],
                                               neg[:, mt % 2, i * D:(i + 1) * D], ALU.is_gt,
                                               ALU.subtract).then_inc(q_done, 1)

        m = Mem(arena, start_c)
        xnf = m.take([KT, S], F32)
        xn = m.take([2, KT, S], F16)
        qkr = m.take([4, D], F32)
        sqk = m.take([2, D], F32)
        ssk = m.take([4, H], F32)
        rmsk = m.take([4, H], F32)
        rk = m.take([4, H], F32)
        stk = m.take([4, H, 3 * DH], F16)
        qs = m.take([H, S], F16)
        ks = m.take([H, S], F16)
        vr = m.take([2, D], F32)
        vh = m.take([2, H, DH + 1], F16)
        vl = m.take([2, H, DH + 1], F16)
        mxs = m.take([2, H], F32)
        mT = m.take([P], F16)
        pf = m.take([3, 2 * S], F32)
        ph = m.take([3, 2, S], F16)
        pl = m.take([3, 2, S], F16)
        rc = m.take([2, 4], F32)
        of = m.take([2, H, DH], F32)
        oTp = m.take([2, KT, S], F16)

        assert m.at <= raw_tl

        KC = SX * SX
        POOL_LOW = 8
        PROJECT_AT = {0: 0, 1: 1, 2: 2, 3: 3, 5: 4, 6: 5}
        ROOT_AT = 4
        NORM_AT = {4: (0,), 5: (1, 2, 3)}
        SPLIT_AT = {5: (0, 1), 6: (2, 3)}
        LOW_AT = {6: (0, 1), 7: (2, 3)}
        STACK_AT = {8: (0,), 9: (1,), 10: (2,), 13: (3,)}
        MAX_AT = {9: (0, 1), 10: (2, 3), 11: (4, 5, 6), 12: (7, 8), 13: (9, 10), 14: (11, 12), 15: (13, 14)}

        vzero = sem("vzero")
        xnt_done, xnf_done, xn_hi, xn_lo = sem("xnt_done"), sem("xnf_done"), sem("xn_hi"), sem("xn_lo")
        qkv_mm, qkv_out, sqk_done, ssk_done = sem("qkv_mm"), sem("qkv_out"), sem("sqk_done"), sem("ssk_done")
        rmsk_done, rk_done, qk_unit, q_gain = sem("rmsk_done"), sem("rk_done"), sem("qk_unit"), sem("q_gain")
        qk_hi, qk_lo = sem("qk_hi"), sem("qk_lo")
        qs_mm, ks_mm, qs_done, ks_done = sem("qs_mm"), sem("ks_mm"), sem("qs_done"), sem("ks_done")
        s_mm, max_done, mT_mm, mT_done, mrow_in = (sem("s_mm"), sem("max_done"), sem("mT_mm"), sem("mT_done"),
                                                   sem("mrow_in"))
        st_mm, exp_done, ph_done, pl_done, av_head = (sem("st_mm"), sem("exp_done"), sem("ph_done"), sem("pl_done"),
                                                      sem("av_head"))
        pool_low = sem("pool_low")
        rc_done, o_done = sem("rc_done"), sem("o_done")
        vh_done, v_done = sem("vh_done"), sem("v_done")
        oT_mm, oTh_done, oTl_done, wo_mm, o2_hi, o2_lo = (sem("oT_mm"), sem("oTh_done"), sem("oTl_done"), sem("wo_mm"),
                                                          sem("o2_hi"), sem("o2_lo"))

        def wait_low(eng, b, h):
            if h < POOL_LOW:
                eng.wait_ge(pl_done, POOL_LOW * b + h + 1)
            else:
                eng.wait_ge(pool_low, (H - POOL_LOW) * b + h - POOL_LOW + 1)

        def heads_of(a):
            return a.rearrange("p (h d) -> p h d", h=H)

        def O_bank(q4):
            return bank[q4 % 2][:, 0:2 * 4 * (DH + 1)].rearrange("p (q h d) -> p q h d", q=2, h=4)

        with nc.Block() as block:

            @block.sync
            def _(sp):
                def load_max(b):
                    sp.wait_ge(mT_done, b + 1)
                    for qt in range(2):
                        sp.dma_start(qs[96:97, :, qt * P:(qt + 1) * P], mT[16 * qt:16 * qt + 16, :])\
                            .then_inc(mrow_in, 16)

                for mt in range(3):
                    load_ternary(sp, mt)
                load_max(0)
                with sp.Fori(0, B - 1) as b:
                    load_max(b + 1)

            @block.tensor
            def _(pe):
                def project(b, i, first=False):
                    if i == 0:
                        pe.wait_ge(xn_lo, b + 1)
                    if i < 2 and not first:
                        pe.wait_ge(o2_lo, 2 * b + i - 1)
                    elif i >= 2:
                        pe.wait_ge(qkv_out, 6 * b + i - 1)
                    half = i // 2 if i < 4 else i - 4
                    col = (i % 2 if i < 4 else 2) * D
                    n = 0
                    for w_, x_ in ((0, 0), (0, 1), (1, 0)):
                        for k in range(KT):
                            mm = nc.tensor.matmul(bank[5 + i % 2][:, :], xn[:, x_, k, half * P:(half + 1) * P],
                                                  wqs[:, w_, k, col:col + D], start=(n == 0), stop=(n == 3 * KT - 1))
                            n += 1
                    mm.then_inc(qkv_mm, 1)

                def stack(b, g):
                    for a, done, mms in ((0, qs_done, qs_mm), (1, ks_done, ks_mm)):
                        if g == 0:
                            pe.wait_ge(qk_lo, 4 * b + 4)
                            pe.wait_ge(qkv_out, 6 * b + 5 + a)
                        else:
                            pe.wait_ge(done, 4 * b + g)
                        T16 = bank[5 + a].bitcast(F16).rearrange("p (h s) -> p h s", h=4)
                        for h in range(4):
                            for half in range(2):
                                mm = nc.tensor.transpose(T16[0:96, h, half * P:(half + 1) * P],
                                                         stk[:, 2 * half + a, 4 * g + h, :], id1[:, :])
                        mm.then_inc(mms, 1)

                def scores(b, h, first=False):
                    if h % 4 == 0:
                        pe.wait_ge(qs_done, 4 * b + h // 4 + 1)
                        pe.wait_ge(ks_done, 4 * b + h // 4 + 1)
                    if h >= 2:
                        pe.wait_ge(max_done, H * b + h - 1)
                    elif h == 1 and not first:
                        pe.wait_ge(mT_done, b)
                    for qt in range(2):
                        mm = nc.tensor.matmul(bank[4 + 3 * (h % 2)][:, qt * S:(qt + 1) * S],
                                              qs[0:96, h, qt * P:(qt + 1) * P], ks[0:96, h, :], start=True, stop=True)
                    mm.then_inc(s_mm, 1)

                def turn_max(b):
                    pe.wait_ge(max_done, H * b + H)
                    nc.tensor.transpose(bank[7][0:32, 0:P], mxs.rearrange("p q h -> p (q h)"), ident)\
                        .then_inc(mT_mm, 1)

                def scores_t(b, h, first=False):
                    if h == 0:
                        pe.wait_ge(mrow_in, 32 * (b + 1))
                    if h >= 2:
                        pe.wait_ge(exp_done, H * b + h - 1)
                    elif not first:
                        pe.wait_ge(exp_done, H * b)
                    for kt in range(2):
                        mm = nc.tensor.matmul(bank[2 + h % 2][:, kt * S:(kt + 1) * S], ks[0:97, h, kt * P:(kt + 1) * P],
                                              qs[0:97, h, :], start=True, stop=True)
                    mm.then_inc(st_mm, 1)

                def values(b, h):
                    if h == 0:
                        pe.wait_ge(v_done, 2 * b + 2)
                    if h % 4 == 0:
                        pe.wait_ge(oTl_done, 4 * b + h // 4 + 1)
                    wait_low(pe, b, h)
                    for qt in range(2):
                        n = 0
                        for kt in range(2):
                            for p_, v_ in ((ph, vh), (ph, vl), (pl, vh)):
                                mm = nc.tensor.matmul(O_bank(h // 4)[:, qt, h % 4, :],
                                                      p_[:, h % 3, kt, qt * P:(qt + 1) * P], v_[:, kt, h, :],
                                                      start=(n == 0), stop=(n == 5))
                                n += 1
                    mm.then_inc(av_head, 1)

                def turn_out(b, q4):
                    pe.wait_ge(o_done, 4 * b + q4 + 1)
                    for qt in range(2):
                        mm = nc.tensor.transpose(bank[q4 % 2][:, qt * P:(qt + 1) * P],
                                                 of[:, qt, 4 * q4:4 * q4 + 4, :].rearrange("p h d -> p (h d)"), ident)
                    mm.then_inc(oT_mm, 1)

                def project_out(b, jp, last):
                    if jp == 0:
                        pe.wait_ge(oTl_done, 4 * b + 6)
                    pe.wait_ge((qs_done, ks_done)[jp], 4 * b + (4 if last else 8))
                    for a in range(2):
                        j = 2 * jp + a
                        n = 0
                        for w_, x_ in ((0, 0), (0, 1), (1, 0)):
                            for k in range(KT):
                                mm = nc.tensor.matmul(bank[5 + jp][:, a * S:(a + 1) * S],
                                                      wos[:, w_, k, j * P:(j + 1) * P], oTp[:, x_, k, :],
                                                      start=(n == 0), stop=(n == 3 * KT - 1))
                                n += 1
                    mm.then_inc(wo_mm, 1)

                def batch(b, last):
                    for h in range(H):
                        if h == 0 and not last:
                            project(b + 1, 0)
                        if h + 2 < H:
                            scores_t(b, h + 2)
                        if h % 4 == 1 and h > 4:
                            turn_out(b, h // 4 - 1)
                        if not last:
                            if h > 0 and h in PROJECT_AT:
                                project(b + 1, PROJECT_AT[h])
                            for g in STACK_AT.get(h, ()):
                                stack(b + 1, g)
                            for i in MAX_AT.get(h, ()):
                                scores(b + 1, i)
                        values(b, h)
                    if not last:
                        scores(b + 1, 15)
                    turn_out(b, 3)
                    if not last:
                        turn_max(b + 1)
                    project_out(b, 0, last)
                    if not last:
                        scores_t(b + 1, 0)
                        scores_t(b + 1, 1)
                    project_out(b, 1, last)

                for i in range(6):
                    project(0, i, True)
                for g in range(4):
                    stack(0, g)
                for h in range(H):
                    scores(0, h, True)
                pe.wait_ge(vzero, 3)
                turn_max(0)
                scores_t(0, 0, True)
                scores_t(0, 1, True)
                with pe.Fori(0, B - 1) as b:
                    batch(b, False)
                batch(B - 1, True)

            @block.scalar
            def _(act):
                A = nc.scalar

                def norm_x(b):
                    act.wait_ge(xnt_done, b + 1)
                    for k in range(KT):
                        A.activation(xnf[:, k, :], xnf[:, k, :], ACT.Identity, scale=ada[:, 0, k, bass.ds(b, 1)],
                                     bias=ada[:, 1, k, bass.ds(b, 1)]).then_inc(xnf_done, 1)
                    act.wait_ge(xnf_done, KT * b + KT)
                    A.activation(xn[:, 0], xnf[:, :, :], ACT.Copy).then_inc(xn_hi, 1)

                def take_out(b, i):
                    act.wait_ge(qkv_mm, 6 * b + i + 1)
                    A.activation(qkr[:, i, :] if i < 4 else vr[:, i - 4, :], bank[5 + i % 2][:, :], ACT.Copy,
                                 scale=1 / SWX if i < 4 else 1 / SW).then_inc(qkv_out, 1)

                def root(b):
                    act.wait_ge(ssk_done, 4 * b + 4)
                    A.activation(rmsk[:, :, :], ssk[:, :, :], ACT.Sqrt, scale=1 / DH, bias=epsb[:, :])\
                        .then_inc(rmsk_done, 1)

                def high_qk(b, i):
                    act.wait_ge(qk_unit, 4 * b + i + 1)
                    A.activation(stk[:, i, :, 0:DH], heads_of(qkr[:, i, :]), ACT.Copy).then_inc(qk_hi, 1)

                def stack(b, g):
                    act.wait_ge(ks_mm, 4 * b + g + 1)
                    A.activation(ks[0:96, 4 * g:4 * g + 4, :].rearrange("p h s -> p (h s)"),
                                 bank[6].bitcast(F16)[0:96, :], ACT.Copy).then_inc(ks_done, 1)

                def turn_max(b):
                    act.wait_ge(mT_mm, b + 1)
                    A.activation(mT[0:32, :], bank[7][0:32, 0:P], ACT.Copy, scale=-1 / KC).then_inc(mT_done, 1)

                def high_v(b):
                    for vt in range(2):
                        act.wait_ge(qkv_out, 6 * b + 5 + vt)
                        A.activation(vh[:, vt, :, 0:DH], heads_of(vr[:, vt, :]), ACT.Copy).then_inc(vh_done, 1)

                def softmax(b, h):
                    act.wait_ge(st_mm, H * b + h + 1)
                    if h >= 3:
                        wait_low(act, b, h - 3)
                    A.activation(pf[:, h % 3, :], bank[2 + h % 2][:, :], ACT.Exp, scale=DH ** -0.5 / KC)\
                        .then_inc(exp_done, 1)
                    act.wait_ge(exp_done, H * b + h + 1)
                    if h >= 3:
                        act.wait_ge(av_head, H * b + h - 2)
                    A.activation(ph[:, h % 3].rearrange("p k s -> p (k s)"), pf[:, h % 3, :], ACT.Copy)\
                        .then_inc(ph_done, 1)

                def high_out(b, q4):
                    act.wait_ge(oT_mm, 4 * b + q4 + 1)
                    A.activation(oTp[:, 0, q4, :], bank[q4 % 2][:, 0:S], ACT.Copy).then_inc(oTh_done, 1)

                def batch(b, last, more):
                    softmax(b, 0)
                    for h in range(H):
                        if h + 1 < H:
                            softmax(b, h + 1)
                        if h % 4 == 1 and h > 4:
                            high_out(b, h // 4 - 1)
                        if not last:
                            if h in PROJECT_AT:
                                take_out(b + 1, PROJECT_AT[h])
                            if h == ROOT_AT:
                                root(b + 1)
                            for n in SPLIT_AT.get(h, ()):
                                high_qk(b + 1, n)
                            for g in STACK_AT.get(h, ()):
                                stack(b + 1, g)
                    high_out(b, 3)
                    if not last:
                        turn_max(b + 1)
                        high_v(b + 1)
                    if more:
                        norm_x(b + 2)
                    for jp in range(2):
                        act.wait_ge(wo_mm, 2 * b + jp + 1)
                        A.activation(o2p[:, 0, 2 * jp:2 * jp + 2, bass.ts(b, S)],
                                     bank[5 + jp].rearrange("p (a s) -> p a s", a=2), ACT.Copy,
                                     scale=1 / SW).then_inc(o2_hi, 1)

                norm_x(0)
                for i in range(4):
                    take_out(0, i)
                root(0)
                take_out(0, 4)
                take_out(0, 5)
                for n in range(4):
                    high_qk(0, n)
                for g in range(4):
                    stack(0, g)
                turn_max(0)
                high_v(0)
                norm_x(1)
                with act.Fori(0, B - 2) as b:
                    batch(b, False, True)
                batch(B - 2, False, False)
                batch(B - 1, True, False)

            @block.vector
            def _(dve):
                V = nc.vector

                def norm_x(b):
                    x1 = hx.rearrange("p t (k b) -> p b k t", k=KT)[:, b]
                    r = rinv.rearrange("p (t b) -> p b t", b=B)[:, b].unsqueeze(1).broadcast_to((P, KT, S))
                    V.tensor_tensor(xnf[:, :, :], x1, r, ALU.mult).then_inc(xnt_done, 1)
                    dve.wait_ge(xn_hi, b + 1)
                    V.tensor_tensor(xn[:, 1], xnf[:, :, :], xn[:, 0], ALU.subtract).then_inc(xn_lo, 1)

                def sum_squares(b, i):
                    dve.wait_ge(sqk_done, 4 * b + i + 1)
                    V.tensor_reduce(ssk[:, i, :], heads_of(sqk[:, i % 2, :]), AX.X, ALU.add).then_inc(ssk_done, 1)

                def invert(b):
                    dve.wait_ge(rmsk_done, b + 1)
                    V.reciprocal(rk[:, :, :], rmsk[:, :, :]).then_inc(rk_done, 1)
                    dve.wait_ge(rk_done, b + 1)

                def normalise_qk(b, i):
                    if i % 2 == 0:
                        dve.wait_ge(q_gain, 2 * b + i // 2 + 1)
                    V.scalar_tensor_tensor(heads_of(qkr[:, i, :]), heads_of(qkr[:, i, :]), SX,
                                           rk[:, i, :].unsqueeze(2).broadcast_to((P, H, DH)), ALU.mult,
                                           ALU.mult).then_inc(qk_unit, 1)

                def low_qk(b, i):
                    lo, again = (1, 2) if i % 2 == 0 else (2, 1)
                    dve.wait_ge(qk_hi, 4 * b + i + 1)
                    V.tensor_copy(stk[:, i, :, again * DH:(again + 1) * DH], stk[:, i, :, 0:DH])
                    V.tensor_tensor(stk[:, i, :, lo * DH:(lo + 1) * DH], heads_of(qkr[:, i, :]), stk[:, i, :, 0:DH],
                                    ALU.subtract).then_inc(qk_lo, 1)

                def stack(b, g):
                    dve.wait_ge(qs_mm, 4 * b + g + 1)
                    V.tensor_copy(qs[0:96, 4 * g:4 * g + 4, :].rearrange("p h s -> p (h s)"),
                                  bank[5].bitcast(F16)[0:96, :]).then_inc(qs_done, 1)

                def maximum(b, h):
                    dve.wait_ge(s_mm, H * b + h + 1)
                    V.tensor_reduce(mxs[:, :, h], bank[4 + 3 * (h % 2)].rearrange("p (q s) -> p q s", q=2), AX.X,
                                    ALU.max).then_inc(max_done, 1)

                def low_v(b):
                    for vt in range(2):
                        dve.wait_ge(vh_done, 2 * b + vt + 1)
                        V.tensor_tensor(vl[:, vt, :, 0:DH], heads_of(vr[:, vt, :]), vh[:, vt, :, 0:DH],
                                        ALU.subtract).then_inc(v_done, 1)

                def low_p(b, h):
                    dve.wait_ge(ph_done, H * b + h + 1)
                    V.tensor_tensor(pl[:, h % 3].rearrange("p k s -> p (k s)"), pf[:, h % 3, :],
                                    ph[:, h % 3].rearrange("p k s -> p (k s)"), ALU.subtract).then_inc(pl_done, 1)

                def normalise(b, q4):
                    O = O_bank(q4)
                    dve.wait_ge(av_head, H * b + 4 * q4 + 4)
                    V.reciprocal(rc[:, :, :], O[:, :, :, DH]).then_inc(rc_done, 1)
                    dve.wait_ge(rc_done, 4 * b + q4 + 1)
                    V.tensor_tensor(of[:, :, 4 * q4:4 * q4 + 4, :], O[:, :, :, 0:DH],
                                    rc[:, :, :].unsqueeze(3).broadcast_to((P, 2, 4, DH)), ALU.mult).then_inc(o_done, 1)

                def low_out(b, q4):
                    dve.wait_ge(oTh_done, 4 * b + q4 + 1)
                    V.tensor_tensor(oTp[:, 1, q4, :], bank[q4 % 2][:, 0:S], oTp[:, 0, q4, :],
                                    ALU.subtract).then_inc(oTl_done, 1)

                def batch(b, last, more):
                    low_p(b, 0)
                    for h in range(H):
                        if h + 1 < POOL_LOW:
                            low_p(b, h + 1)
                        if last and h in (7, 10):
                            quantise(dve, (h - 7) // 3)
                        if h % 4 == 0 and h > 0:
                            normalise(b, h // 4 - 1)
                        if h % 4 == 1 and h > 4:
                            low_out(b, h // 4 - 1)
                        if not last:
                            if 0 < h < 5:
                                sum_squares(b + 1, h - 1)
                            if h == ROOT_AT:
                                invert(b + 1)
                            for i in NORM_AT.get(h, ()):
                                normalise_qk(b + 1, i)
                            for n in LOW_AT.get(h, ()):
                                low_qk(b + 1, n)
                            for g in STACK_AT.get(h, ()):
                                stack(b + 1, g)
                            for i in MAX_AT.get(h, ()):
                                maximum(b + 1, i)
                    normalise(b, 3)
                    if not last:
                        maximum(b + 1, 15)
                    low_out(b, 3)
                    if not last:
                        low_v(b + 1)
                    if more:
                        norm_x(b + 2)
                    for jp in range(2):
                        dve.wait_ge(o2_hi, 2 * b + jp + 1)
                        V.scalar_tensor_tensor(o2p[:, 1, 2 * jp:2 * jp + 2, bass.ts(b, S)],
                                               bank[5 + jp].rearrange("p (a s) -> p a s", a=2), 1 / SW,
                                               o2p[:, 0, 2 * jp:2 * jp + 2, bass.ts(b, S)], ALU.mult,
                                               ALU.subtract).then_inc(o2_lo, 1)

                V.memset(rk[:, :, :], 0.0).then_inc(o2_lo, 2)
                V.memset(rc[:, :, :], 0.0).then_inc(oTl_done, 2)
                norm_x(0)
                for i in range(4):
                    sum_squares(0, i)
                invert(0)
                for i in range(4):
                    normalise_qk(0, i)
                for n in range(4):
                    low_qk(0, n)
                for g in range(4):
                    stack(0, g)
                for h in range(H):
                    maximum(0, h)
                low_v(0)
                norm_x(1)
                with dve.Fori(0, B - 2) as b:
                    batch(b, False, True)
                batch(B - 2, False, False)
                batch(B - 1, True, False)

            @block.gpsimd
            def _(pool):
                G = nc.gpsimd

                def squares(b, i):
                    pool.wait_ge(qkv_out, 6 * b + i + 1)
                    if i >= 2:
                        pool.wait_ge(ssk_done, 4 * b + i - 1)
                    G.tensor_tensor(sqk[:, i % 2, :], qkr[:, i, :], qkr[:, i, :], ALU.mult).then_inc(sqk_done, 1)
                    if i % 2 == 0:
                        pool.wait_ge(sqk_done, 4 * b + i + 1)
                        G.tensor_tensor(heads_of(qkr[:, i, :]), heads_of(qkr[:, i, :]),
                                        gg[:, :].unsqueeze(1).broadcast_to((P, H, DH)), ALU.mult).then_inc(q_gain, 1)

                def low_p(b, h):
                    pool.wait_ge(ph_done, H * b + h + 1)
                    G.tensor_tensor(pl[:, h % 3].rearrange("p k s -> p (k s)"), pf[:, h % 3, :],
                                    ph[:, h % 3].rearrange("p k s -> p (k s)"), ALU.subtract).then_inc(pool_low, 1)

                def batch(b, last):
                    if not last:
                        for i in range(4):
                            squares(b + 1, i)
                    else:
                        pool.wait_ge(ph_done, H * b + 1)
                        negatives(pool, 0)
                        negatives(pool, 1)
                    for h in range(POOL_LOW, H):
                        low_p(b, h)

                nc.gpsimd.memset(vh[:, :, :, DH:DH + 1], 1.0).then_inc(vzero, 1)
                pool.wait_ge(vzero, 1)
                nc.gpsimd.memset(vl[:, :, :, DH:DH + 1], 0.0).then_inc(vzero, 1)
                pool.wait_ge(vzero, 2)
                nc.gpsimd.memset(ks[96:97, :, :], KC).then_inc(vzero, 1)
                pool.wait_ge(vzero, 3)
                for i in range(4):
                    squares(0, i)
                with pool.Fori(0, B - 1) as b:
                    batch(b, False)
                batch(B - 1, True)

        with nc.Block() as block:

            @block.sync
            def _(sp):
                for mt in range(3, HM):
                    sp.wait_ge(q_done, 3 * (mt - 2))
                    load_ternary(sp, mt)
                with sp.Fori(0, NCH) as c:
                    for j in range(KT):
                        sp.wait_ge(y_done, c * KT + j + 1)
                        sp.dma_start(out[:, j, bass.ts(c, CH)], yo[:, j % 2, :]).then_inc(y_out[j % 2], 16)
                sp.wait_ge(y_out[0], 8 * KT * NCH)
                sp.wait_ge(y_out[1], 8 * KT * NCH)

            @block.gpsimd
            def _(pool):
                for mt in range(2, HM):
                    negatives(pool, mt)

            @block.tensor
            def _(pe):
                def chunk(c, first):
                    for mt in range(HM):
                        if first:
                            pe.wait_ge(q_done, 3 * mt + 3)
                        if mt < 2:
                            pe.wait_ge(hdf_done, c * HM + mt)
                        else:
                            pe.wait_ge(hdf_done, c * HM + mt - 1)
                        for a in range(2):
                            n = 0
                            for part in range(2):
                                for k in range(KT):
                                    mm = nc.tensor.matmul(bank[2 * a + mt % 2][:, :], w12[:, mt, a, k, :],
                                                          o2p[:, part, k, bass.ts(c, CH)], start=(n == 0),
                                                          stop=(n == 2 * KT - 1))
                                    n += 1
                        mm.then_inc(up_mm, 1)
                    pe.wait_ge(hdp_lo, c * HM + HM - 2)
                    for j in range(KT):
                        if j < 2:
                            pe.wait_ge(y_done, c * KT + j)
                        else:
                            pe.wait_ge(y_done, c * KT + j - 1)
                        n = 0
                        for mt in range(HM):
                            if j == 0 and mt >= HM - 2:
                                pe.wait_ge(hdp_lo, c * HM + mt + 1)
                            for part in range(2):
                                mm = nc.tensor.matmul(bank[4 + j % 2][:, :], w3q[:, mt, j * P:(j + 1) * P],
                                                      hdp[:, part, mt, :], start=(n == 0), stop=(n == 2 * HM - 1))
                                n += 1
                        mm.then_inc(y_mm, 1)

                chunk(0, True)
                with pe.Fori(1, NCH) as c:
                    chunk(c, False)

            @block.scalar
            def _(act):
                A = nc.scalar

                def chunk(c, first):
                    for mt in range(HM + 1):
                        if mt < HM:
                            act.wait_ge(up_mm, c * HM + mt + 1)
                            A.activation(sgd[:, mt % 2, :], bank[mt % 2][:, :], ACT.Sigmoid, scale=1 / SX)\
                                .then_inc(sgd_done, 1)
                        if mt > 0:
                            act.wait_ge(hdf_done, c * HM + mt)
                            if mt == 1 and not first:
                                act.wait_ge(y_mm, c * KT)
                            A.activation(hdp[:, 0, mt - 1, :], hdf[:, (mt - 1) % 2, :], ACT.Copy).then_inc(hdp_hi, 1)

                chunk(0, True)
                with act.Fori(1, NCH) as c:
                    chunk(c, False)

            @block.vector
            def _(dve):
                V = nc.vector

                def chunk(c, first):
                    for mt in range(HM + 1):
                        if first and mt + 2 < HM:
                            quantise(dve, mt + 2)
                        if mt < HM:
                            dve.wait_ge(hdp_lo, c * HM + (mt - 1 if mt >= 2 else 0))
                            dve.wait_ge(sgd_done, c * HM + mt + 1)
                            V.scalar_tensor_tensor(hdf[:, mt % 2, :], bank[2 + mt % 2][:, :], 1 / SX,
                                                   sgd[:, mt % 2, :], ALU.mult, ALU.mult).then_inc(hdf_done, 1)
                        if mt > 0:
                            dve.wait_ge(hdp_hi, c * HM + mt)
                            V.tensor_tensor(hdp[:, 1, mt - 1, :], hdf[:, (mt - 1) % 2, :], hdp[:, 0, mt - 1, :],
                                            ALU.subtract).then_inc(hdp_lo, 1)
                    for j in range(KT):
                        dve.wait_ge(y_mm, c * KT + j + 1)
                        if not first or j >= 2:
                            dve.wait_ge(y_out[j % 2], (c * 2 + j // 2) * 16)
                        x1 = hx.rearrange("p t (k b) -> p k b t", k=KT)[:, j, bass.ts(c, 2), :]
                        V.tensor_tensor(yo[:, j % 2, :].rearrange("p (b t) -> p b t", b=2),
                                        bank[4 + j % 2].rearrange("p (b t) -> p b t", b=2), x1,
                                        ALU.add).then_inc(y_done, 1)

                chunk(0, True)
                with dve.Fori(1, NCH) as c:
                    chunk(c, False)


NAMES = ["xT", "condT", "wih", "whh", "bias", "wr", "wgu", "wdn", "wemb", "avec", "gqk", "wqkv", "wout",
         "w1f", "w2f", "w3f", "w1T", "w2T", "w3T", "consts"]


def kernel(**inputs):
    import numpy as np
    import concourse.bacc as bacc
    from concourse.bass_utils import run_bass_kernel_spmd

    i = {k: np.asarray(v) for k, v in inputs.items()}

    def rows(w):
        return w.reshape(KT, P, -1).transpose(1, 0, 2)

    a = {}
    a["xT"] = rows(i["x"].transpose(2, 1, 0).reshape(D, NTOK))
    a["condT"] = rows(i["cond_2048"].T)
    a["wih"], a["whh"] = rows(i["L0_cond_W_ih"]), rows(i["L0_cond_W_hh"])
    a["bias"] = np.stack([i["L0_cond_b_ih"].reshape(GM, P).T, i["L0_cond_b_hh"].reshape(GM, P).T], 1)
    a["wr"] = rows(i["L0_ffn_w_gate_router"].T)
    gate = i["L0_ffn_w_gate_proj"].reshape(E * F, D).T.reshape(KT, P, FM, P)
    up = i["L0_ffn_w_up_proj"].reshape(E * F, D).T.reshape(KT, P, FM, P)
    a["wgu"] = np.stack([gate, up]).transpose(2, 3, 0, 1, 4)
    a["wdn"] = i["L0_ffn_w_down_proj"].transpose(0, 2, 1).reshape(FM, P, D).transpose(1, 0, 2)
    a["wemb"] = rows(i["L1_cond_W_emb"])
    a["avec"] = np.concatenate([i["L1_cond_b_emb"].reshape(2 * KT, P).T, i["L1_cond_g_norm"].reshape(KT, P).T], 1)
    a["gqk"] = np.tile(np.stack([i["L1_cond_g_q"], i["L1_cond_g_k"]]), (P, 1, 1))
    a["wqkv"], a["wout"] = rows(i["L1_cond_W_qkv"]), rows(i["L1_cond_W_out"])
    for n in "123":
        a[f"w{n}f"] = i[f"L1_ffn_w{n}"].reshape(P, -1)
    a["w1T"] = i["L1_ffn_w1"].T.reshape(KT, P, HM, P).transpose(1, 2, 0, 3)
    a["w2T"] = i["L1_ffn_w2"].T.reshape(KT, P, HM, P).transpose(1, 2, 0, 3)
    a["w3T"] = i["L1_ffn_w3"].T.reshape(HM, P, D).transpose(1, 0, 2)
    c = np.zeros((P, P + E + FM * P), np.float32)
    c[:, 0:128] = np.eye(P)
    c[:, P:P + E] = np.arange(E)
    for f in range(FM * P):
        c[f // F, P + E + f] = 1.0
        c[E + f // F, P + E + f] = 1.0
    a["consts"] = c

    nc = bacc.Bacc("TRN2", target_bir_lowering=False, num_devices=1)
    arrays, args = {}, []
    for name in NAMES:
        v = np.ascontiguousarray(a[name])
        arrays[f"in_{name}"] = v
        args.append(nc.dram_tensor(f"in_{name}", v.shape, mybir.dt.from_np(v.dtype), kind="ExternalInput").ap())
    y = nc.dram_tensor("out_y", (P, KT, NTOK), F32, kind="ExternalOutput").ap()
    mixed_net_kernel(nc, *args, y)
    r = run_bass_kernel_spmd(nc, [arrays], core_ids=[0])
    got = r.results[0]["out_y"]
    return np.ascontiguousarray(got.reshape(P, KT, B, T).transpose(2, 3, 1, 0).reshape(B, T, D))
```
